# Optimizing a Trainium2 kernel written in Bass

```python
import numpy as np
import jax
import jax.numpy as jnp

def _softmax(x, axis=-1):
    return jax.nn.softmax(x, axis=axis)

def _gelu(x):
    return jax.nn.gelu(x, approximate=True)

def _silu(x):
    return jax.nn.silu(x)

def _sigmoid(x):
    return jax.nn.sigmoid(x)

def _layernorm(x, axis=-1, eps=1e-05):
    m = jnp.mean(x, axis=axis, keepdims=True)
    v = jnp.var(x, axis=axis, keepdims=True)
    return (x - m) / jnp.sqrt(v + eps)

def _scatter_add(tgt, idx, src, axis=0):
    return tgt.at[idx].add(src)

def _segment_sum(src, seg, n):
    return jax.ops.segment_sum(src, seg, n)
kernel_name = 'mk_hybrid_d1_jaxref_r8_f02bd1'

def setup_inputs(seed: int=0):
    np.random.seed(seed)
    _w = jnp.asarray

    def _L0_attn_a_setup():
        import jax, jax.numpy as jnp
        import numpy as np
        from jax import lax
        B_, L_, D_MODEL = (2, 128, 128)
        D_STATE, D_CONV, EXPAND = (16, 4, 2)
        D_INNER = EXPAND * D_MODEL
        DT_RANK = (D_MODEL + 15) // 16
        LN_EPS = 1e-05

        def _silu(v):
            return v * jax.nn.sigmoid(v)

        def _mamba_params(key):
            ks = jax.random.split(key, 6)
            g = lambda k, shp, sc: jax.random.normal(k, shp, jnp.float32) * sc
            return {'in_proj_w': g(ks[0], (2 * D_INNER, D_MODEL), D_MODEL ** (-0.5)), 'conv_w': g(ks[1], (D_INNER, D_CONV), D_CONV ** (-0.5)), 'conv_b': jnp.zeros((D_INNER,), jnp.float32), 'x_proj_w': g(ks[2], (DT_RANK + 2 * D_STATE, D_INNER), D_INNER ** (-0.5)), 'dt_proj_w': g(ks[3], (D_INNER, DT_RANK), DT_RANK ** (-0.5)), 'dt_proj_b': jax.random.uniform(ks[4], (D_INNER,), jnp.float32, -4.0, -2.0), 'A_log': jnp.log(jnp.broadcast_to(jnp.arange(1, D_STATE + 1, dtype=jnp.float32), (D_INNER, D_STATE))), 'D': jnp.ones((D_INNER,), jnp.float32), 'out_proj_w': g(ks[5], (D_MODEL, D_INNER), D_INNER ** (-0.5))}

        def _mamba(x, in_proj_w, conv_w, conv_b, x_proj_w, dt_proj_w, dt_proj_b, A_log, D, out_proj_w):
            b, l, _ = x.shape
            xz = x @ in_proj_w.T
            xi, z = jnp.split(xz, 2, axis=-1)
            xp = jnp.pad(xi, ((0, 0), (D_CONV - 1, 0), (0, 0)))
            xc = conv_b + sum((xp[:, k:k + l, :] * conv_w[:, k] for k in range(D_CONV)))
            xc = _silu(xc)
            dbl = xc @ x_proj_w.T
            dt = jax.nn.softplus(dbl[..., :DT_RANK] @ dt_proj_w.T + dt_proj_b)
            Bm = dbl[..., DT_RANK:DT_RANK + D_STATE]
            Cm = dbl[..., DT_RANK + D_STATE:]
            A = -jnp.exp(A_log)
            dA = jnp.exp(dt[..., None] * A)
            dBu = (dt * xc)[..., None] * Bm[:, :, None, :]

            def step(h, inp):
                dA_t, dBu_t, C_t = inp
                h = dA_t * h + dBu_t
                return (h, jnp.einsum('bdn,bn->bd', h, C_t))
            h0 = jnp.zeros((b, D_INNER, D_STATE), x.dtype)
            _, ys = lax.scan(step, h0, (dA.transpose(1, 0, 2, 3), dBu.transpose(1, 0, 2, 3), Cm.transpose(1, 0, 2)))
            y = ys.transpose(1, 0, 2) + xc * D
            y = y * _silu(z)
            return y @ out_proj_w.T
        key = jax.random.key(seed)
        kx, kf, kb = jax.random.split(key, 3)
        inp = {'x': jax.random.normal(kx, (B_, L_, D_MODEL), jnp.float32)}
        for pref, k in (('fwd_', kf), ('bwd_', kb)):
            for name, val in _mamba_params(k).items():
                inp[pref + name] = val
        inp['ln_gamma'] = jnp.ones((D_MODEL,), jnp.float32)
        inp['ln_beta'] = jnp.zeros((D_MODEL,), jnp.float32)
        return inp
    _L0_attn_a_in = _L0_attn_a_setup()

    def _L0_attn_b_setup():
        import jax, jax.numpy as jnp
        import numpy as np
        B, T, C = (8, 256, 128)
        H = 4 * C
        N_LAYER, LAYER_ID = (12, 2)
        K_CLAMP = 60.0
        LN_EPS = 1e-05

        def _ln(x, g, b):
            m = jnp.mean(x, axis=-1, keepdims=True)
            v = jnp.var(x, axis=-1, keepdims=True)
            return (x - m) * jax.lax.rsqrt(v + LN_EPS) * g + b

        def _mix(x, time_mix, combined_mix):
            c = x.shape[-1]
            xm1 = jnp.pad(x[:, :-1], ((0, 0), (1, 0), (0, 0)))
            xp1 = jnp.pad(x[:, 1:], ((0, 0), (0, 1), (0, 0)))
            xc = jnp.concatenate([xm1[..., :c // 2], xp1[..., c // 2:]], axis=-1)
            return x * time_mix + xm1 * (1.0 - time_mix) + xc * combined_mix

        def _wkv(time_decay, time_first, k, v):
            ed = jnp.exp(-jnp.exp(time_decay))
            eu = jnp.exp(time_first)

            def step(carry, kv_t):
                a, b = carry
                kt, vt = kv_t
                y = (a + eu * kt * vt) / (b + eu * kt)
                return ((ed * a + kt * vt, ed * b + kt), y)
            kT = jnp.swapaxes(k, 0, 1)
            vT = jnp.swapaxes(v, 0, 1)
            z = jnp.zeros_like(kT[0])
            _, y = jax.lax.scan(step, (z, z), (kT, vT))
            return jnp.swapaxes(y, 0, 1)

        def _time_mix_block(x, time_mix, combined_mix, time_decay, time_first, Wk, Wv, Wr, Wo):
            xm = _mix(x, time_mix, combined_mix)
            k = jnp.exp(jnp.minimum(xm @ Wk.T, K_CLAMP))
            v = xm @ Wv.T
            r = xm @ Wr.T
            wkv = _wkv(time_decay, time_first, k, v)
            return jax.nn.sigmoid(r) * wkv @ Wo.T

        def _channel_mix_block(x, time_mix, combined_mix, Fk, Fv, Fr):
            xm = _mix(x, time_mix, combined_mix)
            k = jnp.square(jax.nn.relu(xm @ Fk.T))
            kv = k @ Fv.T
            return jax.nn.sigmoid(xm @ Fr.T) * kv
        key = jax.random.key(seed)
        ks = jax.random.split(key, 9)
        s = 0.02
        x = jax.random.normal(ks[0], (B, T, C), jnp.float32)
        h = np.arange(C, dtype=np.float64)
        frac = (LAYER_ID - 1) / (N_LAYER - 2)
        f1 = 3.0 + frac * (1.2 - 3.0)
        f2 = 0.65 + frac * (0.4 - 0.65)
        decay_speed = np.power(f2, h / (C - 1) * 7.0) * f1
        tm = jnp.concatenate([jnp.zeros(C // 2), jnp.ones(C // 2)]).reshape(1, 1, C).astype(jnp.float32)
        return dict(x=x, ln1_g=jnp.ones((C,), jnp.float32), ln1_b=jnp.zeros((C,), jnp.float32), ln2_g=jnp.ones((C,), jnp.float32), ln2_b=jnp.zeros((C,), jnp.float32), att_time_mix=tm, att_combined_mix=jnp.full((1, 1, C), 0.01, jnp.float32), time_decay=jnp.asarray(np.log(decay_speed), jnp.float32), time_first=jnp.full((C,), float(np.log(0.3)), jnp.float32), Wk=jax.random.normal(ks[1], (C, C), jnp.float32) * s, Wv=jax.random.normal(ks[2], (C, C), jnp.float32) * s, Wr=jax.random.normal(ks[3], (C, C), jnp.float32) * s, Wo=jax.random.normal(ks[4], (C, C), jnp.float32) * s, ffn_time_mix=tm, ffn_combined_mix=jnp.full((1, 1, C), 0.01, jnp.float32), Fk=jax.random.normal(ks[5], (H, C), jnp.float32) * s, Fv=jax.random.normal(ks[6], (C, H), jnp.float32) * s, Fr=jax.random.normal(ks[7], (C, C), jnp.float32) * s)
    _L0_attn_b_in = _L0_attn_b_setup()

    def _L0_ffn_setup():
        import jax, jax.numpy as jnp
        import numpy as np
        B, L, H, E, I = (4, 256, 128, 8, 512)
        S = B * L
        CAP_FACTOR_EVAL = 2.0
        MIN_CAP = 4
        _cap = int(np.floor(CAP_FACTOR_EVAL * S / E))
        _cap += _cap % 2
        CAPACITY = max(_cap, MIN_CAP)

        def _layer_norm(x, g, b, eps=1e-05):
            mu = x.mean(-1, keepdims=True)
            var = ((x - mu) ** 2).mean(-1, keepdims=True)
            return (x - mu) * jax.lax.rsqrt(var + eps) * g + b
        key = jax.random.key(seed)
        ks = jax.random.split(key, 8)
        gate_std = float(np.sqrt(0.1 / H))
        return {'inputs': jax.random.normal(ks[0], (B, L, H), jnp.float32), 'gate_weight': jax.random.normal(ks[1], (E, H), jnp.float32) * gate_std, 'ln_gamma': jnp.ones((H,), jnp.float32), 'ln_beta': jnp.zeros((H,), jnp.float32), 'wi': jax.random.normal(ks[2], (E, H, I), jnp.float32) * float(1.0 / np.sqrt(H)), 'wo': jax.random.normal(ks[3], (E, I, H), jnp.float32) * float(1.0 / np.sqrt(I)), 'conf_w1': jax.random.normal(ks[4], (H // 2, H), jnp.float32) * float(np.sqrt(2.0 / (H + H // 2))), 'conf_b1': -jnp.ones((H // 2,), jnp.float32), 'conf_w2': jax.random.normal(ks[5], (1, H // 2), jnp.float32) * float(np.sqrt(2.0 / (1 + H // 2))), 'conf_b2': -jnp.ones((1,), jnp.float32), 'comp_w': jax.random.normal(ks[6], (1, H), jnp.float32) * float(1.0 / np.sqrt(H)), 'comp_b': jnp.zeros((1,), jnp.float32)}
    _L0_ffn_in = _L0_ffn_setup()
    _d = {'L0_attn_a_x': _L0_attn_a_in['x'], 'L0_attn_a_fwd_in_proj_w': _L0_attn_a_in['fwd_in_proj_w'], 'L0_attn_a_fwd_conv_w': _L0_attn_a_in['fwd_conv_w'], 'L0_attn_a_fwd_conv_b': _L0_attn_a_in['fwd_conv_b'], 'L0_attn_a_fwd_x_proj_w': _L0_attn_a_in['fwd_x_proj_w'], 'L0_attn_a_fwd_dt_proj_w': _L0_attn_a_in['fwd_dt_proj_w'], 'L0_attn_a_fwd_dt_proj_b': _L0_attn_a_in['fwd_dt_proj_b'], 'L0_attn_a_fwd_A_log': _L0_attn_a_in['fwd_A_log'], 'L0_attn_a_fwd_D': _L0_attn_a_in['fwd_D'], 'L0_attn_a_fwd_out_proj_w': _L0_attn_a_in['fwd_out_proj_w'], 'L0_attn_a_bwd_in_proj_w': _L0_attn_a_in['bwd_in_proj_w'], 'L0_attn_a_bwd_conv_w': _L0_attn_a_in['bwd_conv_w'], 'L0_attn_a_bwd_conv_b': _L0_attn_a_in['bwd_conv_b'], 'L0_attn_a_bwd_x_proj_w': _L0_attn_a_in['bwd_x_proj_w'], 'L0_attn_a_bwd_dt_proj_w': _L0_attn_a_in['bwd_dt_proj_w'], 'L0_attn_a_bwd_dt_proj_b': _L0_attn_a_in['bwd_dt_proj_b'], 'L0_attn_a_bwd_A_log': _L0_attn_a_in['bwd_A_log'], 'L0_attn_a_bwd_D': _L0_attn_a_in['bwd_D'], 'L0_attn_a_bwd_out_proj_w': _L0_attn_a_in['bwd_out_proj_w'], 'L0_attn_a_ln_gamma': _L0_attn_a_in['ln_gamma'], 'L0_attn_a_ln_beta': _L0_attn_a_in['ln_beta'], 'L0_attn_b_ln1_g': _L0_attn_b_in['ln1_g'], 'L0_attn_b_ln1_b': _L0_attn_b_in['ln1_b'], 'L0_attn_b_ln2_g': _L0_attn_b_in['ln2_g'], 'L0_attn_b_ln2_b': _L0_attn_b_in['ln2_b'], 'L0_attn_b_att_time_mix': _L0_attn_b_in['att_time_mix'], 'L0_attn_b_att_combined_mix': _L0_attn_b_in['att_combined_mix'], 'L0_attn_b_time_decay': _L0_attn_b_in['time_decay'], 'L0_attn_b_time_first': _L0_attn_b_in['time_first'], 'L0_attn_b_Wk': _L0_attn_b_in['Wk'], 'L0_attn_b_Wv': _L0_attn_b_in['Wv'], 'L0_attn_b_Wr': _L0_attn_b_in['Wr'], 'L0_attn_b_Wo': _L0_attn_b_in['Wo'], 'L0_attn_b_ffn_time_mix': _L0_attn_b_in['ffn_time_mix'], 'L0_attn_b_ffn_combined_mix': _L0_attn_b_in['ffn_combined_mix'], 'L0_attn_b_Fk': _L0_attn_b_in['Fk'], 'L0_attn_b_Fv': _L0_attn_b_in['Fv'], 'L0_attn_b_Fr': _L0_attn_b_in['Fr'], 'L0_ffn_gate_weight': _L0_ffn_in['gate_weight'], 'L0_ffn_ln_gamma': _L0_ffn_in['ln_gamma'], 'L0_ffn_ln_beta': _L0_ffn_in['ln_beta'], 'L0_ffn_wi': _L0_ffn_in['wi'], 'L0_ffn_wo': _L0_ffn_in['wo'], 'L0_ffn_conf_w1': _L0_ffn_in['conf_w1'], 'L0_ffn_conf_b1': _L0_ffn_in['conf_b1'], 'L0_ffn_conf_w2': _L0_ffn_in['conf_w2'], 'L0_ffn_conf_b2': _L0_ffn_in['conf_b2'], 'L0_ffn_comp_w': _L0_ffn_in['comp_w'], 'L0_ffn_comp_b': _L0_ffn_in['comp_b']}
    _x0 = _d['L0_attn_a_x']
    _d['L0_attn_a_x'] = jax.random.normal(jax.random.fold_in(jax.random.key(seed), 1), (16, 256, 128), dtype=_x0.dtype)
    del _x0
    return _d

def reference(L0_attn_a_x, L0_attn_a_fwd_in_proj_w, L0_attn_a_fwd_conv_w, L0_attn_a_fwd_conv_b, L0_attn_a_fwd_x_proj_w, L0_attn_a_fwd_dt_proj_w, L0_attn_a_fwd_dt_proj_b, L0_attn_a_fwd_A_log, L0_attn_a_fwd_D, L0_attn_a_fwd_out_proj_w, L0_attn_a_bwd_in_proj_w, L0_attn_a_bwd_conv_w, L0_attn_a_bwd_conv_b, L0_attn_a_bwd_x_proj_w, L0_attn_a_bwd_dt_proj_w, L0_attn_a_bwd_dt_proj_b, L0_attn_a_bwd_A_log, L0_attn_a_bwd_D, L0_attn_a_bwd_out_proj_w, L0_attn_a_ln_gamma, L0_attn_a_ln_beta, L0_attn_b_ln1_g, L0_attn_b_ln1_b, L0_attn_b_ln2_g, L0_attn_b_ln2_b, L0_attn_b_att_time_mix, L0_attn_b_att_combined_mix, L0_attn_b_time_decay, L0_attn_b_time_first, L0_attn_b_Wk, L0_attn_b_Wv, L0_attn_b_Wr, L0_attn_b_Wo, L0_attn_b_ffn_time_mix, L0_attn_b_ffn_combined_mix, L0_attn_b_Fk, L0_attn_b_Fv, L0_attn_b_Fr, L0_ffn_gate_weight, L0_ffn_ln_gamma, L0_ffn_ln_beta, L0_ffn_wi, L0_ffn_wo, L0_ffn_conf_w1, L0_ffn_conf_b1, L0_ffn_conf_w2, L0_ffn_conf_b2, L0_ffn_comp_w, L0_ffn_comp_b):

    def _L0_attn_a_ref(x, fwd_in_proj_w, fwd_conv_w, fwd_conv_b, fwd_x_proj_w, fwd_dt_proj_w, fwd_dt_proj_b, fwd_A_log, fwd_D, fwd_out_proj_w, bwd_in_proj_w, bwd_conv_w, bwd_conv_b, bwd_x_proj_w, bwd_dt_proj_w, bwd_dt_proj_b, bwd_A_log, bwd_D, bwd_out_proj_w, ln_gamma, ln_beta):
        import jax, jax.numpy as jnp
        import numpy as np
        from jax import lax
        B_, L_, D_MODEL = (2, 128, 128)
        D_STATE, D_CONV, EXPAND = (16, 4, 2)
        D_INNER = EXPAND * D_MODEL
        DT_RANK = (D_MODEL + 15) // 16
        LN_EPS = 1e-05

        def _silu(v):
            return v * jax.nn.sigmoid(v)

        def _mamba_params(key):
            ks = jax.random.split(key, 6)
            g = lambda k, shp, sc: jax.random.normal(k, shp, jnp.float32) * sc
            return {'in_proj_w': g(ks[0], (2 * D_INNER, D_MODEL), D_MODEL ** (-0.5)), 'conv_w': g(ks[1], (D_INNER, D_CONV), D_CONV ** (-0.5)), 'conv_b': jnp.zeros((D_INNER,), jnp.float32), 'x_proj_w': g(ks[2], (DT_RANK + 2 * D_STATE, D_INNER), D_INNER ** (-0.5)), 'dt_proj_w': g(ks[3], (D_INNER, DT_RANK), DT_RANK ** (-0.5)), 'dt_proj_b': jax.random.uniform(ks[4], (D_INNER,), jnp.float32, -4.0, -2.0), 'A_log': jnp.log(jnp.broadcast_to(jnp.arange(1, D_STATE + 1, dtype=jnp.float32), (D_INNER, D_STATE))), 'D': jnp.ones((D_INNER,), jnp.float32), 'out_proj_w': g(ks[5], (D_MODEL, D_INNER), D_INNER ** (-0.5))}

        def _mamba(x, in_proj_w, conv_w, conv_b, x_proj_w, dt_proj_w, dt_proj_b, A_log, D, out_proj_w):
            b, l, _ = x.shape
            xz = x @ in_proj_w.T
            xi, z = jnp.split(xz, 2, axis=-1)
            xp = jnp.pad(xi, ((0, 0), (D_CONV - 1, 0), (0, 0)))
            xc = conv_b + sum((xp[:, k:k + l, :] * conv_w[:, k] for k in range(D_CONV)))
            xc = _silu(xc)
            dbl = xc @ x_proj_w.T
            dt = jax.nn.softplus(dbl[..., :DT_RANK] @ dt_proj_w.T + dt_proj_b)
            Bm = dbl[..., DT_RANK:DT_RANK + D_STATE]
            Cm = dbl[..., DT_RANK + D_STATE:]
            A = -jnp.exp(A_log)
            dA = jnp.exp(dt[..., None] * A)
            dBu = (dt * xc)[..., None] * Bm[:, :, None, :]

            def step(h, inp):
                dA_t, dBu_t, C_t = inp
                h = dA_t * h + dBu_t
                return (h, jnp.einsum('bdn,bn->bd', h, C_t))
            h0 = jnp.zeros((b, D_INNER, D_STATE), x.dtype)
            _, ys = lax.scan(step, h0, (dA.transpose(1, 0, 2, 3), dBu.transpose(1, 0, 2, 3), Cm.transpose(1, 0, 2)))
            y = ys.transpose(1, 0, 2) + xc * D
            y = y * _silu(z)
            return y @ out_proj_w.T
        yf = _mamba(x, fwd_in_proj_w, fwd_conv_w, fwd_conv_b, fwd_x_proj_w, fwd_dt_proj_w, fwd_dt_proj_b, fwd_A_log, fwd_D, fwd_out_proj_w)
        yb = _mamba(jnp.flip(x, 1), bwd_in_proj_w, bwd_conv_w, bwd_conv_b, bwd_x_proj_w, bwd_dt_proj_w, bwd_dt_proj_b, bwd_A_log, bwd_D, bwd_out_proj_w)
        yo = yf + jnp.flip(yb, 1)
        mu = jnp.mean(yo, axis=-1, keepdims=True)
        var = jnp.mean(jnp.square(yo - mu), axis=-1, keepdims=True)
        return ln_gamma * (yo - mu) / jnp.sqrt(var + LN_EPS) + ln_beta

    def _L0_attn_b_ref(x, ln1_g, ln1_b, ln2_g, ln2_b, att_time_mix, att_combined_mix, time_decay, time_first, Wk, Wv, Wr, Wo, ffn_time_mix, ffn_combined_mix, Fk, Fv, Fr):
        import jax, jax.numpy as jnp
        import numpy as np
        B, T, C = (8, 256, 128)
        H = 4 * C
        N_LAYER, LAYER_ID = (12, 2)
        K_CLAMP = 60.0
        LN_EPS = 1e-05

        def _ln(x, g, b):
            m = jnp.mean(x, axis=-1, keepdims=True)
            v = jnp.var(x, axis=-1, keepdims=True)
            return (x - m) * jax.lax.rsqrt(v + LN_EPS) * g + b

        def _mix(x, time_mix, combined_mix):
            c = x.shape[-1]
            xm1 = jnp.pad(x[:, :-1], ((0, 0), (1, 0), (0, 0)))
            xp1 = jnp.pad(x[:, 1:], ((0, 0), (0, 1), (0, 0)))
            xc = jnp.concatenate([xm1[..., :c // 2], xp1[..., c // 2:]], axis=-1)
            return x * time_mix + xm1 * (1.0 - time_mix) + xc * combined_mix

        def _wkv(time_decay, time_first, k, v):
            ed = jnp.exp(-jnp.exp(time_decay))
            eu = jnp.exp(time_first)

            def step(carry, kv_t):
                a, b = carry
                kt, vt = kv_t
                y = (a + eu * kt * vt) / (b + eu * kt)
                return ((ed * a + kt * vt, ed * b + kt), y)
            kT = jnp.swapaxes(k, 0, 1)
            vT = jnp.swapaxes(v, 0, 1)
            z = jnp.zeros_like(kT[0])
            _, y = jax.lax.scan(step, (z, z), (kT, vT))
            return jnp.swapaxes(y, 0, 1)

        def _time_mix_block(x, time_mix, combined_mix, time_decay, time_first, Wk, Wv, Wr, Wo):
            xm = _mix(x, time_mix, combined_mix)
            k = jnp.exp(jnp.minimum(xm @ Wk.T, K_CLAMP))
            v = xm @ Wv.T
            r = xm @ Wr.T
            wkv = _wkv(time_decay, time_first, k, v)
            return jax.nn.sigmoid(r) * wkv @ Wo.T

        def _channel_mix_block(x, time_mix, combined_mix, Fk, Fv, Fr):
            xm = _mix(x, time_mix, combined_mix)
            k = jnp.square(jax.nn.relu(xm @ Fk.T))
            kv = k @ Fv.T
            return jax.nn.sigmoid(xm @ Fr.T) * kv
        x = _ln(x, ln1_g, ln1_b)
        x = x + _time_mix_block(x, att_time_mix, att_combined_mix, time_decay, time_first, Wk, Wv, Wr, Wo)
        x = _ln(x, ln2_g, ln2_b)
        x = x + _channel_mix_block(x, ffn_time_mix, ffn_combined_mix, Fk, Fv, Fr)
        return x

    def _L0_ffn_ref(inputs, gate_weight, ln_gamma, ln_beta, wi, wo, conf_w1, conf_b1, conf_w2, conf_b2, comp_w, comp_b):
        import jax, jax.numpy as jnp
        import numpy as np
        B, L, H, E, I = (4, 256, 128, 8, 512)
        S = B * L
        CAP_FACTOR_EVAL = 2.0
        MIN_CAP = 4
        _cap = int(np.floor(CAP_FACTOR_EVAL * S / E))
        _cap += _cap % 2
        CAPACITY = max(_cap, MIN_CAP)

        def _layer_norm(x, g, b, eps=1e-05):
            mu = x.mean(-1, keepdims=True)
            var = ((x - mu) ** 2).mean(-1, keepdims=True)
            return (x - mu) * jax.lax.rsqrt(var + eps) * g + b
        tokens = inputs.reshape(-1, H)
        residual = tokens
        tokens = _layer_norm(tokens, ln_gamma, ln_beta)
        complexity_score = jax.nn.sigmoid(tokens @ comp_w.T + comp_b).mean()
        hdn = jax.nn.relu(tokens @ conf_w1.T + conf_b1)
        confidence_score = jax.nn.sigmoid(hdn @ conf_w2.T + conf_b2).mean()
        logits = tokens.astype(jnp.float32) @ gate_weight.astype(jnp.float32).T
        probs = jax.nn.softmax(logits, axis=-1)
        top1 = jnp.argmax(logits, axis=-1)
        onehot = jax.nn.one_hot(top1, E, dtype=jnp.int32)
        rank_e = jnp.cumsum(onehot, axis=0) - onehot
        rank = jnp.sum(rank_e * onehot, axis=-1)
        keep = rank < CAPACITY
        weight = jnp.take_along_axis(probs, top1[:, None], axis=-1)[:, 0]
        weight = (weight * keep).astype(tokens.dtype)
        slot = jnp.where(keep, rank, 0)
        dispatch = jnp.zeros((E, CAPACITY, H), tokens.dtype)
        dispatch = dispatch.at[top1, slot].add(tokens * keep[:, None])
        h = jax.nn.gelu(jnp.einsum('ech,ehi->eci', dispatch, wi), approximate=False)
        expert_out = jnp.einsum('eci,eih->ech', h, wo)
        combined = weight[:, None] * expert_out[top1, slot]
        out = (residual + combined).reshape(inputs.shape)
        return out
    x = L0_attn_a_x
    x = x + _L0_attn_a_ref(_layernorm(x, axis=-1), L0_attn_a_fwd_in_proj_w, L0_attn_a_fwd_conv_w, L0_attn_a_fwd_conv_b, L0_attn_a_fwd_x_proj_w, L0_attn_a_fwd_dt_proj_w, L0_attn_a_fwd_dt_proj_b, L0_attn_a_fwd_A_log, L0_attn_a_fwd_D, L0_attn_a_fwd_out_proj_w, L0_attn_a_bwd_in_proj_w, L0_attn_a_bwd_conv_w, L0_attn_a_bwd_conv_b, L0_attn_a_bwd_x_proj_w, L0_attn_a_bwd_dt_proj_w, L0_attn_a_bwd_dt_proj_b, L0_attn_a_bwd_A_log, L0_attn_a_bwd_D, L0_attn_a_bwd_out_proj_w, L0_attn_a_ln_gamma, L0_attn_a_ln_beta)
    x = x + _L0_ffn_ref(_layernorm(x, axis=-1), L0_ffn_gate_weight, L0_ffn_ln_gamma, L0_ffn_ln_beta, L0_ffn_wi, L0_ffn_wo, L0_ffn_conf_w1, L0_ffn_conf_b1, L0_ffn_conf_w2, L0_ffn_conf_b2, L0_ffn_comp_w, L0_ffn_comp_b)
    x = x + _L0_attn_b_ref(_layernorm(x, axis=-1), L0_attn_b_ln1_g, L0_attn_b_ln1_b, L0_attn_b_ln2_g, L0_attn_b_ln2_b, L0_attn_b_att_time_mix, L0_attn_b_att_combined_mix, L0_attn_b_time_decay, L0_attn_b_time_first, L0_attn_b_Wk, L0_attn_b_Wv, L0_attn_b_Wr, L0_attn_b_Wo, L0_attn_b_ffn_time_mix, L0_attn_b_ffn_combined_mix, L0_attn_b_Fk, L0_attn_b_Fv, L0_attn_b_Fr)
    x = x + _L0_ffn_ref(_layernorm(x, axis=-1), L0_ffn_gate_weight, L0_ffn_ln_gamma, L0_ffn_ln_beta, L0_ffn_wi, L0_ffn_wo, L0_ffn_conf_w1, L0_ffn_conf_b1, L0_ffn_conf_w2, L0_ffn_conf_b2, L0_ffn_comp_w, L0_ffn_comp_b)
    return x

_drawn_inputs = setup_inputs


def setup_inputs(seed=0):
    import zlib

    import numpy as np

    out = dict(_drawn_inputs(seed))
    spreads = {'L0_attn_a_fwd_conv_b': (0.0, 0.1),
     'L0_attn_a_fwd_D': (1.0, 0.2),
     'L0_attn_a_bwd_conv_b': (0.0, 0.1),
     'L0_attn_a_bwd_D': (1.0, 0.2),
     'L0_attn_a_ln_gamma': (1.0, 0.2),
     'L0_attn_a_ln_beta': (0.0, 0.1),
     'L0_attn_b_ln1_g': (1.0, 0.2),
     'L0_attn_b_ln1_b': (0.0, 0.1),
     'L0_attn_b_ln2_g': (1.0, 0.2),
     'L0_attn_b_ln2_b': (0.0, 0.269),
     'L0_attn_b_att_combined_mix': (0.009999999776482582, 0.6),
     'L0_attn_b_time_first': (-1.2039728164672852, 0.6),
     'L0_attn_b_ffn_combined_mix': (0.009999999776482582, 0.6),
     'L0_ffn_ln_gamma': (1.0, 0.2),
     'L0_ffn_ln_beta': (0.0, 0.293),
     'L0_ffn_conf_b1': (-1.0, 0.2)}
    factors = {'L0_attn_b_att_time_mix': 8.0,
     'L0_attn_b_time_decay': 8.0,
     'L0_attn_b_Wk': 8.0,
     'L0_attn_b_Wv': 8.0,
     'L0_attn_b_Wr': 8.0,
     'L0_attn_b_Wo': 8.0,
     'L0_attn_b_ffn_time_mix': 8.0,
     'L0_attn_b_Fk': 8.0,
     'L0_attn_b_Fv': 8.0,
     'L0_attn_b_Fr': 8.0}
    for name, (base, spread) in spreads.items():
        noise = np.random.default_rng([zlib.crc32(name.encode()), seed]).standard_normal(out[name].shape)
        drawn = base * np.exp(spread * noise) if base else spread * noise
        out[name] = jnp.asarray(drawn.astype(out[name].dtype))
    for name, factor in factors.items():
        out[name] = (out[name] * factor).astype(out[name].dtype)
    return out
```

```python
from contextlib import ExitStack

import concourse.bass as bass
from concourse import mybir

F32 = mybir.dt.float32
BF16 = mybir.dt.bfloat16
I32 = mybir.dt.int32
ALU = mybir.AluOpType
ACT = mybir.ActivationFunctionType
AX = mybir.AxisListType

P = 128
BATCH, T, D = 16, 256, 128
NTOK = BATCH * T
TILES = NTOK // P
GROUPS = 8
TG = TILES // GROUPS
QUARTERS = 4
TQ = TILES // QUARTERS
PAD = 3
TP = T + 2 * PAD

INNER, STATE, TAPS, RANK = 256, 16, 4, 8
HALVES = INNER // P
CB = 4
CT = CB * T
CHUNKS = BATCH // CB
STEPS = HALVES * STATE

EXPERTS, CAP, FF = 8, 256, 512
FT = FF // P
SLOTS = EXPERTS * CAP
STILES = SLOTS // P
CLAMP = 60.0
EPS = 1e-5

COLS = ["conv_b_f0", "conv_b_f1", "conv_b_b0", "conv_b_b1", "dt_b_f0", "dt_b_f1", "dt_b_b0", "dt_b_b1",
        "D_f0", "D_f1", "D_b0", "D_b1", "ffn_g", "ffn_b", "ln1_g", "ln1_b", "ln2_g", "ln2_b",
        "att_tm", "att_cm", "ffn_tm", "ffn_cm", "decay", "first", "lo_mask", "hi_mask"]
COL = {n: i for i, n in enumerate(COLS)}


def layer(nc, x_in, cols_in, alog_in, rows_in, conv_in, inproj_in, xproj_in, dtproj_in, outproj_in, wsq_in,
          fk_in, fv_in, gate_in, wi_in, wo_in, ident_in, sel_in, tri_in, route_in, out):
    dispatched = nc.dram_tensor("dispatched", (SLOTS + NTOK, D), F32, kind="Internal").ap()
    expert_rows = nc.dram_tensor("expert_rows", (SLOTS, D), F32, kind="Internal").ap()

    with ExitStack() as ctx:
        def sb(name, shape, dt=F32):
            return ctx.enter_context(nc.sbuf_tensor(name, shape, dt))

        sems = {}

        def sem(name):
            if name not in sems:
                sems[name] = ctx.enter_context(nc.semaphore(name))
            return sems[name]

        x = sb("x", [P, TILES, D])
        r = sb("r", [P, TILES, D])
        tokn = sb("tokn", [P, TILES, D])
        xT = sb("xT", [P, BATCH, TP])
        work = sb("work", [P, 4 * NTOK])
        wi = sb("wi", [P, EXPERTS, FF])
        wo = sb("wo", [P, EXPERTS, FT, D])
        w_misc = sb("w_misc", [P, 5120])
        sel = sb("sel", [96, 2 * STATE, P], BF16)
        ident = sb("ident", [P, P])
        tri = sb("tri", [P, 2, P], BF16)
        route = sb("route", [P, EXPERTS + 1 + TILES])
        cols = sb("cols", [P, len(COLS)])
        rows = sb("rows", [P, 2, D])
        acols = sb("acols", [P, 2, HALVES, STATE])
        gateT = sb("gateT", [P, EXPERTS])
        small = sb("small", [P, 16])
        stats = sb("stats", [P, TILES, 6])
        mv = sb("mv", [P, TILES, 2])
        sd = sb("sd", [P, TILES])
        rstd = sb("rstd", [P, TILES])
        PS = ctx.enter_context(nc.psum_tensor("PS", [P, 8, 512], F32))

        ecol, negone = small[:, 0:1], small[:, 1:2]

        def col(name):
            return cols[:, COL[name]:COL[name] + 1]

        inproj = w_misc[:, 0:1024].rearrange("p (r n) -> p r n", r=2)
        convw = w_misc[:, 1024:3072].rearrange("p (r k n) -> p r k n", r=2, k=TAPS)
        xproj = w_misc[:, 3072:3072 + 2 * HALVES * 104].rearrange("p (r h n) -> p r h n", r=2, h=HALVES)
        outproj = w_misc[:, 3520:4032].rearrange("p (r h n) -> p r h n", r=2, h=HALVES)
        diagD = w_misc[:, 4032:4544].rearrange("p (r h n) -> p r h n", r=2, h=HALVES)
        dtproj = w_misc[0:RANK, 4544:5056].rearrange("p (r n) -> p r n", r=2)

        def at(k, n=HALVES):
            return work[:, k * CT:(k + n) * CT].rearrange("p (h t) -> p h t", h=n)

        xc, dt, du, sz = at(0), at(2), at(4), at(6)
        dA, hs, Cs, hC = at(8), at(10), at(12), at(14)
        parts = sb("parts", [96, CT], BF16)
        resid = sb("resid", [96, CT])
        dtr = sb("dtr", [RANK, CT])
        X = [PS[:, 0:2, :], PS[:, 2:4, :]]
        CS = PS[:, 4:6, :]
        Y = PS[:, 6:8, :]
        yo = tokn

        def flat(ap):
            return ap.rearrange("p a n -> p (a n)")

        eo = work[:, 0:2048].rearrange("p (s d) -> p s d", s=STILES)
        dispT = work[:, 2048:4096]
        rowsin = work[:, 4096:6144].rearrange("p (s d) -> p s d", s=STILES)
        hT = work[:, 6144:8192].rearrange("p (b i c) -> p b i c", b=2, i=FT)
        tokT = work[:, 8192:9216].rearrange("p (b t) -> p b t", b=2)
        rt = [work[:, 9216 + 256 * i:9472 + 256 * i].rearrange("p (t e) -> p t e", e=EXPERTS) for i in range(8)]
        rs = [work[:, 11264 + 32 * i:11296 + 32 * i] for i in range(12)]
        onehot = sb("onehot", [P, TILES, EXPERTS], BF16)
        put_at = sb("put_at", [P, TILES], I32)
        get_at = sb("get_at", [P, TILES], I32)
        weight = sb("weight", [P, TILES])
        ones = sb("ones", [P, TILES])

        xm = work[:, 0:NTOK]
        kS = work[:, NTOK:2 * NTOK]
        kvS = work[:, 2 * NTOK:3 * NTOK]
        rS = work[:, 3 * NTOK:4 * NTOK]
        wsq = w_misc[:, 0:640].rearrange("p (w n) -> p w n", w=5)
        fk = w_misc[:, 640:1152]
        fv = w_misc[:, 1152:1664].rearrange("p (i n) -> p i n", i=FT)
        edT = w_misc[:, 1664:1664 + CT].rearrange("p (b t) -> p b t", b=CB)
        a_s, b_s = r, tokn
        k2 = work[:, NTOK:2 * NTOK].rearrange("p (b i t) -> p b i t", b=2, i=FT)
        sg = work[:, 2 * NTOK:2 * NTOK + 1024].rearrange("p (b t) -> p b t", b=2)

        x_dram = x_in.rearrange("(q t p) d -> q p t d", q=QUARTERS, p=P)
        out_dram = out.rearrange("b t d -> (b t) d").rearrange("(q t p) d -> q p t d", q=QUARTERS, p=P)

        SETUP = 18

        block = ctx.enter_context(nc.Block())

        def sp_experts(sp, f):
            sp.wait_ge(sem(f"e{f}_put"), 16 * TILES)
            sp.dma_start(rowsin, dispatched[0:SLOTS, :].rearrange("(s p) d -> p s d", p=P)).then_inc(
                sem(f"e{f}_rows"), 16)
            for e in range(EXPERTS):
                sp.wait_ge(sem(f"e{f}_eo"), e + 1)
                sp.dma_start(expert_rows[CAP * e:CAP * e + CAP, :].rearrange("(s p) d -> p s d", p=P),
                             eo[:, 2 * e:2 * e + 2, :]).then_inc(sem(f"e{f}_stored"), 16)

        def act_experts(act, f):
            act_norm(act, f"e{f}a")
            act_norm(act, f"e{f}b")
            for g in range(GROUPS):
                act.wait_ge(sem(f"e{f}_turned"), g + 1)
                if g >= 2:
                    act.wait_ge(sem(f"e{f}_logit"), g - 1)
                nc.scalar.activation(tokT[:, g % 2, :], PS[:, g % 2, :], ACT.Identity, scale=col("ffn_g"),
                                     bias=col("ffn_b")).then_inc(sem(f"e{f}_tokT"), 1)
            act.wait_ge(sem(f"e{f}_sub"), 1)
            nc.scalar.activation(rt[1], rt[0], ACT.Exp).then_inc(sem(f"e{f}_prob"), 1)
            for g in range(STILES // TG):
                act.wait_ge(sem(f"e{f}_din"), g + 1)
                nc.scalar.activation(dispT[:, 512 * g:512 * g + 512], PS[:, g % 2, :], ACT.Identity,
                                     scale=col("ffn_g"), bias=col("ffn_b")).then_inc(sem(f"e{f}_dT"), 1)
            for e in range(EXPERTS):
                act.wait_ge(sem(f"e{f}_h"), e + 1)
                if e >= 2:
                    act.wait_ge(sem(f"e{f}_o"), e - 1)
                b = 4 + 2 * (e % 2)
                nc.scalar.activation(hT[:, e % 2].rearrange("p i c -> p (i c)"), flat(PS[:, b:b + 2, :]),
                                     ACT.Gelu).then_inc(sem(f"e{f}_gelu"), 1)

        def fold(rev, k):
            return convw[:, rev, k, :]

        def pe_experts(pe, f):
            mm = nc.tensor.matmul
            L = PS[:, 2, 0:TILES * EXPERTS].rearrange("p (t e) -> p t e", e=EXPERTS)

            def logits(g):
                pe.wait_ge(sem(f"e{f}_tokT"), g + 1)
                for i in range(TG):
                    last = mm(L[:, TG * g + i, :], tokT[:, g % 2, P * i:P * i + P], gateT[:], start=True, stop=True)
                last.then_inc(sem(f"e{f}_logit"), 1)

            for g in range(GROUPS):
                if g % 2 == 0:
                    pe.wait_ge(sem(f"e{f}b_out"), g // 2 + 1)
                if g >= 2:
                    pe.wait_ge(sem(f"e{f}_tokT"), g - 1)
                for i in range(TG):
                    last = nc.tensor.transpose(PS[:, g % 2, D * i:D * i + D], tokn[:, TG * g + i, :], ident[:])
                last.then_inc(sem(f"e{f}_turned"), 1)
                if g >= 1:
                    logits(g - 1)
            logits(GROUPS - 1)
            pe.wait_ge(sem(f"e{f}_onehot"), 1)
            oh = onehot[:].rearrange("p t e -> p (t e)")
            mm(PS[:, 3, 0:256], tri[:, 0, :], oh, start=True, stop=True)
            mm(PS[:, 3, 256:512], tri[:, 1, :], oh, start=True, stop=True).then_inc(sem(f"e{f}_counts"), 1)
            pe.wait_ge(sem(f"e{f}_rows"), 16)
            for g in range(STILES // TG):
                if g >= 2:
                    pe.wait_ge(sem(f"e{f}_dT"), g - 1)
                for i in range(TG):
                    last = nc.tensor.transpose(PS[:, g % 2, D * i:D * i + D], rowsin[:, TG * g + i, :], ident[:])
                last.then_inc(sem(f"e{f}_din"), 1)

            def second(e):
                pe.wait_ge(sem(f"e{f}_gelu"), e + 1)
                if e == 0:
                    pe.wait_ge(sem(f"e{f}_index"), 1)
                if e >= 2:
                    pe.wait_ge(sem(f"e{f}_eo"), e - 1)
                for s in range(2):
                    for i in range(FT):
                        last = mm(PS[:, 2 + e % 2, D * s:D * s + D], hT[:, e % 2, i, P * s:P * s + P],
                                  wo[:, e, i, :], start=(i == 0), stop=(i == FT - 1))
                last.then_inc(sem(f"e{f}_o"), 1)

            for e in range(EXPERTS):
                pe.wait_ge(sem(f"e{f}_dT"), e // 2 + 1)
                if e >= 2:
                    pe.wait_ge(sem(f"e{f}_gelu"), e - 1)
                for i in range(FT):
                    last = mm(PS[:, 4 + 2 * (e % 2) + i // 2, CAP * (i % 2):CAP * (i % 2) + CAP],
                              wi[:, e, P * i:P * i + P], dispT[:, CAP * e:CAP * e + CAP], start=True, stop=True)
                last.then_inc(sem(f"e{f}_h"), 1)
                if e >= 1:
                    second(e - 1)
            second(EXPERTS - 1)

        def dve_mix(dve, link, name, prev_w, next_w):
            for g in range(GROUPS):
                xg = xm[:, 512 * g:512 * g + 512].rearrange("p (b t) -> p b t", b=2)
                dve.wait_ge(sem(f"{name}_xm0"), g + 1)
                link(nc.vector.scalar_tensor_tensor(out=xg, in0=xT[:, 2 * g:2 * g + 2, PAD - 1:PAD - 1 + T],
                                                    scalar=prev_w, in1=xg, op0=ALU.mult, op1=ALU.add))
                nc.vector.scalar_tensor_tensor(out=xg, in0=xT[:, 2 * g:2 * g + 2, PAD + 1:PAD + 1 + T],
                                               scalar=next_w, in1=xg, op0=ALU.mult, op1=ALU.add).then_inc(
                    sem(f"{name}_xm"), 1)

        def dve_experts(dve, link, f):
            dve_norm_stats(dve, link, f"e{f}a", x)
            dve_norm_apply(dve, link, f"e{f}a", x, r)
            dve_norm_stats(dve, link, f"e{f}b", r)
            dve_norm_apply(dve, link, f"e{f}b", r, tokn)
            L = PS[:, 2, 0:256].rearrange("p (t e) -> p t e", e=EXPERTS)
            pre = PS[:, 3, 0:256].rearrange("p (t e) -> p t e", e=EXPERTS)
            tot = PS[:, 3, 256:512].rearrange("p (t e) -> p t e", e=EXPERTS)
            mx, mx2, rank, keep, slot, den = rs[0:6]
            own = route[:, EXPERTS + 1:EXPERTS + 1 + TILES]

            def per_expert(v):
                return v.rearrange("p (t e) -> p t e", e=1).broadcast_to([P, TILES, EXPERTS])

            dve.wait_ge(sem(f"e{f}_logit"), GROUPS)
            link(nc.vector.tensor_reduce(mx, L, AX.X, ALU.max))
            nc.vector.tensor_tensor(rt[0], L, per_expert(mx), ALU.subtract).then_inc(sem(f"e{f}_sub"), 1)
            dve.wait_ge(sem(f"e{f}_sub"), 1)
            pri = route[:, 0:EXPERTS].rearrange("p (t e) -> p t e", t=1).broadcast_to([P, TILES, EXPERTS])
            link(nc.vector.scalar_tensor_tensor(out=rt[2], in0=rt[0], scalar=0.0, in1=pri, op0=ALU.is_ge,
                                                op1=ALU.mult))
            link(nc.vector.tensor_reduce(mx2, rt[2], AX.X, ALU.max))
            nc.vector.tensor_tensor(onehot[:], rt[2], per_expert(mx2), ALU.is_equal).then_inc(sem(f"e{f}_onehot"), 1)
            dve.wait_ge(sem(f"e{f}_onehot"), 1)
            dve.wait_ge(sem(f"e{f}_prob"), 1)
            link(nc.vector.tensor_reduce(den, rt[1], AX.X, ALU.add))
            nc.vector.reciprocal(weight[:], den)
            dve.wait_ge(sem("ones"), 1)
            dve.wait_ge(sem(f"e{f}_counts"), 1)
            nc.vector.memset(rt[4][:, 0:1, :], 0.0)
            link(nc.vector.tensor_copy(rt[3], tot))
            for e in range(EXPERTS):
                last = nc.vector.tensor_tensor_scan(rt[4][:, 1:TILES, e], ones[:, 1:TILES], rt[3][:, 0:TILES - 1, e],
                                                    0.0, ALU.mult, ALU.add)
            link(last)
            link(nc.vector.tensor_tensor(rt[5], rt[4], pre, ALU.add))
            link(nc.vector.tensor_tensor(rt[6], rt[5], onehot[:], ALU.mult))
            link(nc.vector.tensor_reduce(rank, rt[6], AX.X, ALU.add))
            link(nc.vector.tensor_scalar(keep, rank, float(CAP), None, ALU.is_lt))
            nc.vector.tensor_tensor(weight[:], weight[:], keep, ALU.mult)
            nc.vector.tensor_scalar(slot, mx2, -float(CAP), float(SLOTS), ALU.mult, ALU.add)
            link(nc.vector.tensor_tensor(rs[6], rank, keep, ALU.mult))
            link(nc.vector.tensor_tensor(slot, slot, rs[6], ALU.add))
            nc.vector.tensor_copy(get_at[:], slot)
            link(nc.vector.tensor_tensor(rs[7], slot, own, ALU.subtract))
            link(nc.vector.tensor_tensor(rs[8], rs[7], keep, ALU.mult))
            link(nc.vector.tensor_tensor(rs[9], rs[8], own, ALU.add))
            nc.vector.tensor_copy(put_at[:], rs[9]).then_inc(sem(f"e{f}_index"), 1)
            for e in range(EXPERTS):
                dve.wait_ge(sem(f"e{f}_o"), e + 1)
                nc.vector.tensor_copy(eo[:, 2 * e:2 * e + 2, :].rearrange("p s d -> p (s d)"),
                                      PS[:, 2 + e % 2, 0:2 * D]).then_inc(sem(f"e{f}_eo"), 1)
            link(nc.vector.tensor_tensor(x[:], x[:], r[:], ALU.add))
            for q in range(QUARTERS):
                dve.wait_ge(sem(f"e{f}_got{q}"), 16 * TQ)
                for j in range(TQ * q, TQ * q + TQ):
                    last = nc.vector.scalar_tensor_tensor(out=x[:, j, :], in0=tokn[:, j, :], scalar=weight[:, j:j + 1],
                                                          in1=x[:, j, :], op0=ALU.mult, op1=ALU.add)
                last.then_inc(sem(f"e{f}_x"), 1)

        def dve_norm_stats(dve, link, name, src, ready=None):
            for q in range(QUARTERS):
                if ready:
                    dve.wait_ge(sem(ready[0]), ready[1](q))
                for j in range(TQ * q, TQ * q + TQ):
                    last = nc.vector.bn_stats(stats[:, j, :], src[:, j, :])
                link(last)
                for j in range(TQ * q, TQ * q + TQ):
                    last = nc.vector.bn_aggr(mv[:, j, :], stats[:, j, :])
                last.then_inc(sem(f"{name}_var"), 1)

        def act_norm(act, name):
            for q in range(QUARTERS):
                act.wait_ge(sem(f"{name}_var"), q + 1)
                nc.scalar.activation(sd[:, TQ * q:TQ * q + TQ], mv[:, TQ * q:TQ * q + TQ, 1], ACT.Sqrt,
                                     bias=ecol).then_inc(sem(f"{name}_sd"), 1)

        def dve_norm_apply(dve, link, name, src, dst):
            for q in range(QUARTERS):
                dve.wait_ge(sem(f"{name}_sd"), q + 1)
                link(nc.vector.reciprocal(rstd[:, TQ * q:TQ * q + TQ], sd[:, TQ * q:TQ * q + TQ]))
                for j in range(TQ * q, TQ * q + TQ):
                    last = nc.vector.tensor_scalar(dst[:, j, :], src[:, j, :], mv[:, j, 0:1], rstd[:, j:j + 1],
                                                   ALU.subtract, ALU.mult)
                last.then_inc(sem(f"{name}_out"), 1)
            dve.wait_ge(sem(f"{name}_out"), QUARTERS)

        def pe_turn(pe, name, src, ready):
            for g in range(GROUPS):
                if g % 2 == 0:
                    pe.wait_ge(sem(ready), g // 2 + 1)
                if g >= 2:
                    pe.wait_ge(sem(f"{name}_out"), g - 1)
                for i in range(TG):
                    last = nc.tensor.transpose(PS[:, g % 2, D * i:D * i + D], src[:, TG * g + i, :], ident[:])
                last.then_inc(sem(f"{name}_in"), 1)

        def act_turn(act, name, scale, bias):
            for g in range(GROUPS):
                act.wait_ge(sem(f"{name}_in"), g + 1)
                nc.scalar.activation(xT[:, 2 * g:2 * g + 2, PAD:PAD + T],
                                     PS[:, g % 2, :].rearrange("p (b t) -> p b t", b=2), ACT.Identity,
                                     scale=scale, bias=bias).then_inc(sem(f"{name}_out"), 1)


        @block.sync
        def _(sp):
            for q in range(QUARTERS):
                sp.dma_start(x[:, TQ * q:TQ * q + TQ, :], x_dram[q]).then_inc(sem(f"x_in{q}"), 16)
            s = sem("setup_in")
            for dst, src in (
                (cols[:], cols_in), (acols[:], alog_in), (ident[:], ident_in), (sel[:], sel_in), (tri[:], tri_in),
                (route[:], route_in), (gateT[:], gate_in), (rows[:], rows_in.partition_broadcast(P)),
                (convw, conv_in.partition_broadcast(P)), (inproj, inproj_in),
                (xproj[:, 0], xproj_in[:, 0]), (xproj[:, 1], xproj_in[:, 1]),
                (outproj[:, 0], outproj_in[:, 0]), (outproj[:, 1], outproj_in[:, 1]),
                (dtproj, dtproj_in), (wi[:], wi_in), (wo[:, 0:4], wo_in[:, 0:4]), (wo[:, 4:8], wo_in[:, 4:8]),
            ):
                sp.dma_start(dst, src).then_inc(s, 16)
            sp.wait_ge(sem("r_zero"), 1)
            sp.dma_start(dispatched[0:SLOTS, :].rearrange("(s p) d -> p s d", p=P), r[:, 0:STILES, :]).then_inc(
                sem("slots_zeroed"), 16)

            sp_experts(sp, 0)
            s = sem("wb_in")
            for dst, src in ((wsq, wsq_in), (fk, fk_in), (fv, fv_in)):
                sp.dma_start(dst, src).then_inc(s, 16)
            sp_experts(sp, 1)
            for q in range(QUARTERS):
                sp.wait_ge(sem("e1_x"), q + 1)
                sp.dma_start(out_dram[q], x[:, TQ * q:TQ * q + TQ, :]).then_inc(sem("stored"), 16)
            sp.wait_ge(sem("stored"), 16 * QUARTERS)

        @block.gpsimd
        def _(pool):
            nc.gpsimd.memset(r[:, 0:STILES, :], 0.0).then_inc(sem("r_zero"), 1)
            nc.gpsimd.memset(xT[:, :, 0:PAD], 0.0)
            nc.gpsimd.memset(xT[:, :, PAD + T:TP], 0.0).then_inc(sem("pads_zero"), 1)
            nc.gpsimd.memset(hC[:, 0, 0:1], 0.0).then_inc(sem("m_hc"), 2)
            nc.gpsimd.memset(hC[:, 1, 0:1], 0.0).then_inc(sem("m_ysum"), 2)
            nc.gpsimd.memset(ones[:], 1.0).then_inc(sem("ones"), 1)
            pool.wait_ge(sem("setup_in"), 16 * SETUP)
            pool.wait_ge(sem("n0_out"), QUARTERS)
            nc.gpsimd.tensor_tensor(x[:], x[:], rows[:, 1:2, :].broadcast_to([P, TILES, D]), ALU.add).then_inc(
                sem("x_beta"), 1)

            for rev in range(2):
                with pool.Fori(0, CHUNKS) as c:
                    u = c + CHUNKS * rev
                    for h in range(HALVES):
                        pool.wait_ge(sem("m_sp"), 2 * u + h + 1)
                        nc.gpsimd.tensor_tensor(dt[:, h], dt[:, h], hs[:, h], ALU.add).then_inc(sem("m_dt"), 1)
                        pool.wait_ge(sem("m_dt"), 2 * u + h + 1)
                        nc.gpsimd.tensor_tensor(du[:, h], dt[:, h], xc[:, h], ALU.mult).then_inc(sem("m_du"), 1)
                    for k in range(STEPS):
                        s = STEPS * u + k
                        pool.wait_ge(sem("m_scan"), s + 3)
                        pool.wait_ge(sem("m_ccopy"), s + 2)
                        pool.wait_ge(sem("m_ysum"), s + 1)
                        nc.gpsimd.tensor_tensor(hC[:, k % 2], hs[:, k % 2], Cs[:, k % 2], ALU.mult).then_inc(
                            sem("m_hc"), 1)

            for f in range(2):
                if f == 0:
                    pool.wait_ge(sem("slots_zeroed"), 16)
                pool.wait_ge(sem(f"e{f}_index"), 1)
                for j in range(TILES):
                    nc.gpsimd.indirect_dma_start(
                        out=dispatched, out_offset=bass.IndirectOffsetOnAxis(ap=put_at[:, j:j + 1], axis=0),
                        in_=tokn[:, j, :], in_offset=None).then_inc(sem(f"e{f}_put"), 16)
                pool.wait_ge(sem(f"e{f}_stored"), 16 * EXPERTS)
                pool.wait_ge(sem(f"e{f}_put"), 16 * TILES)
                for j in range(TILES):
                    nc.gpsimd.indirect_dma_start(
                        out=tokn[:, j, :], out_offset=None, in_=expert_rows,
                        in_offset=bass.IndirectOffsetOnAxis(ap=get_at[:, j:j + 1], axis=0)).then_inc(
                        sem(f"e{f}_got{j // TQ}"), 16)
                if f == 0:
                    for g in range(GROUPS):
                        pool.wait_ge(sem("b_y"), g + 1)
                        pool.wait_ge(sem("b_sig"), 1)
                        sl = slice(512 * g, 512 * g + 512)
                        nc.gpsimd.tensor_tensor(kvS[:, sl], kvS[:, sl], rS[:, sl], ALU.mult).then_inc(
                            sem("b_sy"), 1)
                    for g in range(GROUPS):
                        pool.wait_ge(sem("b_relu"), 2 * g + 2)
                        nc.gpsimd.tensor_tensor(k2[:, g % 2, 0:2], k2[:, g % 2, 0:2], k2[:, g % 2, 0:2],
                                                ALU.mult).then_inc(sem("b_sqp"), 1)

        @block.scalar
        def _(act):
            act.wait_ge(sem("eps"), 1)
            act_norm(act, "n0")
            act.wait_ge(sem("setup_in"), 16 * SETUP)
            act.wait_ge(sem("pads_zero"), 1)
            act_turn(act, "t0", 1.0, 0.0)
            flat_a = acols[:].rearrange("p r h n -> p (r h n)")
            nc.scalar.activation(flat_a, flat_a, ACT.Exp).then_inc(sem("a_exp"), 1)
            act.wait_ge(sem("a_neg"), 1)

            for rev in range(2):
                d = "fb"[rev]
                on = slice(0, T - 1) if rev else slice(1, T)
                with act.Fori(0, CHUNKS) as c:
                    u = c + CHUNKS * rev
                    for i, (src, dst, bias) in enumerate((
                            (X[0], xc[:, 0], col(f"conv_b_{d}0")), (X[1], xc[:, 1], col(f"conv_b_{d}1")),
                            (CS, sz[:, 0], 0.0), (Y, sz[:, 1], 0.0))):
                        act.wait_ge(sem("m_proj"), 4 * u + i + 1)
                        nc.scalar.activation(dst, flat(src), ACT.Silu, bias=bias).then_inc(sem("m_silu"), 1)
                    act.wait_ge(sem("m_xp"), 2 * u + 1)
                    nc.scalar.activation(parts[:], flat(X[0])[0:96], ACT.Copy).then_inc(sem("m_parts"), 1)
                    act.wait_ge(sem("m_xp"), 2 * u + 2)
                    nc.scalar.activation(dtr[:], flat(X[1])[0:RANK], ACT.Copy).then_inc(sem("m_dtr"), 1)
                    act.wait_ge(sem("m_hc"), STEPS * u + 2)
                    for h, src in enumerate((CS, Y)):
                        b = col(f"dt_b_{d}{h}")
                        act.wait_ge(sem("m_dtp"), 2 * u + h + 1)
                        nc.scalar.activation(hs[:, h], flat(src), ACT.Abs, bias=b).then_inc(sem("m_spc"), 1)
                        act.wait_ge(sem("m_spc"), 2 * (2 * u + h) + 1)
                        nc.scalar.activation(hs[:, h], hs[:, h], ACT.Exp, scale=-1.0).then_inc(sem("m_spc"), 1)
                        act.wait_ge(sem("m_spc"), 2 * (2 * u + h) + 2)
                        nc.scalar.activation(hs[:, h], hs[:, h], ACT.Ln, bias=1.0)
                        nc.scalar.activation(dt[:, h], flat(src), ACT.Relu, bias=b).then_inc(sem("m_sp"), 1)
                    for k in range(STEPS):
                        h, n = divmod(k, STATE)
                        s = STEPS * u + k
                        act.wait_ge(sem("m_c"), s + 1)
                        act.wait_ge(sem("m_hc"), s + 1)
                        nc.scalar.activation(Cs[:, k % 2], flat(CS), ACT.Copy).then_inc(sem("m_ccopy"), 1)
                        if n == 0:
                            act.wait_ge(sem("m_dt"), 2 * u + h + 1)
                        act.wait_ge(sem("m_scan"), s + 1)
                        if rev and k < 2:
                            act.wait_ge(sem("m_reset"), 1)
                        nc.scalar.activation(dA[:, k % 2].rearrange("p (b t) -> p b t", b=CB)[:, :, on],
                                             dt[:, h].rearrange("p (b t) -> p b t", b=CB)[:, :, on], ACT.Exp,
                                             scale=acols[:, rev, h, n:n + 1]).then_inc(sem("m_dA"), 1)
                    if rev == 0:
                        act.wait_ge(sem("m_out"), u + 1)
                        nc.scalar.activation(yo[:, bass.ds(c * TQ, TQ), :].rearrange("p t d -> p (t d)"), flat(Y),
                                             ACT.Copy).then_inc(sem("m_evac"), 1)

            act_norm(act, "n1")
            act_experts(act, 0)

            act_norm(act, "n2")
            act_norm(act, "n3")
            act_turn(act, "t3", col("ln1_g"), col("ln1_b"))
            nc.scalar.activation(small[:, 2:3], col("decay"), ACT.Exp).then_inc(sem("b_ed"), 1)
            act.wait_ge(sem("b_ed"), 1)
            nc.scalar.activation(small[:, 3:4], small[:, 2:3], ACT.Exp, scale=-1.0)
            nc.scalar.activation(small[:, 4:5], col("first"), ACT.Exp).then_inc(sem("b_ed"), 1)
            for g in range(GROUPS):
                act.wait_ge(sem("t3_out"), g + 1)
                nc.scalar.activation(xm[:, 512 * g:512 * g + 512].rearrange("p (b t) -> p b t", b=2),
                                     xT[:, 2 * g:2 * g + 2, PAD:PAD + T], ACT.Copy,
                                     scale=col("att_tm")).then_inc(sem("b_xm0"), 1)
            for g in range(GROUPS):
                sl = slice(512 * g, 512 * g + 512)
                act.wait_ge(sem("b_r"), g + 1)
                nc.scalar.activation(rS[:, sl], PS[:, 4 + g % 2, :], ACT.Copy).then_inc(sem("b_rcopy"), 1)
                act.wait_ge(sem("b_min"), g + 1)
                nc.scalar.activation(kS[:, sl], kS[:, sl], ACT.Exp).then_inc(sem("b_exp"), 1)
            act.wait_ge(sem("b_rcopy"), GROUPS)
            nc.scalar.activation(rS, rS, ACT.Sigmoid).then_inc(sem("b_sig"), 1)
            for g in range(GROUPS):
                act.wait_ge(sem("b_att"), g + 1)
                nc.scalar.activation(r[:, TG * g:TG * g + TG, :].rearrange("p t d -> p (t d)"), PS[:, g % 2, :],
                                     ACT.Copy).then_inc(sem("b_x2"), 1)
            act_norm(act, "n4")
            act_turn(act, "t4", col("ln2_g"), col("ln2_b"))
            for g in range(GROUPS):
                act.wait_ge(sem("t4_out"), g + 1)
                nc.scalar.activation(xm[:, 512 * g:512 * g + 512].rearrange("p (b t) -> p b t", b=2),
                                     xT[:, 2 * g:2 * g + 2, PAD:PAD + T], ACT.Copy,
                                     scale=col("ffn_tm")).then_inc(sem("c_xm0"), 1)
            for g in range(GROUPS):
                for i in range(2):
                    act.wait_ge(sem("b_fk"), 2 * g + i + 1)
                    if g >= 2:
                        act.wait_ge(sem("b_fv"), g - 1)
                    nc.scalar.activation(k2[:, g % 2, 2 * i:2 * i + 2].rearrange("p i t -> p (i t)"),
                                         flat(PS[:, 2 * i:2 * i + 2, :]), ACT.Relu).then_inc(sem("b_relu"), 1)
                act.wait_ge(sem("b_fv"), g + 1)
                if g >= 2:
                    act.wait_ge(sem("b_x3"), g - 1)
                nc.scalar.activation(sg[:, g % 2, :], PS[:, 5, :], ACT.Sigmoid).then_inc(sem("b_gate"), 1)
            act_experts(act, 1)

        @block.tensor
        def _(pe):
            pe.wait_ge(sem("setup_in"), 16 * SETUP)
            pe_turn(pe, "t0", r, "n0_out")
            pe.wait_ge(sem("t0_out"), GROUPS)
            pe.wait_ge(sem("m_weights"), 1)
            mm = nc.tensor.matmul
            for rev in range(2):
                with pe.Fori(0, CHUNKS) as c:
                    u = c + CHUNKS * rev
                    pe.wait_ge(sem("m_scan"), STEPS * u + 2)
                    for h in range(HALVES):
                        for q in range(2):
                            for k in range(TAPS):
                                off = 2 * PAD - k if rev else k
                                last = mm(X[h][:, q, :].rearrange("p (b t) -> p b t", b=2),
                                          fold(rev, k)[:, P * h:P * h + P],
                                          xT[:, bass.ds(c * CB + 2 * q, 2), off:off + T],
                                          start=(k == 0), stop=(k == TAPS - 1))
                        last.then_inc(sem("m_proj"), 1)
                    for h, dst in enumerate((CS, Y)):
                        if h == 0:
                            pe.wait_ge(sem("m_ccopy"), STEPS * u + 1)
                        else:
                            pe.wait_ge(sem("m_evac"), u + 1)
                        for q in range(2):
                            last = mm(dst[:, q, :].rearrange("p (b t) -> p b t", b=2),
                                      inproj[:, rev, INNER + P * h:INNER + P * h + P],
                                      xT[:, bass.ds(c * CB + 2 * q, 2), PAD:PAD + T], start=True, stop=True)
                        last.then_inc(sem("m_proj"), 1)
                    pe.wait_ge(sem("m_silu"), 4 * u + 2)
                    for dst, lo, n in ((X[0], 0, 96), (X[1], 96, RANK)):
                        for q in range(2):
                            for h in range(HALVES):
                                last = mm(dst[0:n, q, :], xproj[:, rev, h, lo:lo + n],
                                          xc[:, h, 512 * q:512 * q + 512], start=(h == 0), stop=(h == 1))
                        last.then_inc(sem("m_xp"), 1)
                    pe.wait_ge(sem("m_dtr"), u + 1)
                    pe.wait_ge(sem("m_silu"), 4 * u + 4)
                    for h, dst in enumerate((CS, Y)):
                        for q in range(2):
                            last = mm(dst[:, q, :], dtproj[:, rev, P * h:P * h + P], dtr[:, 512 * q:512 * q + 512],
                                      start=True, stop=True)
                        last.then_inc(sem("m_dtp"), 1)

                    def spread(row, dst):
                        for q in range(2):
                            last = mm(dst[:, q, :], sel[:, row, :], parts[:, 512 * q:512 * q + 512],
                                      start=True, stop=True)
                        return last

                    def sum_states(k):
                        pe.wait_ge(sem("m_hc"), STEPS * u + k + 3)
                        for q in range(2):
                            last = mm(Y[:, q, :], ident[:], hC[:, k % 2, 512 * q:512 * q + 512], start=False,
                                      stop=(k % STATE == STATE - 1))
                        last.then_inc(sem("m_ysum"), 1)

                    pe.wait_ge(sem("m_split"), u + 1)
                    pe.wait_ge(sem("m_sp"), 2 * u + 2)
                    for h in range(HALVES):
                        if h == 1:
                            pe.wait_ge(sem("m_gated"), 2 * u + 1)
                        for q in range(2):
                            mm(Y[:, q, :], diagD[:, rev, h, :], xc[:, h, 512 * q:512 * q + 512],
                               start=True, stop=False)
                        for n in range(STATE):
                            k = STATE * h + n
                            s = STEPS * u + k
                            pe.wait_ge(sem("m_scan"), s + 1)
                            spread(n, X[k % 2]).then_inc(sem("m_b"), 1)
                            pe.wait_ge(sem("m_ccopy"), s + 1)
                            spread(STATE + n, CS).then_inc(sem("m_c"), 1)
                            if n >= 2:
                                sum_states(k - 2)
                        sum_states(STATE * h + STATE - 2)
                        sum_states(STATE * h + STATE - 1)
                    pe.wait_ge(sem("m_gated"), 2 * u + 2)
                    for i in range(TQ):
                        for h in range(HALVES):
                            last = mm(flat(Y)[:, D * i:D * i + D], du[:, h, P * i:P * i + P],
                                      outproj[:, rev, h, :], start=(h == 0), stop=(h == 1))
                    last.then_inc(sem("m_out"), 1)

            pe_experts(pe, 0)

            pe.wait_ge(sem("wb_in"), 16 * 3)
            pe_turn(pe, "t3", tokn, "n3_out")
            for g in range(GROUPS):
                rhs = xm[:, 512 * g:512 * g + 512]
                pe.wait_ge(sem("b_xm"), g + 1)
                if g == 0:
                    pe.wait_ge(sem("t3_out"), GROUPS)
                if g >= 2:
                    pe.wait_ge(sem("b_kv"), g - 1)
                    pe.wait_ge(sem("b_rcopy"), g - 1)
                for w, name in enumerate(("b_k", "b_v", "b_r")):
                    mm(PS[:, 2 * w + g % 2, :], wsq[:, w, :], rhs, start=True, stop=True).then_inc(sem(name), 1)
            pe.wait_ge(sem("b_kv"), GROUPS)
            for g in range(GROUPS):
                pe.wait_ge(sem("b_sy"), g + 1)
                if g >= 2:
                    pe.wait_ge(sem("b_x2"), g - 1)
                for i in range(TG):
                    t0 = PAD + P * (i % 2)
                    dst = PS[:, g % 2, D * i:D * i + D]
                    mm(dst, xT[:, 2 * g + i // 2, t0:t0 + P], ident[:], start=True, stop=False)
                    last = mm(dst, kvS[:, 512 * g + P * i:512 * g + P * i + P], wsq[:, 3, :], start=False, stop=True)
                last.then_inc(sem("b_att"), 1)
            pe_turn(pe, "t4", tokn, "n4_out")
            for g in range(GROUPS):
                pe.wait_ge(sem("c_xm"), g + 1)
                if g == 0:
                    pe.wait_ge(sem("t4_out"), GROUPS)
                    pe.wait_ge(sem("b_rcopy"), GROUPS)
                for i in range(2):
                    if g >= 1:
                        pe.wait_ge(sem("b_relu"), 2 * g + i - 1)
                    for j in range(2):
                        last = mm(PS[:, 2 * i + j, :], fk[:, P * (2 * i + j):P * (2 * i + j) + P],
                                  xm[:, 512 * g:512 * g + 512], start=True, stop=True)
                    last.then_inc(sem("b_fk"), 1)
                pe.wait_ge(sem("b_sqp"), g + 1)
                pe.wait_ge(sem("b_sqv"), g + 1)
                if g >= 1:
                    pe.wait_ge(sem("b_x3"), g)
                    pe.wait_ge(sem("b_gate"), g)
                for i in range(TG):
                    t0 = PAD + P * (i % 2)
                    o = slice(D * i, D * i + D)
                    for j in range(FT):
                        mm(PS[:, 4, o], k2[:, g % 2, j, P * i:P * i + P], fv[:, j, :], start=(j == 0),
                           stop=(j == FT - 1))
                    mm(PS[:, 5, o], xm[:, 512 * g + P * i:512 * g + P * i + P], wsq[:, 4, :], start=True, stop=True)
                    last = mm(PS[:, 6, o], xT[:, 2 * g + i // 2, t0:t0 + P], ident[:], start=True, stop=True)
                last.then_inc(sem("b_fv"), 1)
            pe_experts(pe, 1)

        @block.vector
        def _(dve):
            chain = [0]

            def link(ins):
                chain[0] += 1
                ins.then_inc(sem("dve_chain"), 1)
                dve.wait_ge(sem("dve_chain"), chain[0])

            nc.vector.memset(ecol, EPS).then_inc(sem("eps"), 1)
            dA4 = dA.rearrange("p k (b t) -> p k b t", b=CB)
            nc.vector.memset(dA4[:, 0, :, 0:1], 0.0).then_inc(sem("m_scan"), 1)
            nc.vector.memset(dA4[:, 1, :, 0:1], 0.0).then_inc(sem("m_scan"), 1)
            nc.vector.memset(Cs[:, 0, 0:1], 0.0).then_inc(sem("m_ccopy"), 1)
            nc.vector.memset(Cs[:, 1, 0:1], 0.0).then_inc(sem("m_evac"), 1)
            for q in range(QUARTERS):
                dve.wait_ge(sem(f"x_in{q}"), 16)
            dve.wait_ge(sem("slots_zeroed"), 16)
            dve_norm_stats(dve, link, "n0", x)
            dve_norm_apply(dve, link, "n0", x, r)
            dve.wait_ge(sem("setup_in"), 16 * SETUP)
            for rev in range(2):
                w1 = inproj[:, rev, 0:INNER].rearrange("p (k n) -> p k n", k=1).broadcast_to([P, TAPS, INNER])
                nc.vector.tensor_tensor(convw[:, rev], convw[:, rev], w1, ALU.mult)
                for h in range(HALVES):
                    last = nc.vector.tensor_scalar(diagD[:, rev, h, :], ident[:], col(f"D_{'fb'[rev]}{h}"), None,
                                                   ALU.mult)
            last.then_inc(sem("m_weights"), 1)
            dve.wait_ge(sem("a_exp"), 1)
            flat_a = acols[:].rearrange("p r h n -> p (r h n)")
            nc.vector.tensor_scalar(flat_a, flat_a, -1.0, None, ALU.mult).then_inc(sem("a_neg"), 1)

            for rev in range(2):
                way = slice(None, None, -1) if rev else slice(None)
                if rev:
                    dve.wait_ge(sem("m_scan"), STEPS * CHUNKS + 2)
                    nc.vector.memset(dA4[:, 0, :, T - 1:T], 0.0)
                    nc.vector.memset(dA4[:, 1, :, T - 1:T], 0.0).then_inc(sem("m_reset"), 1)
                with dve.Fori(0, CHUNKS) as c:
                    u = c + CHUNKS * rev
                    x0 = flat(X[0])
                    dve.wait_ge(sem("m_parts"), u + 1)
                    nc.vector.tensor_tensor(resid[0:96], x0[0:96], parts[0:96], ALU.subtract).then_inc(
                        sem("m_res"), 1)
                    dve.wait_ge(sem("m_res"), 3 * u + 1)
                    nc.vector.tensor_copy(parts[32:64], resid[32:64])
                    nc.vector.tensor_copy(parts[64:96], resid[64:96]).then_inc(sem("m_res"), 1)
                    dve.wait_ge(sem("m_res"), 3 * u + 2)
                    nc.vector.tensor_tensor(resid[64:96], resid[64:96], parts[64:96], ALU.subtract).then_inc(
                        sem("m_res"), 1)
                    dve.wait_ge(sem("m_res"), 3 * u + 3)
                    nc.vector.tensor_copy(parts[64:96], resid[64:96]).then_inc(sem("m_split"), 1)
                    for h in range(HALVES):
                        for n in range(STATE):
                            k = STATE * h + n
                            if k < 2:
                                dve.wait_ge(sem("m_du"), 2 * u + k + 1)
                            s = STEPS * u + k
                            xk = flat(X[k % 2])
                            dve.wait_ge(sem("m_b"), s + 1)
                            nc.vector.tensor_tensor(xk, du[:, h], xk, ALU.mult).then_inc(sem("m_dbu"), 1)
                            dve.wait_ge(sem("m_dbu"), s + 1)
                            dve.wait_ge(sem("m_dA"), s + 1)
                            dve.wait_ge(sem("m_hc"), s + 1)
                            nc.vector.tensor_tensor_scan(hs[:, k % 2, way], dA[:, k % 2, way], xk[:, way], 0.0,
                                                         ALU.mult, ALU.add).then_inc(sem("m_scan"), 1)
                        dve.wait_ge(sem("m_ysum"), STEPS * u + STATE * h + STATE + 2)
                        dve.wait_ge(sem("m_silu"), 4 * u + 3 + h)
                        nc.vector.tensor_tensor(du[:, h], flat(Y), sz[:, h], ALU.mult).then_inc(sem("m_gated"), 1)
                    if rev:
                        dve.wait_ge(sem("m_out"), u + 1)
                        yc = yo[:, bass.ds(c * TQ, TQ), :].rearrange("p t d -> p (t d)")
                        nc.vector.tensor_tensor(yc, yc, flat(Y), ALU.add).then_inc(sem("m_evac"), 1)

            dve.wait_ge(sem("m_evac"), 2 * CHUNKS + 1)
            dve.wait_ge(sem("x_beta"), 1)
            dve_norm_stats(dve, link, "n1", yo)
            for q in range(QUARTERS):
                dve.wait_ge(sem("n1_sd"), q + 1)
                tiles = range(TQ * q, TQ * q + TQ)
                nc.vector.reciprocal(rstd[:, TQ * q:TQ * q + TQ], sd[:, TQ * q:TQ * q + TQ])
                for j in tiles:
                    last = nc.vector.scalar_tensor_tensor(out=yo[:, j, :], in0=yo[:, j, :], scalar=mv[:, j, 0:1],
                                                          in1=rows[:, 0, :], op0=ALU.subtract, op1=ALU.mult)
                link(last)
                for j in tiles:
                    last = nc.vector.scalar_tensor_tensor(out=x[:, j, :], in0=yo[:, j, :], scalar=rstd[:, j:j + 1],
                                                          in1=x[:, j, :], op0=ALU.mult, op1=ALU.add)
            link(last)
            dve_experts(dve, link, 0)

            dve_norm_stats(dve, link, "n2", x, ready=("e0_x", lambda q: q + 1))
            dve_norm_apply(dve, link, "n2", x, r)
            dve_norm_stats(dve, link, "n3", r)
            dve_norm_apply(dve, link, "n3", r, tokn)
            mix = small[:, 5:9]
            for i, (tm, cm) in enumerate((("att_tm", "att_cm"), ("ffn_tm", "ffn_cm"))):
                link(nc.vector.tensor_scalar(mix[:, 2 * i:2 * i + 1], col(tm), -1.0, 1.0, ALU.mult, ALU.add))
                link(nc.vector.scalar_tensor_tensor(out=mix[:, 2 * i:2 * i + 1], in0=col(cm), scalar=col("lo_mask"),
                                                    in1=mix[:, 2 * i:2 * i + 1], op0=ALU.mult, op1=ALU.add))
                link(nc.vector.tensor_scalar(mix[:, 2 * i + 1:2 * i + 2], col(cm), col("hi_mask"), None, ALU.mult))
            dve_mix(dve, link, "b", mix[:, 0:1], mix[:, 1:2])
            dve.wait_ge(sem("b_ed"), 2)
            link(nc.vector.memset(edT, 0.0))
            link(nc.vector.tensor_scalar(edT[:, :, 1:T], edT[:, :, 1:T], small[:, 3:4], None, ALU.add))
            for g in range(GROUPS):
                sl = slice(512 * g, 512 * g + 512)
                dve.wait_ge(sem("b_k"), g + 1)
                nc.vector.tensor_scalar(kS[:, sl], PS[:, g % 2, :], CLAMP, None, ALU.min).then_inc(sem("b_min"), 1)
                dve.wait_ge(sem("b_exp"), g + 1)
                dve.wait_ge(sem("b_v"), g + 1)
                nc.vector.tensor_tensor(kvS[:, sl], PS[:, 2 + g % 2, :], kS[:, sl], ALU.mult).then_inc(
                    sem("b_kv"), 1)
            dve.wait_ge(sem("b_kv"), GROUPS)
            dve.wait_ge(sem("t3_in"), GROUPS)
            a3, b3 = (v[:].rearrange("p t d -> p (t d)") for v in (a_s, b_s))
            ed = edT.rearrange("p b t -> p (b t)")
            for m in range(CHUNKS):
                sl = slice(CT * m, CT * m + CT)
                nc.vector.tensor_tensor_scan(a3[:, sl], ed, kvS[:, sl], 0.0, ALU.mult, ALU.add)
                last = nc.vector.tensor_tensor_scan(b3[:, sl], ed, kS[:, sl], 0.0, ALU.mult, ALU.add)
            link(last)

            def seqs(ap):
                return ap.rearrange("p (b t) -> p b t", b=BATCH)

            for cur, prev in ((kvS, a3), (kS, b3)):
                nc.vector.tensor_scalar(seqs(cur)[:, :, 0:1], seqs(cur)[:, :, 0:1], small[:, 4:5], None, ALU.mult)
                last = nc.vector.scalar_tensor_tensor(
                    out=seqs(cur)[:, :, 1:T], in0=seqs(cur)[:, :, 1:T], scalar=small[:, 4:5],
                    in1=seqs(prev)[:, :, 0:T - 1], op0=ALU.mult, op1=ALU.add)
            link(last)
            for g in range(GROUPS):
                sl = slice(512 * g, 512 * g + 512)
                link(nc.vector.reciprocal(kS[:, sl], kS[:, sl]))
                nc.vector.tensor_tensor(kvS[:, sl], kvS[:, sl], kS[:, sl], ALU.mult).then_inc(sem("b_y"), 1)
            dve_norm_stats(dve, link, "n4", r, ready=("b_x2", lambda q: 2 * q + 2))
            dve_norm_apply(dve, link, "n4", r, tokn)
            dve_mix(dve, link, "c", mix[:, 2:3], mix[:, 3:4])
            for g in range(GROUPS):
                dve.wait_ge(sem("b_relu"), 2 * g + 2)
                nc.vector.tensor_tensor(k2[:, g % 2, 2:4], k2[:, g % 2, 2:4], k2[:, g % 2, 2:4],
                                        ALU.mult).then_inc(sem("b_sqv"), 1)
                dve.wait_ge(sem("b_gate"), g + 1)
                xg = x[:, TG * g:TG * g + TG, :].rearrange("p t d -> p (t d)")
                link(nc.vector.tensor_tensor(sg[:, g % 2, :], sg[:, g % 2, :], PS[:, 4, :], ALU.mult))
                link(nc.vector.tensor_tensor(xg, xg, sg[:, g % 2, :], ALU.add))
                nc.vector.tensor_tensor(xg, xg, PS[:, 6, :], ALU.add).then_inc(sem("b_x3"), 1)
            dve.wait_ge(sem("b_x3"), GROUPS)
            dve_experts(dve, link, 1)

def kernel(**inputs):
    import numpy as np
    import ml_dtypes
    import concourse.bacc as bacc
    from concourse.bass_utils import run_bass_kernel_spmd

    A, B, F = "L0_attn_a_", "L0_attn_b_", "L0_ffn_"
    w = {k: np.asarray(v) for k, v in inputs.items()}
    dirs = ("fwd_", "bwd_")

    def halves(name):
        return [w[A + d + name][P * h:P * h + P] for d in dirs for h in range(HALVES)]

    lo = (np.arange(P) < P // 2).astype(np.float32)
    cols = np.stack(halves("conv_b") + halves("dt_proj_b") + halves("D") + [
        w[F + "ln_gamma"], w[F + "ln_beta"], w[B + "ln1_g"], w[B + "ln1_b"], w[B + "ln2_g"], w[B + "ln2_b"],
        w[B + "att_time_mix"].reshape(P), w[B + "att_combined_mix"].reshape(P),
        w[B + "ffn_time_mix"].reshape(P), w[B + "ffn_combined_mix"].reshape(P),
        w[B + "time_decay"], w[B + "time_first"], lo, np.float32(1) - lo], axis=1)

    def xproj(d):
        v = w[A + d + "x_proj_w"]
        return np.concatenate([v[RANK:]] * 3 + [v[:RANK]], axis=0).T.reshape(HALVES, P, 104).transpose(1, 0, 2)

    sel = np.zeros((96, 2 * STATE, P), ml_dtypes.bfloat16)
    for k in range(96):
        sel[k, k % 32] = 1
    tri = np.ones((P, 2, P), ml_dtypes.bfloat16)
    tri[:, 0] = np.triu(np.ones((P, P)), 1)
    tok = np.arange(P)[:, None] + P * np.arange(TILES)[None]
    route = np.concatenate([np.tile(np.arange(EXPERTS, 0, -1), (P, 1)), np.zeros((P, 1)), SLOTS + tok],
                           axis=1).astype(np.float32)
    arrays = {
        "x_in": w[A + "x"].reshape(NTOK, D),
        "cols_in": cols,
        "alog_in": np.stack([w[A + d + "A_log"].reshape(HALVES, P, STATE).transpose(1, 0, 2) for d in dirs], axis=1),
        "rows_in": np.stack([w[A + "ln_gamma"], w[A + "ln_beta"]]),
        "conv_in": np.stack([w[A + d + "conv_w"].T for d in dirs]),
        "inproj_in": np.stack([w[A + d + "in_proj_w"].T for d in dirs], axis=1),
        "xproj_in": np.stack([xproj(d) for d in dirs], axis=1),
        "dtproj_in": np.stack([w[A + d + "dt_proj_w"].T for d in dirs], axis=1),
        "outproj_in": np.stack([w[A + d + "out_proj_w"].T.reshape(HALVES, P, D).transpose(1, 0, 2) for d in dirs],
                               axis=1),
        "wsq_in": np.stack([w[B + n].T for n in ("Wk", "Wv", "Wr", "Wo", "Fr")], axis=1),
        "fk_in": w[B + "Fk"].T,
        "fv_in": w[B + "Fv"].T.reshape(FT, P, D).transpose(1, 0, 2),
        "gate_in": w[F + "gate_weight"].T,
        "wi_in": w[F + "wi"].transpose(1, 0, 2),
        "wo_in": w[F + "wo"].reshape(EXPERTS, FT, P, D).transpose(2, 0, 1, 3),
        "ident_in": np.eye(P, dtype=np.float32),
        "sel_in": sel,
        "tri_in": tri,
        "route_in": route,
    }
    arrays = {k: np.ascontiguousarray(v) for k, v in arrays.items()}
    nc = bacc.Bacc("TRN2", target_bir_lowering=False, num_devices=1)
    args = [nc.dram_tensor(k, v.shape, mybir.dt.from_np(v.dtype), kind="ExternalInput").ap()
            for k, v in arrays.items()]
    args.append(nc.dram_tensor("out", (BATCH, T, D), F32, kind="ExternalOutput").ap())
    layer(nc, *args)
    return run_bass_kernel_spmd(nc, [arrays], core_ids=[0]).results[0]["out"]
```

```python
from contextlib import ExitStack

import concourse.bass as bass
from concourse import mybir

F32 = mybir.dt.float32
BF16 = mybir.dt.bfloat16
I32 = mybir.dt.int32
ALU = mybir.AluOpType
ACT = mybir.ActivationFunctionType
AX = mybir.AxisListType

P = 128
BATCH, T, D = 16, 256, 128
NTOK = BATCH * T
TILES = NTOK // P
GROUPS = 8
TG = TILES // GROUPS
QUARTERS = 4
TQ = TILES // QUARTERS
PAD = 3
TP = T + 2 * PAD

INNER, STATE, TAPS, RANK = 256, 16, 4, 8
HALVES = INNER // P
CB = 4
CT = CB * T
CHUNKS = BATCH // CB
STEPS = HALVES * STATE
LAG = 3
BC = 3 * 2 * STATE
UNITS = 2 * CHUNKS

SCHEDULE = [(("dt", 1, 0), [0]), (("dt", 1, 1), [1]), (("back", 0, 0), [2]), (("back", 0, 1), [3]),
            (("conv", 0, 0), [4, 5, 6, 6]), (("conv", 0, 1), [7, 8, 9, 9]),
            (("back", 1, 0), [10]), (("back", 1, 1), [11]), (("z", 0, 0), [12]),
            (("conv", 1, 0), [13, 14, 15, 15]), (("z", 0, 1), [16]), (("conv", 1, 1), [17, 18, 19, 19]),
            (("z", 1, 0), [20]), (("z", 1, 1), [21]), (("xp", 0), [23, 23]), (("xp", 1), [24, 24]),
            (("dt", 0, 0), [25]), (("dt", 0, 1), [26]), (("out", 0), [27, 28]), (("out", 1), [29, 30])]

SILU_STEP = 22


def bank_tasks(u):
    def has(task):
        if task[:2] == ("dt", 1):
            return 0 <= u < UNITS
        return 0 < u if task[0] in ("back", "out") else u + 1 < UNITS

    return [(task, steps) for task, steps in SCHEDULE if has(task)]


def bank_count(u):
    return sum(len(bank_tasks(v)) for v in range(-1, u))


EXPERTS, CAP, FF = 8, 256, 512
FT = FF // P
SLOTS = EXPERTS * CAP
STILES = SLOTS // P
CLAMP = 60.0
EPS = 1e-5

COLS = ["conv_b_f0", "conv_b_f1", "conv_b_b0", "conv_b_b1", "dt_b_f0", "dt_b_f1", "dt_b_b0", "dt_b_b1",
        "D_f0", "D_f1", "D_b0", "D_b1", "ffn_g", "ffn_b", "ln1_g", "ln1_b", "ln2_g", "ln2_b",
        "att_tm", "att_cm", "ffn_tm", "ffn_cm", "decay", "first", "lo_mask", "hi_mask"]
COL = {n: i for i, n in enumerate(COLS)}


def layer(nc, x_in, cols_in, alog_in, rows_in, conv_in, inproj_in, xproj_in, dtproj_in, outproj_in, wsq_in,
          fk_in, fv_in, gate_in, wi_in, wo_in, ident_in, sel_in, tri_in, route_in, out):
    dispatched = nc.dram_tensor("dispatched", (SLOTS + NTOK, D), F32, kind="Internal").ap()
    expert_rows = nc.dram_tensor("expert_rows", (SLOTS, D), F32, kind="Internal").ap()

    with ExitStack() as ctx:
        def sb(name, shape, dt=F32):
            return ctx.enter_context(nc.sbuf_tensor(name, shape, dt))

        sems = {}

        def sem(name):
            if name not in sems:
                sems[name] = ctx.enter_context(nc.semaphore(name))
            return sems[name]

        x = sb("x", [P, TILES, D])
        r = sb("r", [P, TILES, D])
        tokn = sb("tokn", [P, TILES, D])
        xT = sb("xT", [P, BATCH, TP])
        work = sb("work", [P, 4 * NTOK])
        wi = sb("wi", [P, EXPERTS, FF])
        wo = sb("wo", [P, EXPERTS, FT, D])
        w_misc = sb("w_misc", [P, 5120])
        sel = sb("sel", [96, 2 * STATE, P], BF16)
        ident = sb("ident", [P, P])
        tri = sb("tri", [P, 2, P], BF16)
        route = sb("route", [P, EXPERTS + 1 + TILES])
        cols = sb("cols", [P, len(COLS)])
        rows = sb("rows", [P, 2, D])
        acols = sb("acols", [P, 2, HALVES, STATE])
        gateT = sb("gateT", [P, EXPERTS])
        small = sb("small", [P, 16])
        stats = sb("stats", [P, TILES, 6])
        mv = sb("mv", [P, TILES, 2])
        sd = sb("sd", [P, TILES])
        rstd = sb("rstd", [P, TILES])
        PS = ctx.enter_context(nc.psum_tensor("PS", [P, 8, 512], F32))

        ecol, negone = small[:, 0:1], small[:, 1:2]

        def col(name):
            return cols[:, COL[name]:COL[name] + 1]

        inproj = w_misc[:, 0:1024].rearrange("p (r n) -> p r n", r=2)
        convw = w_misc[:, 1024:3072].rearrange("p (r k n) -> p r k n", r=2, k=TAPS)
        xproj = w_misc[:, 3072:3488].rearrange("p (r h n) -> p r h n", r=2, h=HALVES)
        outproj = w_misc[:, 3488:4000].rearrange("p (r h n) -> p r h n", r=2, h=HALVES)
        dtproj = w_misc[BC:BC + RANK, 4000:4512].rearrange("p (r n) -> p r n", r=2)

        def two(k):
            return work[:, 4 * k * CT:4 * (k + 1) * CT].rearrange("p (c h t) -> p c h t", c=2, h=HALVES)

        xc, dt, du, sz = two(0), two(1), two(2), two(3)
        spare = [v[:].rearrange("p a b -> p (a b)") if len(v.shape) == 3 else v[:].rearrange("p a b c -> p (a b c)")
                 for v in (r, wi, wo)]
        hs = spare[0][:, 0:3 * CT].rearrange("p (k t) -> p k t", k=3)
        hC = spare[1][:, 0:3 * CT].rearrange("p (k t) -> p k t", k=3)
        parked = x[:].rearrange("p t d -> p (t d)")
        resid = parked[0:BC, 0:CT]
        raw = parked[0:BC + RANK, CT:2 * CT]
        dA = [spare[2][:, CT * i:CT * i + CT] for i in range(2)] + [parked[:, 2 * CT:3 * CT]]
        Cs = [spare[2][:, CT * i:CT * i + CT] for i in (2, 3)] + [parked[:, 3 * CT:4 * CT]]
        aux = [spare[0][:, 3 * CT:4 * CT], spare[1][:, 3 * CT:4 * CT]]
        yg = sb("yg", [P, HALVES, CT])
        parts = sb("parts", [BC, 2, CT], BF16)
        X = [PS[:, 0:2, :], PS[:, 2:4, :]]
        CB1 = PS[:, 4, :]
        G = PS[:, 5, :]
        Y = PS[:, 6:8, :]
        yo = tokn

        def flat(ap):
            return ap.rearrange("p a n -> p (a n)")

        eo = work[:, 0:2048].rearrange("p (s d) -> p s d", s=STILES)
        dispT = work[:, 2048:4096]
        rowsin = work[:, 4096:6144].rearrange("p (s d) -> p s d", s=STILES)
        hT = work[:, 6144:8192].rearrange("p (b i c) -> p b i c", b=2, i=FT)
        tokT = work[:, 8192:9216].rearrange("p (b t) -> p b t", b=2)
        rt = [work[:, 9216 + 256 * i:9472 + 256 * i].rearrange("p (t e) -> p t e", e=EXPERTS) for i in range(8)]
        rs = [work[:, 11264 + 32 * i:11296 + 32 * i] for i in range(12)]
        onehot = sb("onehot", [P, TILES, EXPERTS], BF16)
        put_at = sb("put_at", [P, TILES], I32)
        get_at = sb("get_at", [P, TILES], I32)
        weight = sb("weight", [P, TILES])
        ones = sb("ones", [P, TILES])

        xm = work[:, 0:NTOK]
        kS = work[:, NTOK:2 * NTOK]
        kvS = work[:, 2 * NTOK:3 * NTOK]
        rS = work[:, 3 * NTOK:4 * NTOK]
        wsq = w_misc[:, 0:640].rearrange("p (w n) -> p w n", w=5)
        fk = w_misc[:, 640:1152]
        fv = w_misc[:, 1152:1664].rearrange("p (i n) -> p i n", i=FT)
        edT = w_misc[:, 1664:1664 + CT].rearrange("p (b t) -> p b t", b=CB)
        a_s, b_s = r, tokn
        k2 = work[:, NTOK:2 * NTOK].rearrange("p (b i t) -> p b i t", b=2, i=FT)
        sg = work[:, 2 * NTOK:2 * NTOK + 1024].rearrange("p (b t) -> p b t", b=2)

        x_dram = x_in.rearrange("(q t p) d -> q p t d", q=QUARTERS, p=P)
        out_dram = out.rearrange("b t d -> (b t) d").rearrange("(q t p) d -> q p t d", q=QUARTERS, p=P)

        SETUP = 15

        block = ctx.enter_context(nc.Block())

        def sp_experts(sp, f):
            sp.wait_ge(sem(f"e{f}_put"), 16 * TILES)
            sp.dma_start(rowsin, dispatched[0:SLOTS, :].rearrange("(s p) d -> p s d", p=P)).then_inc(
                sem(f"e{f}_rows"), 16)
            for e in range(EXPERTS):
                sp.wait_ge(sem(f"e{f}_eo"), e + 1)
                sp.dma_start(expert_rows[CAP * e:CAP * e + CAP, :].rearrange("(s p) d -> p s d", p=P),
                             eo[:, 2 * e:2 * e + 2, :]).then_inc(sem(f"e{f}_stored"), 16)

        def act_experts(act, f):
            act_norm(act, f"e{f}a")
            act_norm(act, f"e{f}b")
            for g in range(GROUPS):
                act.wait_ge(sem(f"e{f}_turned"), g + 1)
                if g >= 2:
                    act.wait_ge(sem(f"e{f}_logit"), g - 1)
                nc.scalar.activation(tokT[:, g % 2, :], PS[:, g % 2, :], ACT.Identity, scale=col("ffn_g"),
                                     bias=col("ffn_b")).then_inc(sem(f"e{f}_tokT"), 1)
            act.wait_ge(sem(f"e{f}_sub"), 1)
            nc.scalar.activation(rt[1], rt[0], ACT.Exp).then_inc(sem(f"e{f}_prob"), 1)
            for g in range(STILES // TG):
                act.wait_ge(sem(f"e{f}_din"), g + 1)
                nc.scalar.activation(dispT[:, 512 * g:512 * g + 512], PS[:, g % 2, :], ACT.Identity,
                                     scale=col("ffn_g"), bias=col("ffn_b")).then_inc(sem(f"e{f}_dT"), 1)
            for e in range(EXPERTS):
                act.wait_ge(sem(f"e{f}_h"), e + 1)
                if e >= 2:
                    act.wait_ge(sem(f"e{f}_o"), e - 1)
                b = 4 + 2 * (e % 2)
                nc.scalar.activation(hT[:, e % 2].rearrange("p i c -> p (i c)"), flat(PS[:, b:b + 2, :]),
                                     ACT.Gelu).then_inc(sem(f"e{f}_gelu"), 1)

        def pe_experts(pe, f):
            mm = nc.tensor.matmul
            L = PS[:, 2, 0:TILES * EXPERTS].rearrange("p (t e) -> p t e", e=EXPERTS)

            def logits(g):
                pe.wait_ge(sem(f"e{f}_tokT"), g + 1)
                for i in range(TG):
                    last = mm(L[:, TG * g + i, :], tokT[:, g % 2, P * i:P * i + P], gateT[:], start=True, stop=True)
                last.then_inc(sem(f"e{f}_logit"), 1)

            for g in range(GROUPS):
                if g % 2 == 0:
                    pe.wait_ge(sem(f"e{f}b_out"), g // 2 + 1)
                if g >= 2:
                    pe.wait_ge(sem(f"e{f}_tokT"), g - 1)
                for i in range(TG):
                    last = nc.tensor.transpose(PS[:, g % 2, D * i:D * i + D], tokn[:, TG * g + i, :], ident[:])
                last.then_inc(sem(f"e{f}_turned"), 1)
                if g >= 1:
                    logits(g - 1)
            logits(GROUPS - 1)
            pe.wait_ge(sem(f"e{f}_onehot"), 1)
            oh = onehot[:].rearrange("p t e -> p (t e)")
            mm(PS[:, 3, 0:256], tri[:, 0, :], oh, start=True, stop=True)
            mm(PS[:, 3, 256:512], tri[:, 1, :], oh, start=True, stop=True).then_inc(sem(f"e{f}_counts"), 1)
            pe.wait_ge(sem(f"e{f}_rows"), 16)
            for g in range(STILES // TG):
                if g >= 2:
                    pe.wait_ge(sem(f"e{f}_dT"), g - 1)
                for i in range(TG):
                    last = nc.tensor.transpose(PS[:, g % 2, D * i:D * i + D], rowsin[:, TG * g + i, :], ident[:])
                last.then_inc(sem(f"e{f}_din"), 1)

            def second(e):
                pe.wait_ge(sem(f"e{f}_gelu"), e + 1)
                if e == 0:
                    pe.wait_ge(sem("wo_in"), 16)
                    pe.wait_ge(sem(f"e{f}_index"), 1)
                if e >= 2:
                    pe.wait_ge(sem(f"e{f}_eo"), e - 1)
                for s in range(2):
                    for i in range(FT):
                        last = mm(PS[:, 2 + e % 2, D * s:D * s + D], hT[:, e % 2, i, P * s:P * s + P],
                                  wo[:, e, i, :], start=(i == 0), stop=(i == FT - 1))
                last.then_inc(sem(f"e{f}_o"), 1)

            pe.wait_ge(sem("wi_in"), 16)
            for e in range(EXPERTS):
                pe.wait_ge(sem(f"e{f}_dT"), e // 2 + 1)
                if e >= 2:
                    pe.wait_ge(sem(f"e{f}_gelu"), e - 1)
                for i in range(FT):
                    last = mm(PS[:, 4 + 2 * (e % 2) + i // 2, CAP * (i % 2):CAP * (i % 2) + CAP],
                              wi[:, e, P * i:P * i + P], dispT[:, CAP * e:CAP * e + CAP], start=True, stop=True)
                last.then_inc(sem(f"e{f}_h"), 1)
                if e >= 1:
                    second(e - 1)
            second(EXPERTS - 1)

        def dve_mix(dve, link, name, prev_w, next_w):
            for g in range(GROUPS):
                xg = xm[:, 512 * g:512 * g + 512].rearrange("p (b t) -> p b t", b=2)
                dve.wait_ge(sem(f"{name}_xm0"), g + 1)
                link(nc.vector.scalar_tensor_tensor(out=xg, in0=xT[:, 2 * g:2 * g + 2, PAD - 1:PAD - 1 + T],
                                                    scalar=prev_w, in1=xg, op0=ALU.mult, op1=ALU.add))
                nc.vector.scalar_tensor_tensor(out=xg, in0=xT[:, 2 * g:2 * g + 2, PAD + 1:PAD + 1 + T],
                                               scalar=next_w, in1=xg, op0=ALU.mult, op1=ALU.add).then_inc(
                    sem(f"{name}_xm"), 1)

        def dve_experts(dve, link, f):
            dve_norm_stats(dve, link, f"e{f}a", x)
            dve_norm_apply(dve, link, f"e{f}a", x, r)
            dve_norm_stats(dve, link, f"e{f}b", r)
            dve_norm_apply(dve, link, f"e{f}b", r, tokn)
            L = PS[:, 2, 0:256].rearrange("p (t e) -> p t e", e=EXPERTS)
            pre = PS[:, 3, 0:256].rearrange("p (t e) -> p t e", e=EXPERTS)
            tot = PS[:, 3, 256:512].rearrange("p (t e) -> p t e", e=EXPERTS)
            mx, mx2, rank, keep, slot, den = rs[0:6]
            own = route[:, EXPERTS + 1:EXPERTS + 1 + TILES]

            def per_expert(v):
                return v.rearrange("p (t e) -> p t e", e=1).broadcast_to([P, TILES, EXPERTS])

            dve.wait_ge(sem(f"e{f}_logit"), GROUPS)
            link(nc.vector.tensor_reduce(mx, L, AX.X, ALU.max))
            nc.vector.tensor_tensor(rt[0], L, per_expert(mx), ALU.subtract).then_inc(sem(f"e{f}_sub"), 1)
            dve.wait_ge(sem(f"e{f}_sub"), 1)
            pri = route[:, 0:EXPERTS].rearrange("p (t e) -> p t e", t=1).broadcast_to([P, TILES, EXPERTS])
            link(nc.vector.scalar_tensor_tensor(out=rt[2], in0=rt[0], scalar=0.0, in1=pri, op0=ALU.is_ge,
                                                op1=ALU.mult))
            link(nc.vector.tensor_reduce(mx2, rt[2], AX.X, ALU.max))
            nc.vector.tensor_tensor(onehot[:], rt[2], per_expert(mx2), ALU.is_equal).then_inc(sem(f"e{f}_onehot"), 1)
            dve.wait_ge(sem(f"e{f}_onehot"), 1)
            dve.wait_ge(sem(f"e{f}_prob"), 1)
            link(nc.vector.tensor_reduce(den, rt[1], AX.X, ALU.add))
            nc.vector.reciprocal(weight[:], den)
            dve.wait_ge(sem("ones"), 1)
            dve.wait_ge(sem(f"e{f}_counts"), 1)
            nc.vector.memset(rt[4][:, 0:1, :], 0.0)
            link(nc.vector.tensor_copy(rt[3], tot))
            for e in range(EXPERTS):
                last = nc.vector.tensor_tensor_scan(rt[4][:, 1:TILES, e], ones[:, 1:TILES], rt[3][:, 0:TILES - 1, e],
                                                    0.0, ALU.mult, ALU.add)
            link(last)
            link(nc.vector.tensor_tensor(rt[5], rt[4], pre, ALU.add))
            link(nc.vector.tensor_tensor(rt[6], rt[5], onehot[:], ALU.mult))
            link(nc.vector.tensor_reduce(rank, rt[6], AX.X, ALU.add))
            link(nc.vector.tensor_scalar(keep, rank, float(CAP), None, ALU.is_lt))
            nc.vector.tensor_tensor(weight[:], weight[:], keep, ALU.mult)
            nc.vector.tensor_scalar(slot, mx2, -float(CAP), float(SLOTS), ALU.mult, ALU.add)
            link(nc.vector.tensor_tensor(rs[6], rank, keep, ALU.mult))
            link(nc.vector.tensor_tensor(slot, slot, rs[6], ALU.add))
            nc.vector.tensor_copy(get_at[:], slot)
            link(nc.vector.tensor_tensor(rs[7], slot, own, ALU.subtract))
            link(nc.vector.tensor_tensor(rs[8], rs[7], keep, ALU.mult))
            link(nc.vector.tensor_tensor(rs[9], rs[8], own, ALU.add))
            nc.vector.tensor_copy(put_at[:], rs[9]).then_inc(sem(f"e{f}_index"), 1)
            for e in range(EXPERTS):
                dve.wait_ge(sem(f"e{f}_o"), e + 1)
                nc.vector.tensor_copy(eo[:, 2 * e:2 * e + 2, :].rearrange("p s d -> p (s d)"),
                                      PS[:, 2 + e % 2, 0:2 * D]).then_inc(sem(f"e{f}_eo"), 1)
            link(nc.vector.tensor_tensor(x[:], x[:], r[:], ALU.add))
            for q in range(QUARTERS):
                dve.wait_ge(sem(f"e{f}_got{q}"), 16 * TQ)
                for j in range(TQ * q, TQ * q + TQ):
                    last = nc.vector.scalar_tensor_tensor(out=x[:, j, :], in0=tokn[:, j, :], scalar=weight[:, j:j + 1],
                                                          in1=x[:, j, :], op0=ALU.mult, op1=ALU.add)
                last.then_inc(sem(f"e{f}_x"), 1)

        def dve_norm_stats(dve, link, name, src, ready=None):
            for q in range(QUARTERS):
                if ready:
                    dve.wait_ge(sem(ready[0]), ready[1](q))
                for j in range(TQ * q, TQ * q + TQ):
                    last = nc.vector.bn_stats(stats[:, j, :], src[:, j, :])
                link(last)
                for j in range(TQ * q, TQ * q + TQ):
                    last = nc.vector.bn_aggr(mv[:, j, :], stats[:, j, :])
                last.then_inc(sem(f"{name}_var"), 1)

        def act_norm(act, name):
            for q in range(QUARTERS):
                act.wait_ge(sem(f"{name}_var"), q + 1)
                nc.scalar.activation(sd[:, TQ * q:TQ * q + TQ], mv[:, TQ * q:TQ * q + TQ, 1], ACT.Sqrt,
                                     bias=ecol).then_inc(sem(f"{name}_sd"), 1)

        def dve_norm_apply(dve, link, name, src, dst):
            for q in range(QUARTERS):
                dve.wait_ge(sem(f"{name}_sd"), q + 1)
                link(nc.vector.reciprocal(rstd[:, TQ * q:TQ * q + TQ], sd[:, TQ * q:TQ * q + TQ]))
                for j in range(TQ * q, TQ * q + TQ):
                    last = nc.vector.tensor_scalar(dst[:, j, :], src[:, j, :], mv[:, j, 0:1], rstd[:, j:j + 1],
                                                   ALU.subtract, ALU.mult)
                last.then_inc(sem(f"{name}_out"), 1)
            dve.wait_ge(sem(f"{name}_out"), QUARTERS)

        def pe_turn(pe, name, src, ready):
            for g in range(GROUPS):
                if g % 2 == 0:
                    pe.wait_ge(sem(ready), g // 2 + 1)
                if g >= 2:
                    pe.wait_ge(sem(f"{name}_out"), g - 1)
                for i in range(TG):
                    last = nc.tensor.transpose(PS[:, g % 2, D * i:D * i + D], src[:, TG * g + i, :], ident[:])
                last.then_inc(sem(f"{name}_in"), 1)

        def act_turn(act, name, scale, bias):
            for g in range(GROUPS):
                act.wait_ge(sem(f"{name}_in"), g + 1)
                nc.scalar.activation(xT[:, 2 * g:2 * g + 2, PAD:PAD + T],
                                     PS[:, g % 2, :].rearrange("p (b t) -> p b t", b=2), ACT.Identity,
                                     scale=scale, bias=bias).then_inc(sem(f"{name}_out"), 1)


        def task_number(u, task):
            return bank_count(u) + [t for t, _ in bank_tasks(u)].index(task)

        def block512(q):
            return slice(512 * q, 512 * q + 512)

        def pe_spread(u, row, q, dst):
            return nc.tensor.matmul(dst, sel[:, row, :], parts[:, u % 2, block512(q)], start=True, stop=True)

        def pe_input(pe, s):
            u, k = divmod(s, STEPS)
            if k == 0:
                pe.wait_ge(sem("m_split"), u + 1)
            if s >= 2:
                pe.wait_ge(sem("m_scan"), s - 1)
            for q in range(2):
                last = pe_spread(u, k % STATE, q, X[s % 2][:, q, :])
            last.then_inc(sem("m_b"), 1)

        def pe_c(pe, s, q):
            u, k = divmod(s, STEPS)
            if s + q > 0:
                pe.wait_ge(sem("m_ccopy"), 2 * s + q)
            pe_spread(u, STATE + k % STATE, q, CB1).then_inc(sem("m_c"), 1)

        def pe_sum(pe, s, q):
            u, k = divmod(s, STEPS)
            h, n = divmod(k, STATE)
            terms = [hC[:, s % 3]]
            if n == 0:
                if q == 0:
                    if 2 * u + h > 0:
                        pe.wait_ge(sem("m_yout"), 2 * u + h)
                    pe.wait_ge(sem("m_dx"), 2 * u + h + 1)
                terms = [aux[h], hC[:, s % 3]]
            for v, term in enumerate(terms):
                if v == len(terms) - 1 and q == 0:
                    pe.wait_ge(sem("m_hc"), s + 1)
                for i in range(4 * q, 4 * q + 4):
                    last = nc.tensor.matmul(flat(Y)[:, P * i:P * i + P], term[:, P * i:P * i + P], ident[:],
                                            start=(n == 0 and v == 0 and i % 4 == 0),
                                            stop=(n == STATE - 1 and i % 4 == 3), is_transpose=True)
            if q == 1:
                last.then_inc(sem("m_ysum"), 1)

        def act_c(act, s, q):
            act.wait_ge(sem("m_c"), 2 * s + q + 1)
            if s >= 3:
                act.wait_ge(sem("m_hc"), s - 2)
            nc.scalar.activation(Cs[s % 3][:, block512(q)], CB1, ACT.Copy).then_inc(sem("m_ccopy"), 1)

        def act_leave(act, u, h):
            act.wait_ge(sem("m_ysum"), STEPS * u + STATE * (h + 1))
            nc.scalar.activation(du[:, u % 2, h], flat(Y), ACT.Copy).then_inc(sem("m_yout"), 1)

        def pe_bank(pe, u, task, part):
            mm = nc.tensor.matmul
            number = task_number(u, task)
            if part == 0 and number > 0:
                pe.wait_ge(sem("m_gfree"), number)
            kind, q = task[0], task[-1]
            g2 = G.rearrange("p (b t) -> p b t", b=2)
            v = u + 1
            rev, c = divmod(v, CHUNKS)
            seqs = slice(CB * c + 2 * q, CB * c + 2 * q + 2)
            parts_of = 1
            if kind == "z":
                h = task[1]
                last = mm(g2, inproj[:, rev, INNER + P * h:INNER + P * h + P], xT[:, seqs, PAD:PAD + T],
                          start=True, stop=True)
            elif kind == "conv":
                h = task[1]
                parts_of = TAPS
                off = 2 * PAD - part if rev else part
                last = mm(g2, convw[:, rev, part, P * h:P * h + P], xT[:, seqs, off:off + T],
                          start=(part == 0), stop=(part == TAPS - 1))
            elif kind == "xp":
                parts_of = HALVES
                if part == 0:
                    pe.wait_ge(sem("m_silu"), v + 1)
                last = mm(G[0:BC + RANK], xproj[:, rev, part, :], xc[:, v % 2, part, block512(q)],
                          start=(part == 0), stop=(part == 1))
            elif kind == "dt":
                h = task[1]
                last = mm(G, dtproj[:, (v - h) // CHUNKS, P * h:P * h + P], raw[BC:BC + RANK, block512(q)],
                          start=True, stop=True)
            elif kind == "back":
                h = task[1]
                pe.wait_ge(sem("m_yout"), 2 * (u - 1) + h + 1)
                for i in range(4):
                    last = nc.tensor.transpose(G[:, P * i:P * i + P],
                                               du[:, (u - 1) % 2, h, P * (4 * q + i):P * (4 * q + i) + P], ident[:])
            else:
                parts_of = 2
                for i in (2 * part, 2 * part + 1):
                    for h in range(HALVES):
                        last = mm(G[:, D * i:D * i + D], yg[:, h, P * (4 * q + i):P * (4 * q + i) + P],
                                  outproj[:, (u - 1) // CHUNKS, h, :], start=(h == 0), stop=(h == 1))
            if part == parts_of - 1:
                last.then_inc(sem("m_g"), 1)

        def pe_parts(pe, u, step):
            for task, steps in bank_tasks(u):
                for part in range(len(steps)):
                    if steps[part] == step:
                        pe_bank(pe, u, task, part)

        def act_bank(act, u, task):
            number = task_number(u, task)
            kind, q = task[0], task[-1]
            v = u + 1 - (task[:2] == ("dt", 1))
            d = "fb"[min(v, UNITS - 1) // CHUNKS]
            b = block512(q)
            if kind == "back" or (kind == "out" and u > CHUNKS):
                return
            act.wait_ge(sem("m_g"), number + 1)
            if kind == "z":
                if v >= 2:
                    h = task[1]
                    act.wait_ge(sem("m_gfree"), task_number(u, ("back", h, 1)) + 1)
                nc.scalar.activation(sz[:, v % 2, task[1], b], G, ACT.Copy).then_inc(sem("m_gfree"), 1)
            elif kind == "conv":
                nc.scalar.activation(xc[:, v % 2, task[1], b], G, ACT.Identity,
                                     bias=col(f"conv_b_{d}{task[1]}")).then_inc(sem("m_gfree"), 1)
            elif kind == "xp":
                if v >= 1:
                    act.wait_ge(sem("m_split"), v)
                nc.scalar.activation(raw[:, b], G[0:BC + RANK], ACT.Copy).then_inc(sem("m_gfree"), 1)
            elif kind == "dt":
                h = task[1]
                bias = col(f"dt_b_{d}{h}")
                if v >= 1 and q == 0:
                    act.wait_ge(sem("m_ysum"), STEPS * (v - 1) + STATE * h + 1)
                nc.scalar.activation(aux[h][:, b], G, ACT.Abs, bias=bias)
                nc.scalar.activation(dt[:, v % 2, h, b], G, ACT.Relu, bias=bias).then_inc(sem("m_gfree"), 1)
            else:
                c = u - 1
                nc.scalar.activation(yo[:, TQ * c + 4 * q:TQ * c + 4 * q + 4, :].rearrange("p t d -> p (t d)"), G,
                                     ACT.Copy).then_inc(sem("m_gfree"), 1)

        def act_silu(act, v, t, done):
            act.wait_ge(sem("m_gfree"), task_number(v - 1, ("z", 1, 1)) + 1)
            t2 = t[:, v % 2].rearrange("p h t -> p (h t)")
            nc.scalar.activation(t2, t2, ACT.Silu).then_inc(sem(done), 1)

        def act_decay(act, s):
            u, k = divmod(s, STEPS)
            h, n = divmod(k, STATE)
            rev = u // CHUNKS
            on = slice(0, T - 1) if rev else slice(1, T)
            if n == 0:
                act.wait_ge(sem("m_dt"), 2 * u + h + 1)
            if s >= 3:
                act.wait_ge(sem("m_scan"), s - 2)
            if rev and s - STEPS * CHUNKS < 3:
                act.wait_ge(sem("m_reset"), 1)
            nc.scalar.activation(dA[s % 3].rearrange("p (b t) -> p b t", b=CB)[:, :, on],
                                 dt[:, u % 2, h].rearrange("p (b t) -> p b t", b=CB)[:, :, on], ACT.Exp,
                                 scale=acols[:, rev, h, n:n + 1]).then_inc(sem("m_dA"), 1)

        def act_dx(act, u, h):
            act.wait_ge(sem("m_dt"), 2 * u + h + 1)
            nc.scalar.activation(aux[h], xc[:, u % 2, h], ACT.Copy,
                                 scale=col(f"D_{'fb'[u // CHUNKS]}{h}")).then_inc(sem("m_dx"), 1)

        def act_softplus_exp(act, v, h):
            act.wait_ge(sem("m_gfree"), task_number(v - 1 + h, ("dt", h, 1)) + 1)
            nc.scalar.activation(aux[h], aux[h], ACT.Exp, scale=-1.0).then_inc(sem("m_spexp"), 1)

        def act_softplus_ln(act, v, h):
            act.wait_ge(sem("m_spexp"), 2 * v + h + 1)
            nc.scalar.activation(aux[h], aux[h], ACT.Ln, bias=1.0).then_inc(sem("m_sp"), 1)

        def dve_bank(dve, u, task):
            number = task_number(u, task)
            kind, q = task[0], task[-1]
            if kind == "back":
                h = task[1]
                w = u - 1
                dve.wait_ge(sem("m_g"), number + 1)
                dve.wait_ge(sem("m_gate"), w + 1)
                nc.vector.tensor_tensor(yg[:, h, block512(q)], G, sz[:, w % 2, h, block512(q)], ALU.mult).then_inc(
                    sem("m_gfree"), 1)
            elif kind == "out" and u > CHUNKS:
                c = u - 1 - CHUNKS
                dve.wait_ge(sem("m_g"), number + 1)
                yc = yo[:, TQ * c + 4 * q:TQ * c + 4 * q + 4, :].rearrange("p t d -> p (t d)")
                nc.vector.tensor_tensor(yc, yc, G, ALU.add).then_inc(sem("m_gfree"), 1)

        def pool_softplus(pool, v, h):
            pool.wait_ge(sem("m_sp"), 2 * v + h + 1)
            nc.gpsimd.tensor_tensor(dt[:, v % 2, h], dt[:, v % 2, h], aux[h], ALU.add).then_inc(sem("m_dt"), 1)
            pool.wait_ge(sem("m_dt"), 2 * v + h + 1)
            if v >= 2:
                pool.wait_ge(sem("m_g"), task_number(v - 1, ("back", h, 1)) + 1)
            nc.gpsimd.tensor_tensor(du[:, v % 2, h], dt[:, v % 2, h], xc[:, v % 2, h], ALU.mult).then_inc(
                sem("m_du"), 1)

        def dve_split(dve, v, i):
            if i == 0:
                dve.wait_ge(sem("m_gfree"), task_number(v - 1, ("xp", 1)) + 1)
            else:
                dve.wait_ge(sem("m_part"), 3 * v + i)
            p3 = parts[:, v % 2]
            if i == 0:
                nc.vector.tensor_copy(p3, raw[0:BC]).then_inc(sem("m_part"), 1)
            elif i == 1:
                nc.vector.tensor_tensor(resid, raw[0:BC], p3, ALU.subtract).then_inc(sem("m_part"), 1)
            elif i == 2:
                nc.vector.tensor_copy(p3[32:64], resid[32:64])
                nc.vector.tensor_copy(p3[64:96], resid[64:96]).then_inc(sem("m_part"), 1)
            else:
                nc.vector.tensor_tensor(p3[64:96], resid[64:96], p3[64:96], ALU.subtract).then_inc(sem("m_split"), 1)

        @block.sync
        def _(sp):
            for q in range(QUARTERS):
                sp.dma_start(x[:, TQ * q:TQ * q + TQ, :], x_dram[q]).then_inc(sem(f"x_in{q}"), 16)
            s = sem("setup_in")
            for dst, src in (
                (cols[:], cols_in), (acols[:], alog_in), (ident[:], ident_in), (sel[:], sel_in), (tri[:], tri_in),
                (route[:], route_in), (gateT[:], gate_in), (rows[:], rows_in.partition_broadcast(P)),
                (convw, conv_in.partition_broadcast(P)), (inproj, inproj_in),
                (xproj[:, 0], xproj_in[:, 0]), (xproj[:, 1], xproj_in[:, 1]),
                (outproj[:, 0], outproj_in[:, 0]), (outproj[:, 1], outproj_in[:, 1]), (dtproj, dtproj_in),
            ):
                sp.dma_start(dst, src).then_inc(s, 16)
            sp.wait_ge(sem("r_zero"), 1)
            sp.dma_start(dispatched[0:SLOTS, :].rearrange("(s p) d -> p s d", p=P), r[:, 0:STILES, :]).then_inc(
                sem("slots_zeroed"), 16)

            sp.wait_ge(sem("m_split"), UNITS)
            sp.wait_ge(sem("m_gfree"), task_number(UNITS - 1, ("dt", 1, 1)) + 1)
            for q in range(2):
                sp.dma_start(x[:, TQ * q:TQ * q + TQ, :], x_dram[q]).then_inc(sem(f"x_back{q}"), 16)
            sp.wait_ge(sem("m_ysum"), STEPS * UNITS)
            for q in (2, 3):
                sp.dma_start(x[:, TQ * q:TQ * q + TQ, :], x_dram[q]).then_inc(sem(f"x_back{q}"), 16)
            sp.dma_start(wi[:], wi_in).then_inc(sem("wi_in"), 16)
            sp.dma_start(wo[:], wo_in).then_inc(sem("wo_in"), 16)
            sp_experts(sp, 0)
            s = sem("wb_in")
            for dst, src in ((wsq, wsq_in), (fk, fk_in), (fv, fv_in)):
                sp.dma_start(dst, src).then_inc(s, 16)
            sp_experts(sp, 1)
            for q in range(QUARTERS):
                sp.wait_ge(sem("e1_x"), q + 1)
                sp.dma_start(out_dram[q], x[:, TQ * q:TQ * q + TQ, :]).then_inc(sem("stored"), 16)
            sp.wait_ge(sem("stored"), 16 * QUARTERS)

        @block.gpsimd
        def _(pool):
            nc.gpsimd.memset(r[:, 0:STILES, :], 0.0).then_inc(sem("r_zero"), 1)
            nc.gpsimd.memset(xT[:, :, 0:PAD], 0.0)
            nc.gpsimd.memset(xT[:, :, PAD + T:TP], 0.0).then_inc(sem("pads_zero"), 1)
            nc.gpsimd.memset(ones[:], 1.0).then_inc(sem("ones"), 1)
            def add_beta(q):
                pool.wait_ge(sem(f"x_back{q}"), 16)
                xq = x[:, TQ * q:TQ * q + TQ, :]
                nc.gpsimd.tensor_tensor(xq, xq, rows[:, 1:2, :].broadcast_to([P, TQ, D]), ALU.add).then_inc(
                    sem("x_beta"), 1)

            pool.wait_ge(sem("setup_in"), 16 * SETUP)
            pool_softplus(pool, 0, 0)
            for u in range(UNITS):
                for k in range(STEPS):
                    s = STEPS * u + k
                    pool.wait_ge(sem("m_scan"), s + 1)
                    pool.wait_ge(sem("m_ccopy"), 2 * s + 2)
                    if s >= 3:
                        pool.wait_ge(sem("m_ysum"), s - 2)
                    nc.gpsimd.tensor_tensor(hC[:, s % 3], hs[:, s % 3], Cs[s % 3], ALU.mult).then_inc(
                        sem("m_hc"), 1)
                    if k == 8:
                        pool_softplus(pool, u, 1)
                    if k == 28 and u + 1 < UNITS:
                        pool_softplus(pool, u + 1, 0)
                    if k in (8, 16) and u == UNITS - 1:
                        add_beta((k - 8) // 8)
            for q in (2, 3):
                add_beta(q)

            for f in range(2):
                if f == 0:
                    pool.wait_ge(sem("slots_zeroed"), 16)
                pool.wait_ge(sem(f"e{f}_index"), 1)
                for j in range(TILES):
                    nc.gpsimd.indirect_dma_start(
                        out=dispatched, out_offset=bass.IndirectOffsetOnAxis(ap=put_at[:, j:j + 1], axis=0),
                        in_=tokn[:, j, :], in_offset=None).then_inc(sem(f"e{f}_put"), 16)
                pool.wait_ge(sem(f"e{f}_stored"), 16 * EXPERTS)
                pool.wait_ge(sem(f"e{f}_put"), 16 * TILES)
                for j in range(TILES):
                    nc.gpsimd.indirect_dma_start(
                        out=tokn[:, j, :], out_offset=None, in_=expert_rows,
                        in_offset=bass.IndirectOffsetOnAxis(ap=get_at[:, j:j + 1], axis=0)).then_inc(
                        sem(f"e{f}_got{j // TQ}"), 16)
                if f == 0:
                    for g in range(GROUPS):
                        pool.wait_ge(sem("b_y"), g + 1)
                        pool.wait_ge(sem("b_sig"), 1)
                        sl = slice(512 * g, 512 * g + 512)
                        nc.gpsimd.tensor_tensor(kvS[:, sl], kvS[:, sl], rS[:, sl], ALU.mult).then_inc(
                            sem("b_sy"), 1)
                    for g in range(GROUPS):
                        pool.wait_ge(sem("b_relu"), 2 * g + 2)
                        nc.gpsimd.tensor_tensor(k2[:, g % 2, 0:2], k2[:, g % 2, 0:2], k2[:, g % 2, 0:2],
                                                ALU.mult).then_inc(sem("b_sqp"), 1)

        @block.scalar
        def _(act):
            act.wait_ge(sem("eps"), 1)
            act_norm(act, "n0")
            act.wait_ge(sem("setup_in"), 16 * SETUP)
            act.wait_ge(sem("pads_zero"), 1)
            act_turn(act, "t0", 1.0, 0.0)
            flat_a = acols[:].rearrange("p r h n -> p (r h n)")
            nc.scalar.activation(flat_a, flat_a, ACT.Exp).then_inc(sem("a_exp"), 1)
            act.wait_ge(sem("a_neg"), 1)
            act.wait_ge(sem("m_zero"), 1)

            for task, _ in bank_tasks(-1):
                act_bank(act, -1, task)
                if task == ("z", 1, 1):
                    act_silu(act, 0, xc, "m_silu")
                    act_silu(act, 0, sz, "m_gate")
                    nc.scalar.preload_act_table_set("natural_log_exp_and_others")
            act_softplus_exp(act, 0, 0)
            act_softplus_ln(act, 0, 0)
            act_dx(act, 0, 0)
            act_decay(act, 0)
            for u in range(UNITS):
                for k in range(STEPS):
                    s = STEPS * u + k
                    if k == LAG and u > 0:
                        act_leave(act, u - 1, 1)
                    if k == STATE + LAG:
                        act_leave(act, u, 0)
                    if k == 12:
                        act_dx(act, u, 1)
                    act_c(act, s, 0)
                    silu = k == SILU_STEP and u + 1 < UNITS
                    if silu:
                        act_silu(act, u + 1, sz, "m_gate")
                    elif s + 1 < STEPS * UNITS:
                        act_decay(act, s + 1)
                    act_c(act, s, 1)
                    if silu:
                        nc.scalar.preload_act_table_set("natural_log_exp_and_others")
                        act_decay(act, s + 1)
                    for task, steps in bank_tasks(u):
                        if int(steps[-1]) == k:
                            act_bank(act, u, task)
                    if k == SILU_STEP - 1 and u + 1 < UNITS:
                        act_silu(act, u + 1, xc, "m_silu")
                    if k == 4:
                        act_softplus_exp(act, u, 1)
                    if k == 5:
                        act_softplus_ln(act, u, 1)
                    if k == 26 and u + 1 < UNITS:
                        act_softplus_exp(act, u + 1, 0)
                    if k == 27 and u + 1 < UNITS:
                        act_softplus_ln(act, u + 1, 0)
                    if k == 30 and u + 1 < UNITS:
                        act_dx(act, u + 1, 0)
            act_leave(act, UNITS - 1, 1)
            for task, _ in bank_tasks(UNITS):
                act_bank(act, UNITS, task)

            act_norm(act, "n1")
            act_experts(act, 0)

            act_norm(act, "n2")
            act_norm(act, "n3")
            act_turn(act, "t3", col("ln1_g"), col("ln1_b"))
            nc.scalar.activation(small[:, 2:3], col("decay"), ACT.Exp).then_inc(sem("b_ed"), 1)
            act.wait_ge(sem("b_ed"), 1)
            nc.scalar.activation(small[:, 3:4], small[:, 2:3], ACT.Exp, scale=-1.0)
            nc.scalar.activation(small[:, 4:5], col("first"), ACT.Exp).then_inc(sem("b_ed"), 1)
            for g in range(GROUPS):
                act.wait_ge(sem("t3_out"), g + 1)
                nc.scalar.activation(xm[:, 512 * g:512 * g + 512].rearrange("p (b t) -> p b t", b=2),
                                     xT[:, 2 * g:2 * g + 2, PAD:PAD + T], ACT.Copy,
                                     scale=col("att_tm")).then_inc(sem("b_xm0"), 1)
            for g in range(GROUPS):
                sl = slice(512 * g, 512 * g + 512)
                act.wait_ge(sem("b_r"), g + 1)
                nc.scalar.activation(rS[:, sl], PS[:, 4 + g % 2, :], ACT.Copy).then_inc(sem("b_rcopy"), 1)
                act.wait_ge(sem("b_min"), g + 1)
                nc.scalar.activation(kS[:, sl], kS[:, sl], ACT.Exp).then_inc(sem("b_exp"), 1)
            act.wait_ge(sem("b_rcopy"), GROUPS)
            nc.scalar.activation(rS, rS, ACT.Sigmoid).then_inc(sem("b_sig"), 1)
            for g in range(GROUPS):
                act.wait_ge(sem("b_att"), g + 1)
                nc.scalar.activation(r[:, TG * g:TG * g + TG, :].rearrange("p t d -> p (t d)"), PS[:, g % 2, :],
                                     ACT.Copy).then_inc(sem("b_x2"), 1)
            act_norm(act, "n4")
            act_turn(act, "t4", col("ln2_g"), col("ln2_b"))
            for g in range(GROUPS):
                act.wait_ge(sem("t4_out"), g + 1)
                nc.scalar.activation(xm[:, 512 * g:512 * g + 512].rearrange("p (b t) -> p b t", b=2),
                                     xT[:, 2 * g:2 * g + 2, PAD:PAD + T], ACT.Copy,
                                     scale=col("ffn_tm")).then_inc(sem("c_xm0"), 1)
            for g in range(GROUPS):
                for i in range(2):
                    act.wait_ge(sem("b_fk"), 2 * g + i + 1)
                    if g >= 2:
                        act.wait_ge(sem("b_fv"), g - 1)
                    nc.scalar.activation(k2[:, g % 2, 2 * i:2 * i + 2].rearrange("p i t -> p (i t)"),
                                         flat(PS[:, 2 * i:2 * i + 2, :]), ACT.Relu).then_inc(sem("b_relu"), 1)
                act.wait_ge(sem("b_fv"), g + 1)
                if g >= 2:
                    act.wait_ge(sem("b_x3"), g - 1)
                nc.scalar.activation(sg[:, g % 2, :], PS[:, 5, :], ACT.Sigmoid).then_inc(sem("b_gate"), 1)
            act_experts(act, 1)

        @block.tensor
        def _(pe):
            pe.wait_ge(sem("setup_in"), 16 * SETUP)
            pe_turn(pe, "t0", r, "n0_out")
            pe.wait_ge(sem("t0_out"), GROUPS)
            pe.wait_ge(sem("m_weights"), 1)
            mm = nc.tensor.matmul
            for task, steps in bank_tasks(-1):
                for part in range(len(steps)):
                    pe_bank(pe, -1, task, part)
            for u in range(UNITS):
                for k in range(STEPS):
                    s = STEPS * u + k
                    if s == 0:
                        pe_input(pe, 0)
                    pe_c(pe, s, 0)
                    pe_parts(pe, u, k)
                    pe_c(pe, s, 1)
                    if s + 1 < STEPS * UNITS:
                        pe_input(pe, s + 1)
                    if s >= LAG:
                        for q in range(2):
                            pe_sum(pe, s - LAG, q)
                    pe_parts(pe, u, k + 0.5)
            for s in range(STEPS * UNITS - LAG, STEPS * UNITS):
                for q in range(2):
                    pe_sum(pe, s, q)
            for task, steps in bank_tasks(UNITS):
                for part in range(len(steps)):
                    pe_bank(pe, UNITS, task, part)

            pe_experts(pe, 0)

            pe.wait_ge(sem("wb_in"), 16 * 3)
            pe_turn(pe, "t3", tokn, "n3_out")
            for g in range(GROUPS):
                rhs = xm[:, 512 * g:512 * g + 512]
                pe.wait_ge(sem("b_xm"), g + 1)
                if g == 0:
                    pe.wait_ge(sem("t3_out"), GROUPS)
                if g >= 2:
                    pe.wait_ge(sem("b_kv"), g - 1)
                    pe.wait_ge(sem("b_rcopy"), g - 1)
                for w, name in enumerate(("b_k", "b_v", "b_r")):
                    mm(PS[:, 2 * w + g % 2, :], wsq[:, w, :], rhs, start=True, stop=True).then_inc(sem(name), 1)
            pe.wait_ge(sem("b_kv"), GROUPS)
            for g in range(GROUPS):
                pe.wait_ge(sem("b_sy"), g + 1)
                if g >= 2:
                    pe.wait_ge(sem("b_x2"), g - 1)
                for i in range(TG):
                    t0 = PAD + P * (i % 2)
                    dst = PS[:, g % 2, D * i:D * i + D]
                    mm(dst, xT[:, 2 * g + i // 2, t0:t0 + P], ident[:], start=True, stop=False)
                    last = mm(dst, kvS[:, 512 * g + P * i:512 * g + P * i + P], wsq[:, 3, :], start=False, stop=True)
                last.then_inc(sem("b_att"), 1)
            pe_turn(pe, "t4", tokn, "n4_out")
            for g in range(GROUPS):
                pe.wait_ge(sem("c_xm"), g + 1)
                if g == 0:
                    pe.wait_ge(sem("t4_out"), GROUPS)
                    pe.wait_ge(sem("b_rcopy"), GROUPS)
                for i in range(2):
                    if g >= 1:
                        pe.wait_ge(sem("b_relu"), 2 * g + i - 1)
                    for j in range(2):
                        last = mm(PS[:, 2 * i + j, :], fk[:, P * (2 * i + j):P * (2 * i + j) + P],
                                  xm[:, 512 * g:512 * g + 512], start=True, stop=True)
                    last.then_inc(sem("b_fk"), 1)
                pe.wait_ge(sem("b_sqp"), g + 1)
                pe.wait_ge(sem("b_sqv"), g + 1)
                if g >= 1:
                    pe.wait_ge(sem("b_x3"), g)
                    pe.wait_ge(sem("b_gate"), g)
                for i in range(TG):
                    t0 = PAD + P * (i % 2)
                    o = slice(D * i, D * i + D)
                    for j in range(FT):
                        mm(PS[:, 4, o], k2[:, g % 2, j, P * i:P * i + P], fv[:, j, :], start=(j == 0),
                           stop=(j == FT - 1))
                    mm(PS[:, 5, o], xm[:, 512 * g + P * i:512 * g + P * i + P], wsq[:, 4, :], start=True, stop=True)
                    last = mm(PS[:, 6, o], xT[:, 2 * g + i // 2, t0:t0 + P], ident[:], start=True, stop=True)
                last.then_inc(sem("b_fv"), 1)
            pe_experts(pe, 1)

        @block.vector
        def _(dve):
            chain = [0]

            def link(ins):
                chain[0] += 1
                ins.then_inc(sem("dve_chain"), 1)
                dve.wait_ge(sem("dve_chain"), chain[0])

            nc.vector.memset(ecol, EPS).then_inc(sem("eps"), 1)
            dA4 = [v.rearrange("p (b t) -> p b t", b=CB) for v in dA]
            for q in range(QUARTERS):
                dve.wait_ge(sem(f"x_in{q}"), 16)
            dve.wait_ge(sem("slots_zeroed"), 16)
            dve_norm_stats(dve, link, "n0", x)
            dve_norm_apply(dve, link, "n0", x, r)
            dve.wait_ge(sem("setup_in"), 16 * SETUP)
            for rev in range(2):
                w1 = inproj[:, rev, 0:INNER].rearrange("p (k n) -> p k n", k=1).broadcast_to([P, TAPS, INNER])
                last = nc.vector.tensor_tensor(convw[:, rev], convw[:, rev], w1, ALU.mult)
            last.then_inc(sem("m_weights"), 1)
            dve.wait_ge(sem("n0_out"), QUARTERS)
            for v in dA4:
                last = nc.vector.memset(v[:, :, 0:1], 0.0)
            last.then_inc(sem("m_zero"), 1)
            dve.wait_ge(sem("a_exp"), 1)
            flat_a = acols[:].rearrange("p r h n -> p (r h n)")
            nc.vector.tensor_scalar(flat_a, flat_a, -1.0, None, ALU.mult).then_inc(sem("a_neg"), 1)

            for i in range(4):
                dve_split(dve, 0, i)
            for u in range(UNITS):
                rev = u // CHUNKS
                way = slice(None, None, -1) if rev else slice(None)
                if u == CHUNKS:
                    dve.wait_ge(sem("m_scan"), STEPS * u)
                    for v in dA4:
                        last = nc.vector.memset(v[:, :, T - 1:T], 0.0)
                    last.then_inc(sem("m_reset"), 1)
                for k in range(STEPS):
                    h = k // STATE
                    s = STEPS * u + k
                    if 25 <= k < 29 and u + 1 < UNITS:
                        dve_split(dve, u + 1, k - 25)
                    xk = flat(X[s % 2])
                    if k % STATE == 0:
                        dve.wait_ge(sem("m_du"), 2 * u + h + 1)
                    dve.wait_ge(sem("m_b"), s + 1)
                    nc.vector.tensor_tensor(xk, du[:, u % 2, h], xk, ALU.mult).then_inc(sem("m_dbu"), 1)
                    for task, steps in bank_tasks(u):
                        if int(steps[-1]) == k:
                            dve_bank(dve, u, task)
                    dve.wait_ge(sem("m_dbu"), s + 1)
                    dve.wait_ge(sem("m_dA"), s + 1)
                    if s >= 3:
                        dve.wait_ge(sem("m_hc"), s - 2)
                    nc.vector.tensor_tensor_scan(hs[:, s % 3, way], dA[s % 3][:, way], xk[:, way], 0.0,
                                                 ALU.mult, ALU.add).then_inc(sem("m_scan"), 1)
            for task, _ in bank_tasks(UNITS):
                dve_bank(dve, UNITS, task)

            dve.wait_ge(sem("m_gfree"), bank_count(UNITS + 1))
            dve.wait_ge(sem("x_beta"), QUARTERS)
            dve_norm_stats(dve, link, "n1", yo)
            for q in range(QUARTERS):
                dve.wait_ge(sem("n1_sd"), q + 1)
                tiles = range(TQ * q, TQ * q + TQ)
                nc.vector.reciprocal(rstd[:, TQ * q:TQ * q + TQ], sd[:, TQ * q:TQ * q + TQ])
                for j in tiles:
                    last = nc.vector.scalar_tensor_tensor(out=yo[:, j, :], in0=yo[:, j, :], scalar=mv[:, j, 0:1],
                                                          in1=rows[:, 0, :], op0=ALU.subtract, op1=ALU.mult)
                link(last)
                for j in tiles:
                    last = nc.vector.scalar_tensor_tensor(out=x[:, j, :], in0=yo[:, j, :], scalar=rstd[:, j:j + 1],
                                                          in1=x[:, j, :], op0=ALU.mult, op1=ALU.add)
            link(last)
            dve_experts(dve, link, 0)

            dve_norm_stats(dve, link, "n2", x, ready=("e0_x", lambda q: q + 1))
            dve_norm_apply(dve, link, "n2", x, r)
            dve_norm_stats(dve, link, "n3", r)
            dve_norm_apply(dve, link, "n3", r, tokn)
            mix = small[:, 5:9]
            for i, (tm, cm) in enumerate((("att_tm", "att_cm"), ("ffn_tm", "ffn_cm"))):
                link(nc.vector.tensor_scalar(mix[:, 2 * i:2 * i + 1], col(tm), -1.0, 1.0, ALU.mult, ALU.add))
                link(nc.vector.scalar_tensor_tensor(out=mix[:, 2 * i:2 * i + 1], in0=col(cm), scalar=col("lo_mask"),
                                                    in1=mix[:, 2 * i:2 * i + 1], op0=ALU.mult, op1=ALU.add))
                link(nc.vector.tensor_scalar(mix[:, 2 * i + 1:2 * i + 2], col(cm), col("hi_mask"), None, ALU.mult))
            dve_mix(dve, link, "b", mix[:, 0:1], mix[:, 1:2])
            dve.wait_ge(sem("b_ed"), 2)
            link(nc.vector.memset(edT, 0.0))
            link(nc.vector.tensor_scalar(edT[:, :, 1:T], edT[:, :, 1:T], small[:, 3:4], None, ALU.add))
            for g in range(GROUPS):
                sl = slice(512 * g, 512 * g + 512)
                dve.wait_ge(sem("b_k"), g + 1)
                nc.vector.tensor_scalar(kS[:, sl], PS[:, g % 2, :], CLAMP, None, ALU.min).then_inc(sem("b_min"), 1)
                dve.wait_ge(sem("b_exp"), g + 1)
                dve.wait_ge(sem("b_v"), g + 1)
                nc.vector.tensor_tensor(kvS[:, sl], PS[:, 2 + g % 2, :], kS[:, sl], ALU.mult).then_inc(
                    sem("b_kv"), 1)
            dve.wait_ge(sem("b_kv"), GROUPS)
            dve.wait_ge(sem("t3_in"), GROUPS)
            a3, b3 = (v[:].rearrange("p t d -> p (t d)") for v in (a_s, b_s))
            ed = edT.rearrange("p b t -> p (b t)")
            for m in range(CHUNKS):
                sl = slice(CT * m, CT * m + CT)
                nc.vector.tensor_tensor_scan(a3[:, sl], ed, kvS[:, sl], 0.0, ALU.mult, ALU.add)
                last = nc.vector.tensor_tensor_scan(b3[:, sl], ed, kS[:, sl], 0.0, ALU.mult, ALU.add)
            link(last)

            def seqs(ap):
                return ap.rearrange("p (b t) -> p b t", b=BATCH)

            for cur, prev in ((kvS, a3), (kS, b3)):
                nc.vector.tensor_scalar(seqs(cur)[:, :, 0:1], seqs(cur)[:, :, 0:1], small[:, 4:5], None, ALU.mult)
                last = nc.vector.scalar_tensor_tensor(
                    out=seqs(cur)[:, :, 1:T], in0=seqs(cur)[:, :, 1:T], scalar=small[:, 4:5],
                    in1=seqs(prev)[:, :, 0:T - 1], op0=ALU.mult, op1=ALU.add)
            link(last)
            for g in range(GROUPS):
                sl = slice(512 * g, 512 * g + 512)
                link(nc.vector.reciprocal(kS[:, sl], kS[:, sl]))
                nc.vector.tensor_tensor(kvS[:, sl], kvS[:, sl], kS[:, sl], ALU.mult).then_inc(sem("b_y"), 1)
            dve_norm_stats(dve, link, "n4", r, ready=("b_x2", lambda q: 2 * q + 2))
            dve_norm_apply(dve, link, "n4", r, tokn)
            dve_mix(dve, link, "c", mix[:, 2:3], mix[:, 3:4])
            for g in range(GROUPS):
                dve.wait_ge(sem("b_relu"), 2 * g + 2)
                nc.vector.tensor_tensor(k2[:, g % 2, 2:4], k2[:, g % 2, 2:4], k2[:, g % 2, 2:4],
                                        ALU.mult).then_inc(sem("b_sqv"), 1)
                dve.wait_ge(sem("b_gate"), g + 1)
                xg = x[:, TG * g:TG * g + TG, :].rearrange("p t d -> p (t d)")
                link(nc.vector.tensor_tensor(sg[:, g % 2, :], sg[:, g % 2, :], PS[:, 4, :], ALU.mult))
                link(nc.vector.tensor_tensor(xg, xg, sg[:, g % 2, :], ALU.add))
                nc.vector.tensor_tensor(xg, xg, PS[:, 6, :], ALU.add).then_inc(sem("b_x3"), 1)
            dve.wait_ge(sem("b_x3"), GROUPS)
            dve_experts(dve, link, 1)

def kernel(**inputs):
    import numpy as np
    import ml_dtypes
    import concourse.bacc as bacc
    from concourse.bass_utils import run_bass_kernel_spmd

    A, B, F = "L0_attn_a_", "L0_attn_b_", "L0_ffn_"
    w = {k: np.asarray(v) for k, v in inputs.items()}
    dirs = ("fwd_", "bwd_")

    def halves(name):
        return [w[A + d + name][P * h:P * h + P] for d in dirs for h in range(HALVES)]

    lo = (np.arange(P) < P // 2).astype(np.float32)
    cols = np.stack(halves("conv_b") + halves("dt_proj_b") + halves("D") + [
        w[F + "ln_gamma"], w[F + "ln_beta"], w[B + "ln1_g"], w[B + "ln1_b"], w[B + "ln2_g"], w[B + "ln2_b"],
        w[B + "att_time_mix"].reshape(P), w[B + "att_combined_mix"].reshape(P),
        w[B + "ffn_time_mix"].reshape(P), w[B + "ffn_combined_mix"].reshape(P),
        w[B + "time_decay"], w[B + "time_first"], lo, np.float32(1) - lo], axis=1)

    def xproj(d):
        v = w[A + d + "x_proj_w"]
        return np.concatenate([v[RANK:]] * 3 + [v[:RANK]], axis=0).T.reshape(HALVES, P, 104).transpose(1, 0, 2)

    sel = np.zeros((96, 2 * STATE, P), ml_dtypes.bfloat16)
    for k in range(96):
        sel[k, k % 32] = 1
    tri = np.ones((P, 2, P), ml_dtypes.bfloat16)
    tri[:, 0] = np.triu(np.ones((P, P)), 1)
    tok = np.arange(P)[:, None] + P * np.arange(TILES)[None]
    route = np.concatenate([np.tile(np.arange(EXPERTS, 0, -1), (P, 1)), np.zeros((P, 1)), SLOTS + tok],
                           axis=1).astype(np.float32)
    arrays = {
        "x_in": w[A + "x"].reshape(NTOK, D),
        "cols_in": cols,
        "alog_in": np.stack([w[A + d + "A_log"].reshape(HALVES, P, STATE).transpose(1, 0, 2) for d in dirs], axis=1),
        "rows_in": np.stack([w[A + "ln_gamma"], w[A + "ln_beta"]]),
        "conv_in": np.stack([w[A + d + "conv_w"].T for d in dirs]),
        "inproj_in": np.stack([w[A + d + "in_proj_w"].T for d in dirs], axis=1),
        "xproj_in": np.stack([xproj(d) for d in dirs], axis=1),
        "dtproj_in": np.stack([w[A + d + "dt_proj_w"].T for d in dirs], axis=1),
        "outproj_in": np.stack([w[A + d + "out_proj_w"].T.reshape(HALVES, P, D).transpose(1, 0, 2) for d in dirs],
                               axis=1),
        "wsq_in": np.stack([w[B + n].T for n in ("Wk", "Wv", "Wr", "Wo", "Fr")], axis=1),
        "fk_in": w[B + "Fk"].T,
        "fv_in": w[B + "Fv"].T.reshape(FT, P, D).transpose(1, 0, 2),
        "gate_in": w[F + "gate_weight"].T,
        "wi_in": w[F + "wi"].transpose(1, 0, 2),
        "wo_in": w[F + "wo"].reshape(EXPERTS, FT, P, D).transpose(2, 0, 1, 3),
        "ident_in": np.eye(P, dtype=np.float32),
        "sel_in": sel,
        "tri_in": tri,
        "route_in": route,
    }
    arrays = {k: np.ascontiguousarray(v) for k, v in arrays.items()}
    nc = bacc.Bacc("TRN2", target_bir_lowering=False, num_devices=1)
    args = [nc.dram_tensor(k, v.shape, mybir.dt.from_np(v.dtype), kind="ExternalInput").ap()
            for k, v in arrays.items()]
    args.append(nc.dram_tensor("out", (BATCH, T, D), F32, kind="ExternalOutput").ap())
    layer(nc, *args)
    return run_bass_kernel_spmd(nc, [arrays], core_ids=[0]).results[0]["out"]
```

```python
from contextlib import ExitStack

import concourse.bass as bass
from concourse import mybir

F32 = mybir.dt.float32
BF16 = mybir.dt.bfloat16
I32 = mybir.dt.int32
ALU = mybir.AluOpType
ACT = mybir.ActivationFunctionType
AX = mybir.AxisListType

P = 128
BATCH, T, D = 16, 256, 128
NTOK = BATCH * T
TILES = NTOK // P
GROUPS = 8
TG = TILES // GROUPS
QUARTERS = 4
TQ = TILES // QUARTERS
PAD = 3
TP = T + 2 * PAD

INNER, STATE, TAPS, RANK = 256, 16, 4, 8
HALVES = INNER // P
CB = 4
CT = CB * T
CHUNKS = BATCH // CB
STEPS = HALVES * STATE
AHEAD = 2
LAG = 3
MIX_STEPS = GROUPS + 5
ATT_SLOTS = QUARTERS + 6
BC = 3 * 2 * STATE
UNITS = 2 * CHUNKS

SCHEDULE = [(("dt", 1, 0), [0]), (("dt", 1, 1), [1]), (("back", 0, 0), [2]), (("back", 0, 1), [3]),
            (("conv", 0, 0), [4, 5, 6, 6]), (("conv", 0, 1), [7, 8, 9, 9]),
            (("back", 1, 0), [10]), (("back", 1, 1), [11]), (("z", 0, 0), [12]),
            (("conv", 1, 0), [13, 14, 15, 15]), (("z", 0, 1), [16]), (("conv", 1, 1), [17, 18, 19, 19]),
            (("z", 1, 0), [20]), (("z", 1, 1), [21]), (("xp", 0), [23, 23]), (("xp", 1), [24, 24]),
            (("dt", 0, 0), [25]), (("dt", 0, 1), [26]), (("out", 0), [28, 29]), (("out", 1), [30, 31])]

SILU_STEP = 22


def bank_tasks(u):
    def has(task):
        if task[:2] == ("dt", 1):
            return 0 <= u < UNITS
        return 0 < u if task[0] in ("back", "out") else u + 1 < UNITS

    return [(task, steps) for task, steps in SCHEDULE if has(task)]


def bank_count(u):
    return sum(len(bank_tasks(v)) for v in range(-1, u))


EXPERTS, CAP, FF = 8, 256, 512
FT = FF // P
SLOTS = EXPERTS * CAP
STILES = SLOTS // P
SE = CAP // P
ROW = D + 2
CLAMP = 60.0
EPS = 1e-5

COLS = ["conv_b_f0", "conv_b_f1", "conv_b_b0", "conv_b_b1", "dt_b_f0", "dt_b_f1", "dt_b_b0", "dt_b_b1",
        "D_f0", "D_f1", "D_b0", "D_b1", "ffn_g", "ffn_b", "ln1_g", "ln1_b", "ln2_g", "ln2_b",
        "att_tm", "att_cm", "ffn_tm", "ffn_cm", "decay", "first", "lo_mask", "hi_mask"]
COL = {n: i for i, n in enumerate(COLS)}


def layer(nc, x_in, cols_in, alog_in, rows_in, conv_in, inproj_in, xproj_in, dtproj_in, outproj_in, wsq_in,
          fk_in, fv_in, gate_in, wi_in, wo_in, ident_in, sel_in, tri_in, route_in, out):
    dispatched = [nc.dram_tensor(f"dispatched{f}", (SLOTS + NTOK, ROW), F32, kind="Internal").ap() for f in range(2)]
    combined = [nc.dram_tensor(f"combined{f}", (SLOTS + NTOK, D), F32, kind="Internal").ap() for f in range(2)]

    with ExitStack() as ctx:
        def sb(name, shape, dt=F32):
            return ctx.enter_context(nc.sbuf_tensor(name, shape, dt))

        sems = {}

        def sem(name):
            if name not in sems:
                sems[name] = ctx.enter_context(nc.semaphore(name))
            return sems[name]

        x = sb("x", [P, TILES, D])
        r = sb("r", [P, TILES, D])
        rows_out = sb("rows_out", [P, TILES, ROW])
        tokn = rows_out[:, :, 0:D]
        xT = sb("xT", [P, BATCH, TP])
        work = sb("work", [P, 4 * NTOK])
        wi = sb("wi", [P, EXPERTS, FF])
        wo = sb("wo", [P, EXPERTS, FT, D])
        w_misc = sb("w_misc", [P, 5120])
        sel = sb("sel", [96, 2 * STATE, P], BF16)
        ident = sb("ident", [P, P])
        tri = sb("tri", [P, 2, P], BF16)
        route = sb("route", [P, EXPERTS + 2 * TILES + STILES])
        cols = sb("cols", [P, len(COLS)])
        rows = sb("rows", [P, 2, D])
        acols = sb("acols", [P, 2, HALVES, STATE])
        gateT = sb("gateT", [P, EXPERTS])
        small = sb("small", [P, 9])
        stats = sb("stats", [P, TILES, 6])
        mv = sb("mv", [P, TILES, 2])
        var = sb("var", [P, 2, TILES])
        rstd = sb("rstd", [P, 2, TILES])
        shift = sb("shift", [P, 2, TILES])
        minus_half = sb("minus_half", [P, 2, TQ])
        PS = ctx.enter_context(nc.psum_tensor("PS", [P, 8, 512], F32))

        def col(name):
            return cols[:, COL[name]:COL[name] + 1]

        def tiles_of(q):
            return slice(TQ * q, TQ * q + TQ)

        inproj = w_misc[:, 0:1024].rearrange("p (r n) -> p r n", r=2)
        convw = w_misc[:, 1024:3072].rearrange("p (r k n) -> p r k n", r=2, k=TAPS)
        xproj = w_misc[:, 3072:3488].rearrange("p (r h n) -> p r h n", r=2, h=HALVES)
        outproj = w_misc[:, 3488:4000].rearrange("p (r h n) -> p r h n", r=2, h=HALVES)
        dtproj = w_misc[BC:BC + RANK, 4000:4512].rearrange("p (r n) -> p r n", r=2)

        def two(k):
            return work[:, 4 * k * CT:4 * (k + 1) * CT].rearrange("p (c h t) -> p c h t", c=2, h=HALVES)

        xc, dt, du, sz = two(0), two(1), two(2), two(3)
        spare = [v[:].rearrange("p a b -> p (a b)") if len(v.shape) == 3 else v[:].rearrange("p a b c -> p (a b c)")
                 for v in (r, wi, wo)]
        hs = spare[0][:, 0:3 * CT].rearrange("p (k t) -> p k t", k=3)
        hC = spare[1][:, 0:3 * CT].rearrange("p (k t) -> p k t", k=3)
        parked = x[:].rearrange("p t d -> p (t d)")
        resid = parked[0:BC, 0:CT]
        raw = parked[0:BC + RANK, CT:2 * CT]
        dA = [spare[2][:, CT * i:CT * i + CT] for i in range(2)] + [parked[:, 2 * CT:3 * CT]]
        Cs = [spare[2][:, CT * i:CT * i + CT] for i in (2, 3)] + [parked[:, 3 * CT:4 * CT]]
        aux = [spare[0][:, 3 * CT:4 * CT], spare[1][:, 3 * CT:4 * CT]]
        yg = sb("yg", [P, HALVES, CT])
        parts = sb("parts", [BC, 2, CT], BF16)
        X = [PS[:, 0:2, :], PS[:, 2:4, :]]
        CB1 = PS[:, 4, :]
        G = PS[:, 5, :]
        Y = PS[:, 6:8, :]
        yo = tokn

        def flat(ap):
            return ap.rearrange("p a n -> p (a n)")

        eo = work[:, 0:2048].rearrange("p (s d) -> p s d", s=STILES)
        dispT = work[:, 2048:4096]
        hT = work[:, 4096:6144].rearrange("p (b i c) -> p b i c", b=2, i=FT)
        tokT = work[:, 12288:13312].rearrange("p (b t) -> p b t", b=2)
        slot_rows = work[:, 7168:7168 + STILES * ROW].rearrange("p (s d) -> p s d", s=STILES)
        rt = [work[:, 9728 + 64 * i:9792 + 64 * i].rearrange("p (t e) -> p t e", e=EXPERTS) for i in range(8)]
        rs = [work[:, 11264 + 8 * i:11272 + 8 * i] for i in range(12)]
        got = r
        onehot = sb("onehot", [P, TILES, EXPERTS], BF16)
        put_at = sb("put_at", [P, TILES], I32)
        back_at = sb("back_at", [P, STILES], I32)

        xm = work[:, 0:NTOK]
        kS = work[:, NTOK:2 * NTOK]
        kvS = work[:, 2 * NTOK:3 * NTOK]
        rS = work[:, 3 * NTOK:4 * NTOK]
        wsq = w_misc[:, 0:640].rearrange("p (w n) -> p w n", w=5)
        fk = w_misc[:, 640:1152]
        fv = w_misc[:, 1152:1664].rearrange("p (i n) -> p i n", i=FT)
        edT = w_misc[:, 1664:1664 + CT].rearrange("p (b t) -> p b t", b=CB)
        k2 = work[:, NTOK:2 * NTOK].rearrange("p (b i t) -> p b i t", b=2, i=FT)
        sg = work[:, 2 * NTOK:2 * NTOK + 1024].rearrange("p (b t) -> p b t", b=2)

        x_dram = x_in.rearrange("(q t p) d -> q p t d", q=QUARTERS, p=P)
        out_dram = out.rearrange("b t d -> (b t) d").rearrange("(q t p) d -> q p t d", q=QUARTERS, p=P)

        SETUP = 15

        block = ctx.enter_context(nc.Block())

        def one_bank(f, q):
            return f == 1 and q < QUARTERS - 1

        def turn_bank(f, g):
            return PS[:, 7 if one_bank(f, g // 2) else g % 2, :]

        def logit_bank(f, q):
            return PS[:, 7 if one_bank(f, q) else 2 + q % 2, 0:TQ * EXPERTS].rearrange("p (t e) -> p t e", e=EXPERTS)

        def count_bank(f, q):
            return PS[:, 7 if one_bank(f, q) else 4 + q % 2, 0:TQ * EXPERTS].rearrange("p (t e) -> p t e", e=EXPERTS)

        def sp_experts(sp, f):
            sp.wait_ge(sem(f"e{f}_put"), 16 * TILES)
            for g in range(4):
                n = EXPERTS // 4
                src = dispatched[f][CAP * n * g:CAP * n * (g + 1), :].rearrange("(e p i) d -> p e i d", e=n, i=SE)
                sp.dma_start(slot_rows[:, SE * n * g:SE * n * (g + 1), :].rearrange("p (e i) d -> p e i d", e=n),
                             src).then_inc(sem(f"e{f}_rows{g}"), 16)
            sp.wait_ge(sem(f"e{f}_back"), 16 * STILES)
            src = combined[f][SLOTS:SLOTS + NTOK, :].rearrange("(t p) d -> p t d", p=P)
            for q in range(QUARTERS):
                sp.dma_start(got[:, tiles_of(q), :], src[:, tiles_of(q), :]).then_inc(sem(f"e{f}_got{q}"), 16)

        def act_tokens(act, f, g):
            act.wait_ge(sem(f"e{f}_turned"), g + 1)
            if g >= 2:
                act.wait_ge(sem(f"e{f}_logit"), g - 1)
            nc.scalar.activation(tokT[:, g % 2, :], turn_bank(f, g), ACT.Identity, scale=col("ffn_g"),
                                 bias=col("ffn_b")).then_inc(sem(f"e{f}_tokT"), 1)

        def act_probs(act, f, q):
            act.wait_ge(sem(f"e{f}_sub"), q + 1)
            if q >= 2:
                act.wait_ge(sem(f"e{f}_den"), q - 1)
            nc.scalar.activation(rt[2 + q % 2], rt[q % 2], ACT.Exp).then_inc(sem(f"e{f}_prob"), 1)

        def act_route(act):
            for i in range(QUARTERS + 2):
                for q in (range(2) if i == 0 else (i + 1,)):
                    if q >= QUARTERS:
                        continue
                    act.wait_ge(sem("n1_shift"), q + 1)
                    for j in range(TQ * q, TQ * q + TQ):
                        last = nc.scalar.activation(yo[:, j, :], yo[:, j, :], ACT.Identity,
                                                    scale=rstd[:, 0, j:j + 1], bias=shift[:, 0, j:j + 1])
                    last.then_inc(sem("n1_unit"), 1)
                if 0 <= i - 1 < QUARTERS:
                    for g in (2 * i - 2, 2 * i - 1):
                        act_tokens(act, 0, g)
                if 0 <= i - 2:
                    act_probs(act, 0, i - 2)

        def act_experts(act, f):
            for g in range(STILES // TG):
                act.wait_ge(sem(f"e{f}_din"), g + 1)
                nc.scalar.activation(dispT[:, 512 * g:512 * g + 512], PS[:, g % 2, :], ACT.Identity,
                                     scale=col("ffn_g"), bias=col("ffn_b")).then_inc(sem(f"e{f}_dT"), 1)
            for e in range(EXPERTS):
                act.wait_ge(sem(f"e{f}_h"), e + 1)
                if e >= 2:
                    act.wait_ge(sem(f"e{f}_o"), e - 1)
                b = 4 + 2 * (e % 2)
                nc.scalar.activation(hT[:, e % 2].rearrange("p i c -> p (i c)"), flat(PS[:, b:b + 2, :]),
                                     ACT.Gelu).then_inc(sem(f"e{f}_gelu"), 1)

        def pe_tokens(pe, f, g):
            if g % 2 == 0:
                pe.wait_ge(sem(f"e{f}_out"), g // 2 + 1)
            if f == 0 and g >= 2:
                pe.wait_ge(sem(f"e{f}_tokT"), g - 1)
            if one_bank(f, g // 2) and g >= 1:
                pe.wait_ge(sem(f"e{f}_tokT"), g)
            if one_bank(f, g // 2) and g % 2 == 0 and g >= 2:
                pe.wait_ge(sem(f"e{f}_index"), g // 2)
            if f == 1 and not one_bank(f, g // 2):
                pe.wait_ge(sem("b_relu"), 2 * GROUPS)
                pe.wait_ge(sem("b_gate"), GROUPS)
            for i in range(TG):
                last = nc.tensor.transpose(turn_bank(f, g)[:, D * i:D * i + D], tokn[:, TG * g + i, :], ident[:])
            last.then_inc(sem(f"e{f}_turned"), 1)

        def pe_logits(pe, f, q):
            if f == 0 and q >= 2:
                pe.wait_ge(sem(f"e{f}_sub"), q - 1)
            for g in (2 * q, 2 * q + 1):
                pe.wait_ge(sem(f"e{f}_tokT"), 2 * q + 2 if one_bank(f, q) else g + 1)
                for i in range(TG):
                    last = nc.tensor.matmul(logit_bank(f, q)[:, TG * (g % 2) + i, :],
                                            tokT[:, g % 2, P * i:P * i + P], gateT[:], start=True, stop=True)
                last.then_inc(sem(f"e{f}_logit"), 1)

        def pe_counts(pe, f, q):
            mm = nc.tensor.matmul
            pe.wait_ge(sem(f"e{f}_onehot"), q + 1)
            if f == 0 and q >= 2:
                pe.wait_ge(sem(f"e{f}_index"), q - 1)
            earlier = count_bank(f, q)
            mm(earlier, tri[:, 0, :], onehot[:, tiles_of(q), :], start=True, stop=False)
            for j in range(TQ * q + TQ - 1):
                to = slice(max(j + 1, TQ * q), TQ * q + TQ)
                last = mm(earlier[:, to.start - TQ * q:, :], tri[:, 1, :],
                          onehot[:, j:j + 1, :].broadcast_to([P, to.stop - to.start, EXPERTS]), start=False,
                          stop=(j == TQ * q + TQ - 2))
            last.then_inc(sem(f"e{f}_counts"), 1)

        def pe_route(pe):
            for q in range(QUARTERS + 1):
                if q < QUARTERS:
                    pe_tokens(pe, 0, 2 * q)
                    pe_tokens(pe, 0, 2 * q + 1)
                    pe_logits(pe, 0, q)
                if q >= 1:
                    pe_counts(pe, 0, q - 1)

        def pe_experts(pe, f):
            mm = nc.tensor.matmul
            for g in range(STILES // TG):
                pe.wait_ge(sem(f"e{f}_rows{g}"), 16)
                if g >= 2:
                    pe.wait_ge(sem(f"e{f}_dT"), g - 1)
                for i in range(TG):
                    last = nc.tensor.transpose(PS[:, g % 2, D * i:D * i + D], slot_rows[:, TG * g + i, 0:D], ident[:])
                last.then_inc(sem(f"e{f}_din"), 1)

            def second(e):
                pe.wait_ge(sem(f"e{f}_gelu"), e + 1)
                if e == 0:
                    pe.wait_ge(sem("wo_in"), 16)
                if e >= 2:
                    pe.wait_ge(sem(f"e{f}_eo"), e - 1)
                for s in range(SE):
                    for i in range(FT):
                        last = mm(PS[:, 2 + e % 2, D * s:D * s + D], hT[:, e % 2, i, P * s:P * s + P],
                                  wo[:, e, i, :], start=(i == 0), stop=(i == FT - 1))
                last.then_inc(sem(f"e{f}_o"), 1)

            pe.wait_ge(sem("wi_in"), 16)
            pe.wait_ge(sem(f"e{f}_index"), QUARTERS)
            for e in range(EXPERTS):
                pe.wait_ge(sem(f"e{f}_dT"), e // 2 + 1)
                if e >= 2:
                    pe.wait_ge(sem(f"e{f}_gelu"), e - 1)
                for i in range(FT):
                    last = mm(PS[:, 4 + 2 * (e % 2) + i // 2, CAP * (i % 2):CAP * (i % 2) + CAP],
                              wi[:, e, P * i:P * i + P], dispT[:, CAP * e:CAP * e + CAP], start=True, stop=True)
                last.then_inc(sem(f"e{f}_h"), 1)
                if e >= 1:
                    second(e - 1)
            second(EXPERTS - 1)

        def pool_put(pool, f, tiles):
            for j in tiles:
                pool.wait_ge(sem(f"e{f}_index"), j // TQ + 1)
                nc.gpsimd.indirect_dma_start(
                    out=dispatched[f], out_offset=bass.IndirectOffsetOnAxis(ap=put_at[:, j:j + 1], axis=0),
                    in_=rows_out[:, j, :], in_offset=None).then_inc(sem(f"e{f}_put"), 16)

        def pool_route(pool):
            for i in range(QUARTERS + 3):
                for q in (range(2) if i == 0 else (i + 1,)):
                    if q >= QUARTERS:
                        continue
                    pool.wait_ge(sem("n1_unit"), q + 1)
                    nc.gpsimd.tensor_tensor(yo[:, tiles_of(q), :], yo[:, tiles_of(q), :],
                                            rows[:, 0:1, :].broadcast_to([P, TQ, D]), ALU.mult).then_inc(
                        sem("n1_gamma"), 1)
                if i < QUARTERS:
                    pool_rstd(pool, "e0", i, slice(0, 2))
                if 0 <= i - 3:
                    pool_put(pool, 0, range(TQ * (i - 3), TQ * (i - 2)))

        def pool_experts(pool, f):
            for e in range(EXPERTS):
                pool.wait_ge(sem(f"e{f}_eo"), e + 1)
                for s in range(SE * e, SE * e + SE):
                    nc.gpsimd.indirect_dma_start(
                        out=combined[f], out_offset=bass.IndirectOffsetOnAxis(ap=back_at[:, s:s + 1], axis=0),
                        in_=eo[:, s, :], in_offset=None).then_inc(sem(f"e{f}_back"), 16)

        def dve_mix(dve, link, name, q, prev_w, next_w):
            for g in (2 * q, 2 * q + 1):
                xg = xm[:, 512 * g:512 * g + 512].rearrange("p (b t) -> p b t", b=2)
                dve.wait_ge(sem(f"{name}_xm0"), g + 1)
                link(nc.vector.scalar_tensor_tensor(out=xg, in0=xT[:, 2 * g:2 * g + 2, PAD - 1:PAD - 1 + T],
                                                    scalar=prev_w, in1=xg, op0=ALU.mult, op1=ALU.add))
                nc.vector.scalar_tensor_tensor(out=xg, in0=xT[:, 2 * g:2 * g + 2, PAD + 1:PAD + 1 + T],
                                               scalar=next_w, in1=xg, op0=ALU.mult, op1=ALU.add).then_inc(
                    sem(f"{name}_xm"), 1)

        def dve_router(dve, link, f):
            mx, rank, keep, t1, t2, t3, t4, t5 = rs[2:10]
            token = route[:, EXPERTS:EXPERTS + TILES]
            own = route[:, EXPERTS + TILES:EXPERTS + 2 * TILES]
            pri = route[:, 0:EXPERTS].rearrange("p (t e) -> p t e", t=1).broadcast_to([P, TQ, EXPERTS])

            def per_expert(v):
                return v.rearrange("p (t e) -> p t e", e=1).broadcast_to([P, TQ, EXPERTS])

            def choose(q):
                qs = tiles_of(q)
                sub, first = rt[q % 2], rs[q % 2]
                dve.wait_ge(sem(f"e{f}_logit"), 2 * q + 2)
                link(nc.vector.tensor_reduce(mx, logit_bank(f, q), AX.X, ALU.max))
                if q >= 2:
                    dve.wait_ge(sem(f"e{f}_prob"), q - 1)
                nc.vector.tensor_tensor(sub, logit_bank(f, q), per_expert(mx), ALU.subtract).then_inc(sem(f"e{f}_sub"), 1)
                dve.wait_ge(sem(f"e{f}_sub"), q + 1)
                link(nc.vector.scalar_tensor_tensor(out=rt[4], in0=sub, scalar=0.0, in1=pri, op0=ALU.is_ge,
                                                    op1=ALU.mult))
                link(nc.vector.tensor_reduce(first, rt[4], AX.X, ALU.max))
                nc.vector.tensor_tensor(onehot[:, qs, :], rt[4], per_expert(first), ALU.is_equal).then_inc(
                    sem(f"e{f}_onehot"), 1)

            def place(q):
                qs = tiles_of(q)
                first = rs[q % 2]
                dve.wait_ge(sem(f"e{f}_onehot"), q + 1)
                dve.wait_ge(sem(f"e{f}_counts"), q + 1)
                link(nc.vector.tensor_tensor(rt[5], count_bank(f, q), onehot[:, qs, :], ALU.mult))
                link(nc.vector.tensor_reduce(rank, rt[5], AX.X, ALU.add))
                nc.vector.tensor_scalar(keep, rank, float(CAP), None, ALU.is_lt)
                link(nc.vector.scalar_tensor_tensor(out=t1, in0=first, scalar=-float(CAP), in1=rank, op0=ALU.mult,
                                                    op1=ALU.add))
                link(nc.vector.tensor_tensor(t2, t1, token[:, qs], ALU.subtract))
                link(nc.vector.tensor_tensor(t3, t2, keep, ALU.mult))
                link(nc.vector.tensor_tensor(t4, t3, own[:, qs], ALU.add))
                nc.vector.tensor_copy(put_at[:, qs], t4)
                dve.wait_ge(sem(f"e{f}_prob"), q + 1)
                nc.vector.tensor_reduce(t5, rt[2 + q % 2], AX.X, ALU.add).then_inc(sem(f"e{f}_den"), 1)
                dve.wait_ge(sem(f"e{f}_den"), q + 1)
                link(nc.vector.reciprocal(mx, t5))
                nc.vector.tensor_tensor(rows_out[:, qs, D + 1], mx, keep, ALU.mult).then_inc(sem(f"e{f}_index"), 1)
                dve.wait_ge(sem(f"e{f}_index"), q + 1)

            return choose, place

        def dve_route(dve, link):
            choose, place = dve_router(dve, link, 0)
            for i in range(QUARTERS + 3):
                if i < QUARTERS:
                    dve.wait_ge(sem("n1_gamma"), i + 1)
                    dve.wait_ge(sem("x_beta"), QUARTERS)
                    link(nc.vector.tensor_tensor(x[:, tiles_of(i), :], x[:, tiles_of(i), :],
                                                 yo[:, tiles_of(i), :], ALU.add))
                    dve_stats(dve, link, "e0", x, i)
                if 0 <= i - 1 < QUARTERS:
                    dve_apply(dve, "e0", x, tokn, i - 1, 1)
                if 0 <= i - 2 < QUARTERS:
                    choose(i - 2)
                if 0 <= i - 3:
                    place(i - 3)

        def dve_experts(dve, link, f):
            link(nc.vector.tensor_scalar(shift[:, 1, :], rstd[:, 0, :], 1.0, None, ALU.add))
            link(nc.vector.tensor_tensor(shift[:, 0, :], mv[:, :, 0], rstd[:, 0, :], ALU.mult))
            for j in range(TILES):
                last = nc.vector.tensor_scalar(x[:, j, :], x[:, j, :], shift[:, 1, j:j + 1], shift[:, 0, j:j + 1],
                                               ALU.mult, ALU.subtract)
            last.then_inc(sem(f"e{f}_own"), 1)
            for g in range(4):
                dve.wait_ge(sem(f"e{f}_rows{g}"), 16)
            link(nc.vector.tensor_copy(back_at[:], slot_rows[:, :, D]))
            for e in range(EXPERTS):
                dve.wait_ge(sem(f"e{f}_o"), e + 1)
                for i in range(SE):
                    last = nc.vector.tensor_scalar(eo[:, SE * e + i, :], PS[:, 2 + e % 2, D * i:D * i + D],
                                                   slot_rows[:, SE * e + i, D + 1:D + 2], None, ALU.mult)
                last.then_inc(sem(f"e{f}_eo"), 1)

        def combine(eng, add, f, q, done):
            eng.wait_ge(sem(f"e{f}_got{q}"), 16)
            eng.wait_ge(sem(f"e{f}_own"), 1)
            add(x[:, tiles_of(q), :], x[:, tiles_of(q), :], got[:, tiles_of(q), :], ALU.add).then_inc(
                sem(done), 1)

        def dve_stats(dve, link, name, src, q):
            for j in range(TQ * q, TQ * q + TQ):
                last = nc.vector.bn_stats(stats[:, j, :], src[:, j, :])
            link(last)
            for j in range(TQ * q, TQ * q + TQ):
                last = nc.vector.bn_aggr(mv[:, j, :], stats[:, j, :])
            link(last)
            nc.vector.tensor_scalar(var[:, 0, tiles_of(q)], mv[:, tiles_of(q), 1], EPS, None, ALU.add)
            nc.vector.tensor_scalar(var[:, 1, tiles_of(q)], mv[:, tiles_of(q), 1], 1.0 + EPS, EPS * EPS, ALU.mult,
                                    ALU.add).then_inc(sem(f"{name}_var"), 1)

        def pool_rstd(pool, name, q, which):
            pool.wait_ge(sem(f"{name}_var"), q + 1)
            nc.gpsimd.tensor_tensor(rstd[:, which, tiles_of(q)], var[:, which, tiles_of(q)], minus_half[:, which],
                                    ALU.pow).then_inc(sem(f"{name}_rstd"), 1)

        def dve_apply(dve, name, src, dst, q, which):
            dve.wait_ge(sem(f"{name}_rstd"), q + 1)
            for j in range(TQ * q, TQ * q + TQ):
                last = nc.vector.tensor_scalar(dst[:, j, :], src[:, j, :], mv[:, j, 0:1],
                                               rstd[:, which, j:j + 1], ALU.subtract, ALU.mult)
            last.then_inc(sem(f"{name}_out"), 1)

        def pe_turn(pe, name, src, ready, q, banks, turn=None):
            pe.wait_ge(sem(ready), q + 1)
            for k in range(2):
                g, n = 2 * q + k, 2 * (q if turn is None else turn) + k
                if n >= len(banks):
                    pe.wait_ge(sem(f"{name}_out"), n - len(banks) + 1)
                for i in range(TG):
                    last = nc.tensor.transpose(PS[:, banks[n % len(banks)], D * i:D * i + D], src[:, TG * g + i, :],
                                               ident[:])
                last.then_inc(sem(f"{name}_in"), 1)

        def act_turn(act, name, scale, bias, q, banks, turn=None):
            for k in range(2):
                g, n = 2 * q + k, 2 * (q if turn is None else turn) + k
                act.wait_ge(sem(f"{name}_in"), n + 1)
                nc.scalar.activation(xT[:, 2 * g:2 * g + 2, PAD:PAD + T],
                                     PS[:, banks[n % len(banks)], :].rearrange("p (b t) -> p b t", b=2),
                                     ACT.Identity, scale=scale, bias=bias).then_inc(sem(f"{name}_out"), 1)

        def act_mix(act, turned, name, tm, q):
            for g in (2 * q, 2 * q + 1):
                act.wait_ge(sem(turned), g + 1)
                nc.scalar.activation(xm[:, 512 * g:512 * g + 512].rearrange("p (b t) -> p b t", b=2),
                                     xT[:, 2 * g:2 * g + 2, PAD:PAD + T], ACT.Copy, scale=tm).then_inc(sem(name), 1)

        def task_number(u, task):
            return bank_count(u) + [t for t, _ in bank_tasks(u)].index(task)

        def task_bank(u, task):
            return PS[:, 5 - (task_number(u, task) - bank_count(u)) % 2, :] if u in (-1, UNITS) else G

        def block512(q):
            return slice(512 * q, 512 * q + 512)

        def pe_spread(u, row, q, dst):
            return nc.tensor.matmul(dst, sel[:, row, :], parts[:, u % 2, block512(q)], start=True, stop=True)

        def pe_input(pe, s):
            u, k = divmod(s, STEPS)
            if k == 0:
                pe.wait_ge(sem("m_split"), u + 1)
            if s >= 2:
                pe.wait_ge(sem("m_scan"), s - 1)
            for q in range(2):
                last = pe_spread(u, k % STATE, q, X[s % 2][:, q, :])
            last.then_inc(sem("m_b"), 1)

        def pe_c(pe, s, q):
            u, k = divmod(s, STEPS)
            if s + q > 0:
                pe.wait_ge(sem("m_ccopy"), 2 * s + q)
            pe_spread(u, STATE + k % STATE, q, CB1).then_inc(sem("m_c"), 1)

        def pe_sum(pe, s, q):
            u, k = divmod(s, STEPS)
            h, n = divmod(k, STATE)
            terms = [hC[:, s % 3]]
            if n == 0:
                if q == 0:
                    if 2 * u + h > 0:
                        pe.wait_ge(sem("m_yout"), 2 * u + h)
                    pe.wait_ge(sem("m_dx"), 2 * u + h + 1)
                terms = [aux[h], hC[:, s % 3]]
            for v, term in enumerate(terms):
                if v == len(terms) - 1 and q == 0:
                    pe.wait_ge(sem("m_hc"), s + 1)
                for i in range(4 * q, 4 * q + 4):
                    last = nc.tensor.matmul(flat(Y)[:, P * i:P * i + P], term[:, P * i:P * i + P], ident[:],
                                            start=(n == 0 and v == 0 and i % 4 == 0),
                                            stop=(n == STATE - 1 and i % 4 == 3), is_transpose=True)
            if q == 1:
                last.then_inc(sem("m_ysum"), 1)

        def act_c(act, s, q):
            act.wait_ge(sem("m_c"), 2 * s + q + 1)
            if s >= 3:
                act.wait_ge(sem("m_hc"), s - 2)
            nc.scalar.activation(Cs[s % 3][:, block512(q)], CB1, ACT.Copy).then_inc(sem("m_ccopy"), 1)

        def act_leave(act, u, h):
            act.wait_ge(sem("m_ysum"), STEPS * u + STATE * (h + 1))
            nc.scalar.activation(du[:, u % 2, h], flat(Y), ACT.Copy).then_inc(sem("m_yout"), 1)

        def pe_bank(pe, u, task, part):
            mm = nc.tensor.matmul
            number = task_number(u, task)
            G = task_bank(u, task)
            before = number - 1 if u in (-1, UNITS) and number > bank_count(u) else number
            if part == 0 and before > 0:
                pe.wait_ge(sem("m_gfree"), before)
            if part == 0 and u == UNITS:
                pe.wait_ge(sem("m_ccopy"), 2 * STEPS * UNITS)
            kind, q = task[0], task[-1]
            g2 = G.rearrange("p (b t) -> p b t", b=2)
            v = u + 1
            rev, c = divmod(v, CHUNKS)
            seqs = slice(CB * c + 2 * q, CB * c + 2 * q + 2)
            parts_of = 1
            if kind == "z":
                h = task[1]
                last = mm(g2, inproj[:, rev, INNER + P * h:INNER + P * h + P], xT[:, seqs, PAD:PAD + T],
                          start=True, stop=True)
            elif kind == "conv":
                h = task[1]
                parts_of = TAPS
                off = 2 * PAD - part if rev else part
                last = mm(g2, convw[:, rev, part, P * h:P * h + P], xT[:, seqs, off:off + T],
                          start=(part == 0), stop=(part == TAPS - 1))
            elif kind == "xp":
                parts_of = HALVES
                if part == 0:
                    pe.wait_ge(sem("m_silu"), v + 1)
                last = mm(G[0:BC + RANK], xproj[:, rev, part, :], xc[:, v % 2, part, block512(q)],
                          start=(part == 0), stop=(part == 1))
            elif kind == "dt":
                h = task[1]
                last = mm(G, dtproj[:, (v - h) // CHUNKS, P * h:P * h + P], raw[BC:BC + RANK, block512(q)],
                          start=True, stop=True)
            elif kind == "back":
                h = task[1]
                pe.wait_ge(sem("m_yout"), 2 * (u - 1) + h + 1)
                for i in range(4):
                    last = nc.tensor.transpose(G[:, P * i:P * i + P],
                                               du[:, (u - 1) % 2, h, P * (4 * q + i):P * (4 * q + i) + P], ident[:])
            else:
                parts_of = 2
                for i in (2 * part, 2 * part + 1):
                    for h in range(HALVES):
                        last = mm(G[:, D * i:D * i + D], yg[:, h, P * (4 * q + i):P * (4 * q + i) + P],
                                  outproj[:, (u - 1) // CHUNKS, h, :], start=(h == 0), stop=(h == 1))
            if part == parts_of - 1:
                last.then_inc(sem("m_g"), 1)

        def pe_parts(pe, u, step):
            for task, steps in bank_tasks(u):
                for part in range(len(steps)):
                    if steps[part] == step:
                        pe_bank(pe, u, task, part)

        def act_bank(act, u, task):
            number = task_number(u, task)
            kind, q = task[0], task[-1]
            v = u + 1 - (task[:2] == ("dt", 1))
            d = "fb"[min(v, UNITS - 1) // CHUNKS]
            b = block512(q)
            if kind == "back" or (kind == "out" and u > CHUNKS):
                return
            act.wait_ge(sem("m_g"), number + 1)
            G = task_bank(u, task)
            if kind == "z":
                if v >= 2:
                    h = task[1]
                    act.wait_ge(sem("m_gfree"), task_number(u, ("back", h, 1)) + 1)
                nc.scalar.activation(sz[:, v % 2, task[1], b], G, ACT.Copy).then_inc(sem("m_gfree"), 1)
            elif kind == "conv":
                nc.scalar.activation(xc[:, v % 2, task[1], b], G, ACT.Identity,
                                     bias=col(f"conv_b_{d}{task[1]}")).then_inc(sem("m_gfree"), 1)
            elif kind == "xp":
                if v >= 1:
                    act.wait_ge(sem("m_split"), v)
                nc.scalar.activation(raw[:, b], G[0:BC + RANK], ACT.Copy).then_inc(sem("m_gfree"), 1)
            elif kind == "dt":
                h = task[1]
                bias = col(f"dt_b_{d}{h}")
                if v >= 1 and q == 0:
                    act.wait_ge(sem("m_ysum"), STEPS * (v - 1) + STATE * h + 1)
                nc.scalar.activation(aux[h][:, b], G, ACT.Abs, bias=bias)
                nc.scalar.activation(dt[:, v % 2, h, b], G, ACT.Relu, bias=bias).then_inc(sem("m_gfree"), 1)
            else:
                c = u - 1
                if u == 1 and q == 0:
                    act.wait_ge(sem("slots_empty"), 16 * 6)
                nc.scalar.activation(yo[:, TQ * c + 4 * q:TQ * c + 4 * q + 4, :],
                                     G.rearrange("p (t d) -> p t d", d=D), ACT.Copy).then_inc(sem("m_gfree"), 1)

        def act_silu(act, v, t, done):
            act.wait_ge(sem("m_gfree"), task_number(v - 1, ("z", 1, 1)) + 1)
            t2 = t[:, v % 2].rearrange("p h t -> p (h t)")
            nc.scalar.activation(t2, t2, ACT.Silu).then_inc(sem(done), 1)

        def act_decay(act, s):
            u, k = divmod(s, STEPS)
            h, n = divmod(k, STATE)
            rev = u // CHUNKS
            on = slice(0, T - 1) if rev else slice(1, T)
            if n == 0:
                act.wait_ge(sem("m_dt"), 2 * u + h + 1)
            if s >= 3:
                act.wait_ge(sem("m_scan"), s - 2)
            if rev and s - STEPS * CHUNKS < 3:
                act.wait_ge(sem("m_reset"), s - STEPS * CHUNKS + 1)
            nc.scalar.activation(dA[s % 3].rearrange("p (b t) -> p b t", b=CB)[:, :, on],
                                 dt[:, u % 2, h].rearrange("p (b t) -> p b t", b=CB)[:, :, on], ACT.Exp,
                                 scale=acols[:, rev, h, n:n + 1]).then_inc(sem("m_dA"), 1)

        def act_dx(act, u, h):
            act.wait_ge(sem("m_dt"), 2 * u + h + 1)
            nc.scalar.activation(aux[h], xc[:, u % 2, h], ACT.Copy,
                                 scale=col(f"D_{'fb'[u // CHUNKS]}{h}")).then_inc(sem("m_dx"), 1)

        def act_softplus_exp(act, v, h):
            act.wait_ge(sem("m_gfree"), task_number(v - 1 + h, ("dt", h, 1)) + 1)
            nc.scalar.activation(aux[h], aux[h], ACT.Exp, scale=-1.0).then_inc(sem("m_spexp"), 1)

        def act_softplus_ln(act, v, h):
            act.wait_ge(sem("m_spexp"), 2 * v + h + 1)
            nc.scalar.activation(aux[h], aux[h], ACT.Ln, bias=1.0).then_inc(sem("m_sp"), 1)

        def dve_bank(dve, u, task):
            number = task_number(u, task)
            kind, q = task[0], task[-1]
            G = task_bank(u, task)
            if kind == "back":
                h = task[1]
                w = u - 1
                dve.wait_ge(sem("m_g"), number + 1)
                dve.wait_ge(sem("m_gate"), w + 1)
                nc.vector.tensor_tensor(yg[:, h, block512(q)], G, sz[:, w % 2, h, block512(q)], ALU.mult).then_inc(
                    sem("m_gfree"), 1)
            elif kind == "out" and u > CHUNKS:
                c = u - 1 - CHUNKS
                dve.wait_ge(sem("m_g"), number + 1)
                yc = yo[:, TQ * c + 4 * q:TQ * c + 4 * q + 4, :]
                nc.vector.tensor_tensor(yc, yc, G.rearrange("p (t d) -> p t d", d=D), ALU.add).then_inc(
                    sem("m_gfree"), 1)

        def pool_softplus(pool, v, h):
            pool.wait_ge(sem("m_sp"), 2 * v + h + 1)
            nc.gpsimd.tensor_tensor(dt[:, v % 2, h], dt[:, v % 2, h], aux[h], ALU.add).then_inc(sem("m_dt"), 1)
            pool.wait_ge(sem("m_dt"), 2 * v + h + 1)
            if v >= 2:
                pool.wait_ge(sem("m_g"), task_number(v - 1, ("back", h, 1)) + 1)
            nc.gpsimd.tensor_tensor(du[:, v % 2, h], dt[:, v % 2, h], xc[:, v % 2, h], ALU.mult).then_inc(
                sem("m_du"), 1)

        def dve_split(dve, v, i):
            if i == 0:
                dve.wait_ge(sem("m_gfree"), task_number(v - 1, ("xp", 1)) + 1)
            else:
                dve.wait_ge(sem("m_part"), 3 * v + i)
            p3 = parts[:, v % 2]
            if i == 0:
                nc.vector.tensor_copy(p3, raw[0:BC]).then_inc(sem("m_part"), 1)
            elif i == 1:
                nc.vector.tensor_tensor(resid, raw[0:BC], p3, ALU.subtract).then_inc(sem("m_part"), 1)
            elif i == 2:
                nc.vector.tensor_copy(p3[32:64], resid[32:64])
                nc.vector.tensor_copy(p3[64:96], resid[64:96]).then_inc(sem("m_part"), 1)
            else:
                nc.vector.tensor_tensor(p3[64:96], resid[64:96], p3[64:96], ALU.subtract).then_inc(sem("m_split"), 1)

        @block.sync
        def _(sp):
            for q in range(QUARTERS):
                sp.dma_start(x[:, TQ * q:TQ * q + TQ, :], x_dram[q]).then_inc(sem(f"x_in{q}"), 16)
            s = sem("setup_in")
            for dst, src in (
                (cols[:], cols_in), (acols[:], alog_in), (ident[:], ident_in), (sel[:], sel_in), (tri[:], tri_in),
                (route[:], route_in), (gateT[:], gate_in), (rows[:], rows_in.partition_broadcast(P)),
                (convw, conv_in.partition_broadcast(P)), (inproj, inproj_in),
                (xproj[:, 0], xproj_in[:, 0]), (xproj[:, 1], xproj_in[:, 1]),
                (outproj[:, 0], outproj_in[:, 0]), (outproj[:, 1], outproj_in[:, 1]), (dtproj, dtproj_in),
            ):
                sp.dma_start(dst, src).then_inc(s, 16)
            sp.wait_ge(sem("slots_made"), 1)
            for f in range(2):
                sp.dma_start(dispatched[f][0:SLOTS, :].rearrange("(e p i) d -> p e i d", e=EXPERTS, i=SE),
                             rows_out[:, 0:STILES, :].rearrange("p (e i) d -> p e i d", e=EXPERTS)).then_inc(
                    sem("slots_empty"), 16)
                for i in range(2):
                    sp.dma_start(combined[f][SLOTS * (i + 1):SLOTS * (i + 2), :].rearrange("(s p) d -> p s d", p=P),
                                 rows_out[:, 0:STILES, 0:D]).then_inc(sem("slots_empty"), 16)

            sp.wait_ge(sem("m_split"), UNITS)
            sp.wait_ge(sem("m_gfree"), task_number(UNITS - 1, ("dt", 1, 1)) + 1)
            for q in range(2):
                sp.dma_start(x[:, TQ * q:TQ * q + TQ, :], x_dram[q]).then_inc(sem(f"x_back{q}"), 16)
            sp.wait_ge(sem("m_ysum"), STEPS * UNITS)
            for q in (2, 3):
                sp.dma_start(x[:, TQ * q:TQ * q + TQ, :], x_dram[q]).then_inc(sem(f"x_back{q}"), 16)
            sp.dma_start(wi[:], wi_in).then_inc(sem("wi_in"), 16)
            sp.dma_start(wo[:], wo_in).then_inc(sem("wo_in"), 16)
            sp_experts(sp, 0)
            s = sem("wb_in")
            for dst, src in ((wsq, wsq_in), (fk, fk_in), (fv, fv_in)):
                sp.dma_start(dst, src).then_inc(s, 16)
            sp_experts(sp, 1)
            for q in range(QUARTERS):
                sp.wait_ge(sem("x_pool" if q % 2 else "x_dve"), (4 if q % 2 else 2) + q // 2)
                sp.dma_start(out_dram[q], x[:, TQ * q:TQ * q + TQ, :]).then_inc(sem("stored"), 16)
            sp.wait_ge(sem("stored"), 16 * QUARTERS)

        @block.gpsimd
        def _(pool):
            nc.gpsimd.memset(minus_half[:], -0.5).then_inc(sem("minus_half"), 1)
            pool.wait_ge(sem("minus_half"), 1)
            nc.gpsimd.memset(xT[:, :, 0:PAD], 0.0)
            nc.gpsimd.memset(xT[:, :, PAD + T:TP], 0.0).then_inc(sem("pads_zero"), 1)
            nc.gpsimd.memset(rows_out[:, 0:STILES, :], 0.0).then_inc(sem("rows_zero"), 1)
            for q in range(QUARTERS):
                pool_rstd(pool, "n0", q, 0)
            def add_beta(q):
                pool.wait_ge(sem(f"x_back{q}"), 16)
                xq = x[:, TQ * q:TQ * q + TQ, :]
                nc.gpsimd.tensor_tensor(xq, xq, rows[:, 1:2, :].broadcast_to([P, TQ, D]), ALU.add).then_inc(
                    sem("x_beta"), 1)

            pool.wait_ge(sem("setup_in"), 16 * SETUP)
            pool.wait_ge(sem("rows_zero"), 1)
            nc.gpsimd.tensor_copy(rows_out[:, 0:STILES, D], route[:, EXPERTS + 2 * TILES:]).then_inc(
                sem("slots_made"), 1)
            pool_softplus(pool, 0, 0)
            for u in range(UNITS):
                for k in range(STEPS):
                    s = STEPS * u + k
                    pool.wait_ge(sem("m_scan"), s + 1)
                    pool.wait_ge(sem("m_ccopy"), 2 * s + 2)
                    if s >= 3:
                        pool.wait_ge(sem("m_ysum"), s - 2)
                    nc.gpsimd.tensor_tensor(hC[:, s % 3], hs[:, s % 3], Cs[s % 3], ALU.mult).then_inc(
                        sem("m_hc"), 1)
                    if k == 8:
                        pool_softplus(pool, u, 1)
                    if k == 27 and u + 1 < UNITS:
                        pool_softplus(pool, u + 1, 0)
                    if k in (8, 16) and u == UNITS - 1:
                        add_beta((k - 8) // 8)
            for q in (2, 3):
                add_beta(q)

            pool.wait_ge(sem("slots_empty"), 16 * 6)
            nc.gpsimd.tensor_copy(rows_out[:, :, D], route[:, EXPERTS + TILES:EXPERTS + 2 * TILES]).then_inc(
                sem("own_rows"), 1)
            pool.wait_ge(sem("own_rows"), 1)
            for q in range(QUARTERS):
                pool_rstd(pool, "n1", q, 0)
            for f in range(2):
                if f == 0:
                    pool_route(pool)
                pool_experts(pool, f)
                if f == 0:
                    for i in range(ATT_SLOTS):
                        if i + 1 < QUARTERS:
                            combine(pool, nc.gpsimd.tensor_tensor, 0, i + 1, "x_pool")
                        if i < QUARTERS:
                            pool_rstd(pool, "n3", i, 1)
                        if 0 <= i - 3 < QUARTERS:
                            sl = slice(CT * (i - 3), CT * (i - 2))
                            pool.wait_ge(sem("b_num"), i - 2)
                            pool.wait_ge(sem("b_sig"), 2 * i - 4)
                            nc.gpsimd.tensor_tensor(kvS[:, sl], kvS[:, sl], rS[:, sl], ALU.mult).then_inc(
                                sem("b_gated"), 1)
                            pool.wait_ge(sem("b_gated"), i - 2)
                            pool.wait_ge(sem("b_rec"), i - 2)
                            nc.gpsimd.tensor_tensor(kvS[:, sl], kvS[:, sl], kS[:, sl], ALU.mult).then_inc(
                                sem("b_sy"), 1)
                        if 0 <= i - 4 < QUARTERS:
                            pool_rstd(pool, "n4", i - 4, 0)
                    for g in range(MIX_STEPS):
                        if g < GROUPS:
                            pool.wait_ge(sem("b_relu"), 2 * g + 2)
                            nc.gpsimd.tensor_tensor(k2[:, g % 2, 0:2], k2[:, g % 2, 0:2], k2[:, g % 2, 0:2],
                                                    ALU.mult).then_inc(sem("b_sqp"), 1)
                        if g >= 2 and g % 2 == 0 and g < GROUPS:
                            pool_rstd(pool, "e1", g // 2 - 1, slice(0, 2))
                        if g in (6, 7):
                            pool_put(pool, 1, range(TQ // 2 * (g - 6), TQ // 2 * (g - 5)))
                        elif g == GROUPS:
                            pool_put(pool, 1, range(TQ, TQ + TQ // 2))
                            pool_rstd(pool, "e1", QUARTERS - 1, slice(0, 2))
                            pool_put(pool, 1, range(TQ + TQ // 2, 2 * TQ))
                        elif g > GROUPS and g % 2 == 0:
                            pool_put(pool, 1, range(TQ // 2 * (g - 6), TQ // 2 * (g - 4)))
                else:
                    for q in (1, 3):
                        combine(pool, nc.gpsimd.tensor_tensor, 1, q, "x_pool")

        @block.scalar
        def _(act):
            act.wait_ge(sem("setup_in"), 16 * SETUP)
            act.wait_ge(sem("pads_zero"), 1)
            act_turn(act, "t0", 1.0, 0.0, 0, (0, 1))
            flat_a = acols[:].rearrange("p r h n -> p (r h n)")
            nc.scalar.activation(flat_a, flat_a, ACT.Exp).then_inc(sem("a_exp"), 1)
            act.wait_ge(sem("a_neg"), 1)
            act.wait_ge(sem("m_zero"), 1)

            for task, _ in bank_tasks(-1):
                act_bank(act, -1, task)
                if task == ("z", 1, 1):
                    act_turn(act, "t0", 1.0, 0.0, QUARTERS - 1, (0, 1), turn=1)
                    act_silu(act, 0, xc, "m_silu")
                    act_silu(act, 0, sz, "m_gate")
                    nc.scalar.preload_act_table_set("natural_log_exp_and_others")
            act_softplus_exp(act, 0, 0)
            act_softplus_ln(act, 0, 0)
            for q in (1, 2):
                act_turn(act, "t0", 1.0, 0.0, q, (0, 1), turn=q + 1)
            act_dx(act, 0, 0)
            for s in range(AHEAD):
                act_decay(act, s)
            for u in range(UNITS):
                for k in range(STEPS):
                    s = STEPS * u + k
                    if k == LAG and u > 0:
                        act_leave(act, u - 1, 1)
                    if k == STATE + LAG:
                        act_leave(act, u, 0)
                    if k == 12:
                        act_dx(act, u, 1)
                    act_c(act, s, 0)
                    silu = k == SILU_STEP and u + 1 < UNITS
                    if silu:
                        act_silu(act, u + 1, sz, "m_gate")
                    elif s + AHEAD < STEPS * UNITS:
                        act_decay(act, s + AHEAD)
                    act_c(act, s, 1)
                    if silu:
                        nc.scalar.preload_act_table_set("natural_log_exp_and_others")
                        act_decay(act, s + AHEAD)
                    for task, steps in bank_tasks(u):
                        if steps[-1] == k:
                            act_bank(act, u, task)
                    if k == SILU_STEP - 1 and u + 1 < UNITS:
                        act_silu(act, u + 1, xc, "m_silu")
                    if k == 4:
                        act_softplus_exp(act, u, 1)
                    if k == 5:
                        act_softplus_ln(act, u, 1)
                    if k == 26 and u + 1 < UNITS:
                        act_softplus_exp(act, u + 1, 0)
                    if k == 27 and u + 1 < UNITS:
                        act_softplus_ln(act, u + 1, 0)
                    if k == 30 and u + 1 < UNITS:
                        act_dx(act, u + 1, 0)
            act_leave(act, UNITS - 1, 1)
            for task, _ in bank_tasks(UNITS):
                act_bank(act, UNITS, task)

            act_route(act)
            act_experts(act, 0)

            nc.scalar.activation(small[:, 2:3], col("decay"), ACT.Exp).then_inc(sem("b_ed"), 1)
            act.wait_ge(sem("b_ed"), 1)
            nc.scalar.activation(small[:, 3:4], small[:, 2:3], ACT.Exp, scale=-1.0)
            nc.scalar.activation(small[:, 4:5], col("first"), ACT.Exp).then_inc(sem("b_ed"), 1)
            for i in range(ATT_SLOTS):
                if 0 <= i - 1 < QUARTERS:
                    act_turn(act, "t3", col("ln1_g"), col("ln1_b"), i - 1, (0,))
                    act_mix(act, "t3_out", "b_xm0", col("att_tm"), i - 1)
                if 0 <= i - 2 < QUARTERS:
                    for g in (2 * i - 4, 2 * i - 3):
                        act.wait_ge(sem("b_min"), g + 1)
                        sl = slice(512 * g, 512 * g + 512)
                        nc.scalar.activation(kS[:, sl], kS[:, sl], ACT.Exp).then_inc(sem("b_exp"), 1)
                    for g in (2 * i - 4, 2 * i - 3):
                        act.wait_ge(sem("b_r"), g + 1)
                        nc.scalar.activation(rS[:, 512 * g:512 * g + 512], PS[:, 5, :], ACT.Sigmoid).then_inc(
                            sem("b_sig"), 1)
                if 0 <= i - 3 < QUARTERS:
                    for g in (2 * i - 6, 2 * i - 5):
                        act.wait_ge(sem("b_att"), g + 1)
                        nc.scalar.activation(r[:, TG * g:TG * g + TG, :].rearrange("p t d -> p (t d)"), PS[:, 6, :],
                                             ACT.Copy).then_inc(sem("b_x2"), 1)
                if 0 <= i - 5 < QUARTERS:
                    act_turn(act, "t4", col("ln2_g"), col("ln2_b"), i - 5, (7,))
                    act_mix(act, "t4_out", "c_xm0", col("ffn_tm"), i - 5)
            for g in range(MIX_STEPS):
                q, odd = divmod(g - 4, 2)
                if g < GROUPS:
                    for i in range(2):
                        act.wait_ge(sem("b_fk"), 2 * g + i + 1)
                        if g >= 2:
                            act.wait_ge(sem("b_fv"), g - 1)
                        nc.scalar.activation(k2[:, g % 2, 2 * i:2 * i + 2].rearrange("p i t -> p (i t)"),
                                             flat(PS[:, 2 * i:2 * i + 2, :]), ACT.Relu).then_inc(sem("b_relu"), 1)
                if 0 <= q < QUARTERS and not odd:
                    act_tokens(act, 1, 2 * q)
                if 1 <= g <= GROUPS:
                    act.wait_ge(sem("b_fv"), g)
                    if g >= 3:
                        act.wait_ge(sem("b_x3"), g - 2)
                    nc.scalar.activation(sg[:, (g - 1) % 2, :], PS[:, 5, :], ACT.Sigmoid).then_inc(
                        sem("b_gate"), 1)
                if 0 <= q < QUARTERS and not odd:
                    act_tokens(act, 1, 2 * q + 1)
                elif 0 <= q < QUARTERS:
                    act_probs(act, 1, q)
            act_experts(act, 1)

        @block.tensor
        def _(pe):
            pe.wait_ge(sem("setup_in"), 16 * SETUP)
            pe_turn(pe, "t0", r, "n0_out", 0, (0, 1))
            pe.wait_ge(sem("t0_out"), GROUPS // QUARTERS)
            pe.wait_ge(sem("m_weights"), 1)
            mm = nc.tensor.matmul
            for task, steps in bank_tasks(-1):
                for part in range(len(steps)):
                    pe_bank(pe, -1, task, part)
                if task == ("z", 1, 1):
                    pe_turn(pe, "t0", r, "n0_out", QUARTERS - 1, (0, 1), turn=1)
            for q in (1, 2):
                pe_turn(pe, "t0", r, "n0_out", q, (0, 1), turn=q + 1)
            pe.wait_ge(sem("t0_out"), GROUPS)
            pe.wait_ge(sem("m_gfree"), bank_count(0))
            for u in range(UNITS):
                for k in range(STEPS):
                    s = STEPS * u + k
                    if s == 0:
                        pe_input(pe, 0)
                    pe_c(pe, s, 0)
                    pe_parts(pe, u, k)
                    pe_c(pe, s, 1)
                    if s + 1 < STEPS * UNITS:
                        pe_input(pe, s + 1)
                    if s >= LAG:
                        for q in range(2):
                            pe_sum(pe, s - LAG, q)
            for s in range(STEPS * UNITS - LAG, STEPS * UNITS):
                for q in range(2):
                    pe_sum(pe, s, q)
            for task, steps in bank_tasks(UNITS):
                for part in range(len(steps)):
                    pe_bank(pe, UNITS, task, part)

            pe_route(pe)
            pe_experts(pe, 0)

            pe.wait_ge(sem("wb_in"), 16 * 3)
            for i in range(ATT_SLOTS):
                if 0 <= i - 1 < QUARTERS:
                    pe_turn(pe, "t3", tokn, "n3_out", i - 1, (0,))
                if 0 <= i - 2 < QUARTERS:
                    for g in (2 * i - 4, 2 * i - 3):
                        pe.wait_ge(sem("b_xm"), g + 1)
                        if g >= 2:
                            pe.wait_ge(sem("b_min"), g - 1)
                            pe.wait_ge(sem("b_kv"), g - 1)
                        rhs = xm[:, 512 * g:512 * g + 512]
                        mm(PS[:, 1 + g % 2, :], wsq[:, 0, :], rhs, start=True, stop=True).then_inc(sem("b_k"), 1)
                        mm(PS[:, 3 + g % 2, :], wsq[:, 1, :], rhs, start=True, stop=True).then_inc(sem("b_v"), 1)
                    for g in (2 * i - 4, 2 * i - 3):
                        if g >= 1:
                            pe.wait_ge(sem("b_sig"), g)
                        mm(PS[:, 5, :], wsq[:, 2, :], xm[:, 512 * g:512 * g + 512], start=True, stop=True).then_inc(
                            sem("b_r"), 1)
                if 0 <= i - 3 < QUARTERS:
                    pe.wait_ge(sem("b_sy"), i - 2)
                    for g in (2 * i - 6, 2 * i - 5):
                        if g >= 1:
                            pe.wait_ge(sem("b_x2"), g)
                        for j in range(TG):
                            t0 = PAD + P * (j % 2)
                            dst = PS[:, 6, D * j:D * j + D]
                            mm(dst, xT[:, 2 * g + j // 2, t0:t0 + P], ident[:], start=True, stop=False)
                            last = mm(dst, kvS[:, 512 * g + P * j:512 * g + P * j + P], wsq[:, 3, :], start=False,
                                      stop=True)
                        last.then_inc(sem("b_att"), 1)
                if 0 <= i - 5 < QUARTERS:
                    pe_turn(pe, "t4", tokn, "n4_out", i - 5, (7,))

            def hidden(g):
                pe.wait_ge(sem("c_xm"), g + 1)
                if g == 0:
                    pe.wait_ge(sem("t3_out"), GROUPS)
                    pe.wait_ge(sem("b_min"), GROUPS)
                    pe.wait_ge(sem("b_kv"), GROUPS)
                    pe.wait_ge(sem("b_sig"), GROUPS)
                    pe.wait_ge(sem("b_x2"), GROUPS)
                for i in range(2):
                    if g >= 1:
                        pe.wait_ge(sem("b_relu"), 2 * g + i - 1)
                    for j in range(2):
                        last = mm(PS[:, 2 * i + j, :], fk[:, P * (2 * i + j):P * (2 * i + j) + P],
                                  xm[:, 512 * g:512 * g + 512], start=True, stop=True)
                    last.then_inc(sem("b_fk"), 1)

            def value(g):
                pe.wait_ge(sem("b_sqp"), g + 1)
                pe.wait_ge(sem("b_sqv"), g + 1)
                if g >= 1:
                    pe.wait_ge(sem("b_x3"), g)
                    pe.wait_ge(sem("b_gate"), g)
                for i in range(TG):
                    t0 = PAD + P * (i % 2)
                    o = slice(D * i, D * i + D)
                    for j in range(FT):
                        mm(PS[:, 4, o], k2[:, g % 2, j, P * i:P * i + P], fv[:, j, :], start=(j == 0),
                           stop=(j == FT - 1))
                    mm(PS[:, 5, o], xm[:, 512 * g + P * i:512 * g + P * i + P], wsq[:, 4, :], start=True, stop=True)
                    last = nc.tensor.transpose(PS[:, 6, o], xT[:, 2 * g + i // 2, t0:t0 + P], ident[:])
                last.then_inc(sem("b_fv"), 1)

            for g in range(MIX_STEPS):
                q, odd = divmod(g - 4, 2)
                if g < GROUPS:
                    hidden(g)
                if 0 <= q < QUARTERS and not odd:
                    pe_tokens(pe, 1, 2 * q)
                elif 0 <= q < QUARTERS:
                    pe_logits(pe, 1, q)
                if 1 <= g <= GROUPS:
                    value(g - 1)
                if 0 <= q < QUARTERS and not odd:
                    pe_tokens(pe, 1, 2 * q + 1)
                elif 0 <= q < QUARTERS:
                    pe_counts(pe, 1, q)
            pe.wait_ge(sem("b_relu"), 2 * GROUPS)
            pe.wait_ge(sem("b_x3"), GROUPS)
            pe.wait_ge(sem("b_gate"), GROUPS)
            pe_experts(pe, 1)

        @block.vector
        def _(dve):
            chain = [0]

            def link(ins):
                chain[0] += 1
                ins.then_inc(sem("dve_chain"), 1)
                dve.wait_ge(sem("dve_chain"), chain[0])

            dA4 = [v.rearrange("p (b t) -> p b t", b=CB) for v in dA]
            for i in range(QUARTERS + 1):
                if i < QUARTERS:
                    dve.wait_ge(sem(f"x_in{i}"), 16)
                    dve_stats(dve, link, "n0", x, i)
                if i >= 1:
                    dve_apply(dve, "n0", x, r, i - 1, 0)
                if i == 1:
                    dve.wait_ge(sem("setup_in"), 16 * SETUP)
                    for rev in range(2):
                        w1 = inproj[:, rev, 0:INNER].rearrange("p (k n) -> p k n", k=1).broadcast_to(
                            [P, TAPS, INNER])
                        last = nc.vector.tensor_tensor(convw[:, rev], convw[:, rev], w1, ALU.mult)
                    last.then_inc(sem("m_weights"), 1)
            dve.wait_ge(sem("n0_out"), QUARTERS)
            for v in dA4:
                last = nc.vector.memset(v[:, :, 0:1], 0.0)
            last.then_inc(sem("m_zero"), 1)
            dve.wait_ge(sem("a_exp"), 1)
            flat_a = acols[:].rearrange("p r h n -> p (r h n)")
            nc.vector.tensor_scalar(flat_a, flat_a, -1.0, None, ALU.mult).then_inc(sem("a_neg"), 1)

            for i in range(4):
                dve_split(dve, 0, i)
            for u in range(UNITS):
                rev = u // CHUNKS
                way = slice(None, None, -1) if rev else slice(None)
                for k in range(STEPS):
                    h = k // STATE
                    s = STEPS * u + k
                    if 25 <= k < 29 and u + 1 < UNITS:
                        dve_split(dve, u + 1, k - 25)
                    xk = flat(X[s % 2])
                    if k % STATE == 0:
                        dve.wait_ge(sem("m_du"), 2 * u + h + 1)
                    dve.wait_ge(sem("m_b"), s + 1)
                    nc.vector.tensor_tensor(xk, du[:, u % 2, h], xk, ALU.mult).then_inc(sem("m_dbu"), 1)
                    for task, steps in bank_tasks(u):
                        if steps[-1] == k:
                            dve_bank(dve, u, task)
                    dve.wait_ge(sem("m_dbu"), s + 1)
                    dve.wait_ge(sem("m_dA"), s + 1)
                    if s >= 3:
                        dve.wait_ge(sem("m_hc"), s - 2)
                    nc.vector.tensor_tensor_scan(hs[:, s % 3, way], dA[s % 3][:, way], xk[:, way], 0.0,
                                                 ALU.mult, ALU.add).then_inc(sem("m_scan"), 1)
                    if 0 < STEPS * CHUNKS - s <= 3:
                        dve.wait_ge(sem("m_scan"), s + 1)
                        nc.vector.memset(dA4[s % 3][:, :, T - 1:T], 0.0).then_inc(sem("m_reset"), 1)
            def output_stats(q):
                done = (UNITS, ("out", 1)) if q == QUARTERS - 1 else (CHUNKS + 1 + q, ("out", 1))
                dve.wait_ge(sem("m_gfree"), task_number(*done) + 1)
                dve_stats(dve, link, "n1", yo, q)

            def output_shift(q):
                dve.wait_ge(sem("n1_rstd"), q + 1)
                nc.vector.scalar_tensor_tensor(out=shift[:, 0, tiles_of(q)], in0=mv[:, tiles_of(q), 0], scalar=-1.0,
                                               in1=rstd[:, 0, tiles_of(q)], op0=ALU.mult, op1=ALU.mult).then_inc(
                    sem("n1_shift"), 1)

            output_stats(0)
            output_stats(1)
            for task, _ in bank_tasks(UNITS):
                dve_bank(dve, UNITS, task)
            output_shift(0)
            output_shift(1)
            for q in (2, 3):
                output_stats(q)
                output_shift(q)
            dve_route(dve, link)
            dve_experts(dve, link, 0)

            mix = small[:, 5:9]
            for i, (tm, cm) in enumerate((("att_tm", "att_cm"), ("ffn_tm", "ffn_cm"))):
                link(nc.vector.tensor_scalar(mix[:, 2 * i:2 * i + 1], col(tm), -1.0, 1.0, ALU.mult, ALU.add))
                link(nc.vector.scalar_tensor_tensor(out=mix[:, 2 * i:2 * i + 1], in0=col(cm), scalar=col("lo_mask"),
                                                    in1=mix[:, 2 * i:2 * i + 1], op0=ALU.mult, op1=ALU.add))
                link(nc.vector.tensor_scalar(mix[:, 2 * i + 1:2 * i + 2], col(cm), col("hi_mask"), None, ALU.mult))
            dve.wait_ge(sem("b_ed"), 2)
            link(nc.vector.memset(edT, 0.0))
            link(nc.vector.tensor_scalar(edT[:, :, 1:T], edT[:, :, 1:T], small[:, 3:4], None, ALU.add))
            a3 = r[:].rearrange("p t d -> p (t d)")
            b3 = rows_out[:].rearrange("p t d -> p (t d)")[:, 0:NTOK]
            ed = edT.rearrange("p b t -> p (b t)")

            def seqs(ap, q):
                return ap[:, CT * q:CT * q + CT].rearrange("p (b t) -> p b t", b=CB)

            def clamp(q):
                for g in (2 * q, 2 * q + 1):
                    dve.wait_ge(sem("b_k"), g + 1)
                    nc.vector.tensor_scalar(kS[:, 512 * g:512 * g + 512], PS[:, 1 + g % 2, :], CLAMP, None,
                                            ALU.min).then_inc(sem("b_min"), 1)

            def key_value(q):
                for g in (2 * q, 2 * q + 1):
                    sl = slice(512 * g, 512 * g + 512)
                    dve.wait_ge(sem("b_exp"), g + 1)
                    dve.wait_ge(sem("b_v"), g + 1)
                    nc.vector.tensor_tensor(kvS[:, sl], PS[:, 3 + g % 2, :], kS[:, sl], ALU.mult).then_inc(
                        sem("b_kv"), 1)

            def wkv(q):
                sl = slice(CT * q, CT * q + CT)
                dve.wait_ge(sem("b_kv"), 2 * q + 2)
                dve.wait_ge(sem("t3_in"), 2 * q + 2)
                nc.vector.tensor_tensor_scan(a3[:, sl], ed, kvS[:, sl], 0.0, ALU.mult, ALU.add)
                link(nc.vector.tensor_tensor_scan(b3[:, sl], ed, kS[:, sl], 0.0, ALU.mult, ALU.add))
                for cur, prev, done in ((kvS, a3, "b_num"), (kS, b3, "b_den")):
                    c, p = seqs(cur, q), seqs(prev, q)
                    nc.vector.tensor_scalar(c[:, :, 0:1], c[:, :, 0:1], small[:, 4:5], None, ALU.mult)
                    nc.vector.scalar_tensor_tensor(out=c[:, :, 1:T], in0=c[:, :, 1:T], scalar=small[:, 4:5],
                                                   in1=p[:, :, 0:T - 1], op0=ALU.mult, op1=ALU.add).then_inc(
                        sem(done), 1)
                dve.wait_ge(sem("b_den"), q + 1)
                nc.vector.reciprocal(kS[:, sl], kS[:, sl]).then_inc(sem("b_rec"), 1)

            for i in range(ATT_SLOTS + 1):
                if i < QUARTERS:
                    if i == 0:
                        combine(dve, nc.vector.tensor_tensor, 0, 0, "x_dve")
                    dve.wait_ge(sem("x_pool" if i else "x_dve"), max(i, 1))
                    dve_stats(dve, link, "n3", x, i)
                if 0 <= i - 1 < QUARTERS:
                    dve_apply(dve, "n3", x, tokn, i - 1, 1)
                if 0 <= i - 2 < QUARTERS:
                    dve_mix(dve, link, "b", i - 2, mix[:, 0:1], mix[:, 1:2])
                if 0 <= i - 3 < QUARTERS:
                    key_value(i - 3)
                    wkv(i - 3)
                if 0 <= i - 2 < QUARTERS:
                    clamp(i - 2)
                if 0 <= i - 4 < QUARTERS:
                    dve.wait_ge(sem("b_x2"), 2 * i - 6)
                    dve_stats(dve, link, "n4", r, i - 4)
                if 0 <= i - 5 < QUARTERS:
                    dve_apply(dve, "n4", r, tokn, i - 5, 0)
                if 0 <= i - 6 < QUARTERS:
                    dve_mix(dve, link, "c", i - 6, mix[:, 2:3], mix[:, 3:4])
            nc.vector.tensor_copy(rows_out[:, :, D], route[:, EXPERTS + TILES:EXPERTS + 2 * TILES])
            choose, place = dve_router(dve, link, 1)
            for g in range(MIX_STEPS):
                q, odd = divmod(g - 4, 2)
                if q >= 1 and not odd:
                    place(q - 1)
                if g < GROUPS:
                    dve.wait_ge(sem("b_relu"), 2 * g + 2)
                    nc.vector.tensor_tensor(k2[:, g % 2, 2:4], k2[:, g % 2, 2:4], k2[:, g % 2, 2:4],
                                            ALU.mult).then_inc(sem("b_sqv"), 1)
                if 0 <= q < QUARTERS and odd:
                    choose(q)
                if g >= 3 and g % 2 == 1 and g <= GROUPS + 1:
                    dve_apply(dve, "e1", x, tokn, (g - 3) // 2, 1)
                if 1 <= g <= GROUPS:
                    c = g - 1
                    dve.wait_ge(sem("b_gate"), g)
                    xg = x[:, TG * c:TG * c + TG, :].rearrange("p t d -> p (t d)")
                    link(nc.vector.tensor_tensor(sg[:, c % 2, :], sg[:, c % 2, :], PS[:, 4, :], ALU.mult))
                    link(nc.vector.tensor_tensor(xg, xg, sg[:, c % 2, :], ALU.add))
                    nc.vector.tensor_tensor(xg, xg, PS[:, 6, :], ALU.add).then_inc(sem("b_x3"), 1)
                if g >= 2 and g % 2 == 0 and g <= GROUPS:
                    dve.wait_ge(sem("b_x3"), g)
                    dve_stats(dve, link, "e1", x, g // 2 - 1)
            dve_experts(dve, link, 1)
            for q in (0, 2):
                combine(dve, nc.vector.tensor_tensor, 1, q, "x_dve")

def kernel(**inputs):
    import numpy as np
    import ml_dtypes
    import concourse.bacc as bacc
    from concourse.bass_utils import run_bass_kernel_spmd

    A, B, F = "L0_attn_a_", "L0_attn_b_", "L0_ffn_"
    w = {k: np.asarray(v) for k, v in inputs.items()}
    dirs = ("fwd_", "bwd_")

    def halves(name):
        return [w[A + d + name][P * h:P * h + P] for d in dirs for h in range(HALVES)]

    lo = (np.arange(P) < P // 2).astype(np.float32)
    cols = np.stack(halves("conv_b") + halves("dt_proj_b") + halves("D") + [
        w[F + "ln_gamma"], w[F + "ln_beta"], w[B + "ln1_g"], w[B + "ln1_b"], w[B + "ln2_g"], w[B + "ln2_b"],
        w[B + "att_time_mix"].reshape(P), w[B + "att_combined_mix"].reshape(P),
        w[B + "ffn_time_mix"].reshape(P), w[B + "ffn_combined_mix"].reshape(P),
        w[B + "time_decay"], w[B + "time_first"], lo, np.float32(1) - lo], axis=1)

    def xproj(d):
        v = w[A + d + "x_proj_w"]
        return np.concatenate([v[RANK:]] * 3 + [v[:RANK]], axis=0).T.reshape(HALVES, P, 104).transpose(1, 0, 2)

    sel = np.zeros((96, 2 * STATE, P), ml_dtypes.bfloat16)
    for k in range(96):
        sel[k, k % 32] = 1
    tri = np.ones((P, 2, P), ml_dtypes.bfloat16)
    tri[:, 0] = np.triu(np.ones((P, P)), 1)
    tok = np.arange(P)[:, None] + P * np.arange(TILES)[None]
    spare = (CAP * np.arange(EXPERTS)[None, :, None] + SE * np.arange(P)[:, None, None]
             + np.arange(SE)[None, None]).reshape(P, STILES)
    route = np.concatenate([np.tile(np.arange(EXPERTS, 0, -1), (P, 1)), tok, SLOTS + tok, spare],
                           axis=1).astype(np.float32)
    arrays = {
        "x_in": w[A + "x"].reshape(NTOK, D),
        "cols_in": cols,
        "alog_in": np.stack([w[A + d + "A_log"].reshape(HALVES, P, STATE).transpose(1, 0, 2) for d in dirs], axis=1),
        "rows_in": np.stack([w[A + "ln_gamma"], w[A + "ln_beta"]]),
        "conv_in": np.stack([w[A + d + "conv_w"].T for d in dirs]),
        "inproj_in": np.stack([w[A + d + "in_proj_w"].T for d in dirs], axis=1),
        "xproj_in": np.stack([xproj(d) for d in dirs], axis=1),
        "dtproj_in": np.stack([w[A + d + "dt_proj_w"].T for d in dirs], axis=1),
        "outproj_in": np.stack([w[A + d + "out_proj_w"].T.reshape(HALVES, P, D).transpose(1, 0, 2) for d in dirs],
                               axis=1),
        "wsq_in": np.stack([w[B + n].T for n in ("Wk", "Wv", "Wr", "Wo", "Fr")], axis=1),
        "fk_in": w[B + "Fk"].T,
        "fv_in": w[B + "Fv"].T.reshape(FT, P, D).transpose(1, 0, 2),
        "gate_in": w[F + "gate_weight"].T,
        "wi_in": w[F + "wi"].transpose(1, 0, 2),
        "wo_in": w[F + "wo"].reshape(EXPERTS, FT, P, D).transpose(2, 0, 1, 3),
        "ident_in": np.eye(P, dtype=np.float32),
        "sel_in": sel,
        "tri_in": tri,
        "route_in": route,
    }
    arrays = {k: np.ascontiguousarray(v) for k, v in arrays.items()}
    nc = bacc.Bacc("TRN2", target_bir_lowering=False, num_devices=1)
    args = [nc.dram_tensor(k, v.shape, mybir.dt.from_np(v.dtype), kind="ExternalInput").ap()
            for k, v in arrays.items()]
    args.append(nc.dram_tensor("out", (BATCH, T, D), F32, kind="ExternalOutput").ap())
    layer(nc, *args)
    return run_bass_kernel_spmd(nc, [arrays], core_ids=[0]).results[0]["out"]
```
